# Optimizing a Trainium2 kernel written in Bass

```python
import numpy as np
import jax
import jax.numpy as jnp

def _softmax(x, axis=-1):
    return jax.nn.softmax(x, axis=axis)

def _gelu(x):
    return jax.nn.gelu(x, approximate=True)

def _silu(x):
    return jax.nn.silu(x)

def _sigmoid(x):
    return jax.nn.sigmoid(x)

def _layernorm(x, axis=-1, eps=1e-05):
    m = jnp.mean(x, axis=axis, keepdims=True)
    v = jnp.var(x, axis=axis, keepdims=True)
    return (x - m) / jnp.sqrt(v + eps)

def _scatter_add(tgt, idx, src, axis=0):
    return tgt.at[idx].add(src)

def _segment_sum(src, seg, n):
    return jax.ops.segment_sum(src, seg, n)
kernel_name = 'mk_decoder_postln_d1_seqx_r4_5eb078'

def setup_inputs(seed: int=0):
    np.random.seed(seed)
    _w = jnp.asarray

    def _rec_inputs():
        import jax
        import jax.numpy as jnp
        _rk = jax.random.key(seed)
        x = 6.313e-05 + 0.9998 * jax.random.normal(jax.random.fold_in(_rk, 1), (4, 1024, 256), jnp.float32)
        _lenS = 1024 - jax.random.randint(jax.random.fold_in(_rk, 7), (4,), 0, max(1, 1024 // 4) + 1, jnp.int32)
        _lenS2 = 154 - jax.random.randint(jax.random.fold_in(_rk, 8), (4,), 0, max(1, 154 // 4) + 1, jnp.int32)
        _ctx_1024P = jax.random.normal(jax.random.fold_in(_rk, 11), (4, 16, 256), jnp.float32)
        _ctx_1024c = jax.random.dirichlet(jax.random.fold_in(_rk, 511), 0.3 * jnp.ones((16,), jnp.float32), (4, 154))
        _ctx_1024t = jnp.einsum('bsk,bkd->bsd', _ctx_1024c, _ctx_1024P)
        _ctx_1024t = _ctx_1024t * jax.lax.rsqrt(jnp.mean(jnp.square(_ctx_1024t)) + 1e-12) * 0.953939
        ctx_1024 = -0.000214406 + 1.00034 * (_ctx_1024t + 0.3 * jax.random.normal(jax.random.fold_in(_rk, 611), (4, 154, 256), jnp.float32))
        return (x, ctx_1024)
    x, ctx_1024 = _rec_inputs()

    def _L0_attn_setup():
        import jax, jax.numpy as jnp
        import numpy as np
        D_MODEL = 256
        EXPAND = 2
        D_INNER = D_MODEL * EXPAND
        C = 8
        B, T = (4, 512)
        key = jax.random.key(seed)
        ks = jax.random.split(key, 8)
        x = jax.random.normal(ks[0], (B, T, D_MODEL), jnp.float32)
        a = np.log(1.0 / np.exp(np.log(0.999) / C) - 1.0)
        b = np.log(1.0 / np.exp(np.log(0.9) / C) - 1.0)
        omega = (a + (b - a) * jax.random.uniform(ks[1], (1, 1, D_INNER))).astype(jnp.float32)
        s = 0.02
        Win = (jax.random.normal(ks[2], (2 * D_INNER, D_MODEL)) * s).astype(jnp.float32)
        Wl = (jax.random.normal(ks[3], (D_INNER, D_INNER)) * s).astype(jnp.float32)
        bl = jnp.zeros((D_INNER,), jnp.float32)
        Wv = (jax.random.normal(ks[4], (D_INNER, D_INNER)) * s).astype(jnp.float32)
        bv = jnp.zeros((D_INNER,), jnp.float32)
        Wout = (jax.random.normal(ks[5], (D_MODEL, D_INNER)) * s).astype(jnp.float32)
        return dict(x=x, omega=omega, Win=Win, Wl=Wl, bl=bl, Wv=Wv, bv=bv, Wout=Wout)
    _L0_attn_all = _L0_attn_setup()
    _L0_attn_in = {k: v for k, v in _L0_attn_all.items() if k in ('omega', 'Win', 'Wl', 'bl', 'Wv', 'bv', 'Wout')}
    del _L0_attn_all

    def _L0_xattn_setup():
        import jax, jax.numpy as jnp
        import numpy as np
        from jax import lax
        BIG = jnp.float32(1e+30)

        def _pairwise_euclidean(a, b):
            aa = jnp.sum(a * a, axis=-1)[:, None]
            bb = jnp.sum(b * b, axis=-1)[None, :]
            ab = a @ b.T
            return jnp.sqrt(jnp.maximum(aa + bb - 2.0 * ab, 0.0))

        def _dtw_cost(D):
            row0 = jnp.cumsum(D[0])

            def row_step(prev_row, d_row):
                first = d_row[0] + prev_row[0]

                def col_step(left, inp):
                    d_ij, up, diag = inp
                    r = d_ij + jnp.minimum(jnp.minimum(up, left), diag)
                    return (r, r)
                _, rest = lax.scan(col_step, first, (d_row[1:], prev_row[1:], prev_row[:-1]))
                row = jnp.concatenate([first[None], rest])
                return (row, row)
            _, rows = lax.scan(row_step, row0, D[1:])
            return jnp.concatenate([row0[None], rows], axis=0)

        def _backtrack(R, T1, T2):
            L = T1 + T2 - 1

            def step(carry, _):
                i, j, done = carry
                valid = jnp.logical_not(done)
                cd = jnp.where((i > 0) & (j > 0), R[jnp.maximum(i - 1, 0), jnp.maximum(j - 1, 0)], BIG)
                cu = jnp.where(i > 0, R[jnp.maximum(i - 1, 0), j], BIG)
                cl = jnp.where(j > 0, R[i, jnp.maximum(j - 1, 0)], BIG)
                choice = jnp.argmin(jnp.stack([cd, cu, cl]))
                ni = jnp.where(choice <= 1, i - 1, i)
                nj = jnp.where((choice == 0) | (choice == 2), j - 1, j)
                at_origin = (i == 0) & (j == 0)
                ni = jnp.where(at_origin, 0, ni)
                nj = jnp.where(at_origin, 0, nj)
                return ((ni, nj, done | at_origin), (i, j, valid))
            init = (jnp.int32(T1 - 1), jnp.int32(T2 - 1), jnp.bool_(False))
            _, (i_idx, j_idx, valid) = lax.scan(step, init, None, length=L)
            return (i_idx, j_idx, valid)

        def _align_one(small, large):
            T_small, d = small.shape
            T_large = large.shape[0]
            D = _pairwise_euclidean(small, large)
            R = _dtw_cost(D)
            i_idx, j_idx, valid = _backtrack(R, T_small, T_large)
            contrib = small[i_idx] * valid[:, None].astype(small.dtype)
            expanded = jnp.zeros((T_large, d), dtype=small.dtype).at[j_idx].add(contrib)
            return expanded
        key = jax.random.key(seed)
        k1, k2 = jax.random.split(key)
        teacher = jax.random.normal(k1, (16, 100, 256), dtype=jnp.float32)
        student = jax.random.normal(k2, (16, 150, 256), dtype=jnp.float32)
        return {'teacher_features': teacher, 'student_features': student}
    _L0_xattn_all = _L0_xattn_setup()
    _L0_xattn_in = {k: v for k, v in _L0_xattn_all.items() if k in ()}
    del _L0_xattn_all

    def _L0_ffn_setup():
        import jax, jax.numpy as jnp
        import numpy as np
        B, N, D = (4, 512, 256)
        SPARSITY = 0.01
        key = jax.random.key(seed)
        k1, k2, k3 = jax.random.split(key, 3)
        x = jax.random.normal(k1, (B, N, D), dtype=jnp.float32)
        spatial = jax.random.normal(k2, (D, D), dtype=jnp.float32) * 0.02
        freq = jnp.fft.fft(spatial, axis=-1)
        k = int(D * SPARSITY)
        mag = jnp.abs(freq)
        kth = jax.lax.top_k(mag, k)[0][:, -1:]
        w_sparse = jnp.where(mag >= kth, freq, 0.0 + 0j)
        bias = jax.random.normal(k3, (D,), dtype=jnp.float32) * 0.01
        return {'x': x, 'w_freq_real': jnp.real(w_sparse).astype(jnp.float32), 'w_freq_imag': jnp.imag(w_sparse).astype(jnp.float32), 'bias': bias}
    _L0_ffn_all = _L0_ffn_setup()
    _L0_ffn_in = {k: v for k, v in _L0_ffn_all.items() if k in ('w_freq_real', 'w_freq_imag', 'bias')}
    del _L0_ffn_all
    return {'x': x, 'ctx_1024': ctx_1024, 'L0_attn_omega': _L0_attn_in['omega'], 'L0_attn_Win': _L0_attn_in['Win'], 'L0_attn_Wl': _L0_attn_in['Wl'], 'L0_attn_bl': _L0_attn_in['bl'], 'L0_attn_Wv': _L0_attn_in['Wv'], 'L0_attn_bv': _L0_attn_in['bv'], 'L0_attn_Wout': _L0_attn_in['Wout'], 'L0_ffn_w_freq_real': _L0_ffn_in['w_freq_real'], 'L0_ffn_w_freq_imag': _L0_ffn_in['w_freq_imag'], 'L0_ffn_bias': _L0_ffn_in['bias']}

def reference(x, ctx_1024, L0_attn_omega, L0_attn_Win, L0_attn_Wl, L0_attn_bl, L0_attn_Wv, L0_attn_bv, L0_attn_Wout, L0_ffn_w_freq_real, L0_ffn_w_freq_imag, L0_ffn_bias):
    import jax
    import jax.numpy as jnp

    def _L0_attn_ref(x, omega, Win, Wl, bl, Wv, bv, Wout):
        import jax, jax.numpy as jnp
        import numpy as np
        D_MODEL = 256
        EXPAND = 2
        D_INNER = D_MODEL * EXPAND
        C = 8
        B, T = (4, 512)
        xz = jnp.einsum('btd,ed->bte', x, Win)
        xi, z = jnp.split(xz, 2, axis=-1)
        log_lam = -C * jax.nn.softplus(omega) * jax.nn.sigmoid(jnp.einsum('bti,ji->btj', xi, Wl) + bl)
        lam = jnp.exp(log_lam)
        v = jnp.einsum('bti,ji->btj', xi, Wv) + bv
        h0 = xi[:, 0]

        def step(h_prev, inp):
            x_t, v_t, lam_t = inp
            vh = jnp.sum(v_t * h_prev, axis=-1, keepdims=True)
            vv = jnp.sum(v_t * v_t, axis=-1, keepdims=True)
            Qh = h_prev - 2.0 * v_t * (vh / vv)
            h = lam_t * Qh + (1.0 - lam_t) * x_t
            return (h, h)
        xs = (jnp.swapaxes(xi[:, 1:], 0, 1), jnp.swapaxes(v[:, 1:], 0, 1), jnp.swapaxes(lam[:, 1:], 0, 1))
        _, hs = jax.lax.scan(step, h0, xs)
        h = jnp.concatenate([h0[:, None], jnp.swapaxes(hs, 0, 1)], axis=1)
        return jnp.einsum('bti,di->btd', jax.nn.silu(z) * h, Wout)

    def _L0_xattn_ref(teacher_features, student_features):
        import jax, jax.numpy as jnp
        import numpy as np
        from jax import lax
        BIG = jnp.float32(1e+30)

        def _pairwise_euclidean(a, b):
            aa = jnp.sum(a * a, axis=-1)[:, None]
            bb = jnp.sum(b * b, axis=-1)[None, :]
            ab = a @ b.T
            return jnp.sqrt(jnp.maximum(aa + bb - 2.0 * ab, 0.0))

        def _dtw_cost(D):
            row0 = jnp.cumsum(D[0])

            def row_step(prev_row, d_row):
                first = d_row[0] + prev_row[0]

                def col_step(left, inp):
                    d_ij, up, diag = inp
                    r = d_ij + jnp.minimum(jnp.minimum(up, left), diag)
                    return (r, r)
                _, rest = lax.scan(col_step, first, (d_row[1:], prev_row[1:], prev_row[:-1]))
                row = jnp.concatenate([first[None], rest])
                return (row, row)
            _, rows = lax.scan(row_step, row0, D[1:])
            return jnp.concatenate([row0[None], rows], axis=0)

        def _backtrack(R, T1, T2):
            L = T1 + T2 - 1

            def step(carry, _):
                i, j, done = carry
                valid = jnp.logical_not(done)
                cd = jnp.where((i > 0) & (j > 0), R[jnp.maximum(i - 1, 0), jnp.maximum(j - 1, 0)], BIG)
                cu = jnp.where(i > 0, R[jnp.maximum(i - 1, 0), j], BIG)
                cl = jnp.where(j > 0, R[i, jnp.maximum(j - 1, 0)], BIG)
                choice = jnp.argmin(jnp.stack([cd, cu, cl]))
                ni = jnp.where(choice <= 1, i - 1, i)
                nj = jnp.where((choice == 0) | (choice == 2), j - 1, j)
                at_origin = (i == 0) & (j == 0)
                ni = jnp.where(at_origin, 0, ni)
                nj = jnp.where(at_origin, 0, nj)
                return ((ni, nj, done | at_origin), (i, j, valid))
            init = (jnp.int32(T1 - 1), jnp.int32(T2 - 1), jnp.bool_(False))
            _, (i_idx, j_idx, valid) = lax.scan(step, init, None, length=L)
            return (i_idx, j_idx, valid)

        def _align_one(small, large):
            T_small, d = small.shape
            T_large = large.shape[0]
            D = _pairwise_euclidean(small, large)
            R = _dtw_cost(D)
            i_idx, j_idx, valid = _backtrack(R, T_small, T_large)
            contrib = small[i_idx] * valid[:, None].astype(small.dtype)
            expanded = jnp.zeros((T_large, d), dtype=small.dtype).at[j_idx].add(contrib)
            return expanded
        return jax.vmap(_align_one)(teacher_features, student_features)

    def _L0_ffn_ref(x, w_freq_real, w_freq_imag, bias):
        import jax, jax.numpy as jnp
        import numpy as np
        B, N, D = (4, 512, 256)
        SPARSITY = 0.01
        w = jax.lax.complex(w_freq_real, w_freq_imag)
        x_freq = jnp.fft.fft(x, axis=-1)
        y_freq = jnp.einsum('bnd,do->bno', x_freq, w)
        y = jnp.real(jnp.fft.ifft(y_freq, axis=-1))
        return y + bias
    x = _layernorm(x + _L0_attn_ref(x, L0_attn_omega, L0_attn_Win, L0_attn_Wl, L0_attn_bl, L0_attn_Wv, L0_attn_bv, L0_attn_Wout), axis=-1)
    x = _layernorm(x + _L0_xattn_ref(ctx_1024, x), axis=-1)
    x = _layernorm(x + _L0_ffn_ref(x, L0_ffn_w_freq_real, L0_ffn_w_freq_imag, L0_ffn_bias), axis=-1)
    return x

_drawn_inputs = setup_inputs


def setup_inputs(seed=0):
    import zlib

    import numpy as np

    out = dict(_drawn_inputs(seed))
    spreads = {'L0_attn_bl': (0.0, 0.8), 'L0_attn_bv': (0.0, 0.8)}
    factors = {'L0_attn_omega': 8.0,
     'L0_attn_Win': 7.808,
     'L0_attn_Wl': 8.0,
     'L0_attn_Wv': 8.0,
     'L0_attn_Wout': 7.904,
     'L0_ffn_bias': 6.94}
    for name, (base, spread) in spreads.items():
        noise = np.random.default_rng([zlib.crc32(name.encode()), seed]).standard_normal(out[name].shape)
        drawn = base * np.exp(spread * noise) if base else spread * noise
        out[name] = jnp.asarray(drawn.astype(out[name].dtype))
    for name, factor in factors.items():
        out[name] = (out[name] * factor).astype(out[name].dtype)
    return out
```

```python
import math
from contextlib import ExitStack

import concourse.bass as bass
from concourse import mybir

ALU = mybir.AluOpType
ACT = mybir.ActivationFunctionType
AX = mybir.AxisListType
F32 = mybir.dt.float32
BF16 = mybir.dt.bfloat16
I32 = mybir.dt.int32

P = 128
B, T, D = 4, 1024, 256
DI = 512
KD = D // P
CT = DI // P
L = 32
NCH = 4
GT = L * NCH
NG = T // GT
CB = CT * B
SEG = NCH * CB
NTOK = B * GT
L1 = L + 1
LEVELS = (2, 4, 8, 16)
SAFE = math.exp(40.0)
TSTART = 10
TOPS = TSTART + 3 * (len(LEVELS) - 1) + 2 + B


def recurrence_block(nc, dram, HG, cst):
    with ExitStack() as ctx:
        def sb(name, shape, dt=F32):
            return ctx.enter_context(nc.sbuf_tensor(name, shape, dt))

        def sem(name):
            return ctx.enter_context(nc.semaphore(name))

        bank = [ctx.enter_context(nc.psum_tensor(f"bank{i}", [P, 512], F32)) for i in range(8)]
        PJ = bank[0:4]
        GR, TI, CQ, CP = bank[4:8]

        win_t = sb("win_t", [P, KD, 2 * DI])
        wc = sb("wc", [P, 2, KD, DI])
        bias = cst["bias"]
        tri = cst["tri"]
        xT = sb("xT", [P, 2, KD, B, GT])
        lam = [sb(f"lam{i}", [P, SEG, L1]) for i in range(2)]
        S = sb("S", [P, SEG, L1])
        V = [sb(f"V{i}", [P, SEG, L]) for i in range(2)]
        X = [sb(f"X{i}", [P, SEG, L]) for i in range(2)]
        U = [sb(f"U{i}", [P, SEG, L]) for i in range(2)]
        KB = sb("KB", [P, SEG, 2, L])
        keep = sb("keep", [P, CB, L1])
        sz = sb("sz", [P, 2, NTOK])
        E = sb("E", [P, CB, L1])
        H = [sb(f"H{i}", [P, CB, L1]) for i in range(2)]
        gm = sb("gm", [P, NCH, 2, L])
        vc = sb("vc", [P, NCH, 2])
        negc = [sb(f"negc{i}", [P, NCH]) for i in range(2)]
        w = [sb(f"w{i}", [P, NCH]) for i in range(2)]
        N = sb("N", [P, NCH, L])
        Tm = sb("Tm", [P, NCH, L])
        St = sb("St", [P, NCH, L])
        Ym = sb("Ym", [P, NCH, L])
        Sd = [sb(f"Sd{i}", [P, NCH, B, L]) for i in range(2)]
        qs = sb("qs", [P, 1])
        rng = sb("rng", [P, NG])
        sp = sb("sp", [P, 8, CT])
        slope = cst["slope"]
        HGf = HG[:, :, :, :].rearrange("p c b t -> p (c b t)")
        wlv = HGf[:, 0:2 * CT * DI].rearrange("p (w i j) -> p w i j", w=2, i=CT)
        win_x = HGf[:, 2 * CT * DI:2 * CT * DI + CT * D].rearrange("p (i d) -> p i d", i=CT)

        ld = {k: sem("ld_" + k) for k in ("w", "small", "x0", "x1")}
        s_const, s_wc, s_wce, s_slope = sem("s_const"), sem("s_wc"), sem("s_wce"), sem("s_slope")
        pe = {k: sem("pe_" + k) for k in "lzvx"}
        ev = {k: sem("ev_" + k) for k in "lvxz"}
        act_sz = sem("act_sz")
        s_fix = sem("s_fix")
        s_scan, s_gex, s_lam, s_ginv = sem("s_scan"), sem("s_gex"), sem("s_lam"), sem("s_ginv")
        s_u, s_kb, s_nb, s_a, s_rng = sem("s_u"), sem("s_kb"), sem("s_nb"), sem("s_a"), sem("s_rng")
        pe_gram, s_t, pe_y, act_y, pe_t = sem("pe_gram"), sem("s_t"), sem("pe_y"), sem("act_y"), sem("pe_t")
        pe_q, s_qs, pe_p, s_e, s_h, s_g = sem("pe_q"), sem("s_qs"), sem("pe_p"), sem("s_e"), sem("s_h"), sem("s_g")
        xfree = sem("xfree")
        s_flag = sem("s_flag")

        def seg(t, n, c):
            return t[:, :, :].rearrange("p (n c b) l -> p c b n l", n=NCH, c=CT)[:, c]

        block = ctx.enter_context(nc.Block())

        @block.sync
        def _(sp_):
            sp_.dma_start(wlv, dram["wlv_t"].rearrange("w (i p) j -> p w i j", p=P)).then_inc(ld["w"], 16)
            sp_.dma_start(win_x, dram["win"][0:DI, :].rearrange("(i p) d -> p i d", p=P)).then_inc(ld["w"], 16)
            sp_.dma_start(win_t[:, :, :], dram["win_t"].rearrange("(k p) n -> p k n", p=P)).then_inc(ld["w"], 16)
            sp_.dma_start(bias[:, :, :], dram["bias"]).then_inc(ld["small"], 16)
            for k in ("tri", "eye", "quad", "last"):
                sp_.dma_start(cst[k][:], dram[k]).then_inc(ld["small"], 16)

            def load_x(g, par):
                for k in range(KD):
                    src = dram["x_t"].rearrange("k p b (g t) -> g k p b t", t=GT)
                    if isinstance(g, int):
                        s = src[g, k]
                    else:
                        s = src[bass.ds(g, 1), k].rearrange("o p b t -> (o p) b t")
                    sp_.dma_start(xT[:, par, k], s).then_inc(ld[f"x{par}"], 16)

            for g in range(NG):
                if g >= 2:
                    sp_.wait_ge(pe["x"], CT * (g - 1))
                load_x(g, g % 2)

        def group_loop(body):
            body(-1, 1, False, True, True)
            body(0, 0, True, True, True)
            body(1, 1, True, True, True)
            body(2, 0, True, True, True)
            body(3, 1, True, True, True)
            body(4, 0, True, True, True)
            body(5, 1, True, True, True)
            body(6, 0, True, True, False)
            body(7, 1, True, False, False)

        @block.tensor
        def _(te):
            te.wait_ge(ld["w"], 48)
            for j in range(2):
                for m in range(KD):
                    for i in range(CT):
                        last = te.matmul(PJ[2 * j + m][:, :], win_x[:, i, m * P:(m + 1) * P], wlv[:, j, i, :],
                                         start=(i == 0), stop=(i == CT - 1))
                    last.then_inc(s_wc, 1)

            def project(kind, G, par, c):
                before = {"l": ("z", 0), "v": ("l", 0), "x": ("v", 0), "z": ("x", 1)}[kind]
                if not (kind == "z" and isinstance(G, int) and G == 0):
                    te.wait_ge(ev[before[0]], CT * (G - before[1]) + c + 1)
                if kind == "z" and c == 0:
                    te.wait_ge(ld[f"x{par}"], 16 * KD * (G // 2 + 1))
                for k in range(KD):
                    if kind in "lv":
                        lhs = wc[:, 0 if kind == "l" else 1, k, c * P:(c + 1) * P]
                    else:
                        o = DI * (kind == "z") + c * P
                        lhs = win_t[:, k, o:o + P]
                    last = te.matmul(PJ[c][:, :], lhs, xT[:, par, k, :, :], start=(k == 0), stop=(k == KD - 1))
                last.then_inc(pe[kind], 1)

            def gram(G, par):
                te.wait_ge(s_kb, 2 * (G + 1))
                te.wait_ge(s_u, G + 1)
                for n in range(NCH):
                    for c in range(CT):
                        for b in range(B):
                            s = (n * CT + c) * B + b
                            last = te.matmul(GR[L * b:L * b + L, 2 * L * n:2 * L * (n + 1)], U[par][:, s, :],
                                             KB[:, s, :, :], start=(c == 0), stop=(c == CT - 1))
                last.then_inc(pe_gram, 1)

            def level_y(G, lv):
                te.wait_ge(s_t, TOPS * G + TSTART + 3 * lv)
                for n in range(NCH):
                    for b in range(B):
                        q = slice(L * b, L * b + L)
                        last = te.matmul(TI[q, L * n:L * n + L], N[q, n, :], St[q, n, :], start=True, stop=True)
                last.then_inc(pe_y, 1)

            def level_t(G, lv):
                te.wait_ge(act_y, len(LEVELS) * G + lv + 1)
                for n in range(NCH):
                    for b in range(B):
                        q = slice(L * b, L * b + L)
                        last = te.matmul(TI[q, P + L * n:P + L * n + L], Ym[q, n, :], Tm[q, n, :], start=True, stop=True)
                last.then_inc(pe_t, 1)

            def chain_q(g, par, n):
                te.wait_ge(s_h, NCH * g + n + 1)
                h0 = H[(n + 1) % 2]
                for c in range(CT):
                    for b in range(B):
                        last = te.matmul(CQ[L * b:L * b + L, 0:1], U[par][:, (n * CT + c) * B + b, :],
                                         h0[:, c * B + b, L:L1], start=(c == 0), stop=(c == CT - 1))
                last.then_inc(pe_q, 1)

            def chain_p(g, par, n):
                te.wait_ge(s_qs, NCH * g + n + 1)
                te.matmul(CP[:, 0:P], qs[:, 0:1].broadcast_to([P, P]), Sd[par][:, n, :, :],
                          start=True, stop=True).then_inc(pe_p, 1)

            te.wait_ge(s_wce, 4)
            for c in range(CT):
                project("z", 0, 0, c)
            for c in range(CT):
                project("l", 0, 0, c)

            def body(g, par, chain, do_vx, do_zl):
                nxt = 1 - par
                if chain:
                    chain_q(g, par, 0)
                if do_vx:
                    project("v", g + 1, nxt, 0)
                if chain:
                    chain_p(g, par, 0)
                if do_vx:
                    for c in range(1, CT):
                        project("v", g + 1, nxt, c)
                if chain:
                    chain_q(g, par, 1)
                if do_vx:
                    project("x", g + 1, nxt, 0)
                if chain:
                    chain_p(g, par, 1)
                if do_vx:
                    for c in range(1, CT):
                        project("x", g + 1, nxt, c)
                if chain:
                    chain_q(g, par, 2)
                if do_zl:
                    project("z", g + 2, par, 0)
                if chain:
                    chain_p(g, par, 2)
                if do_zl:
                    project("z", g + 2, par, 1)
                if do_vx:
                    gram(g + 1, nxt)
                if do_zl:
                    project("z", g + 2, par, 2)
                if do_vx:
                    level_y(g + 1, 0)
                if do_zl:
                    project("z", g + 2, par, 3)
                if do_vx:
                    level_t(g + 1, 0)
                if chain:
                    chain_q(g, par, 3)
                if do_zl:
                    project("l", g + 2, par, 0)
                if chain:
                    chain_p(g, par, 3)
                for lv in range(1, len(LEVELS)):
                    if do_vx:
                        level_y(g + 1, lv)
                    if do_zl:
                        project("l", g + 2, par, lv)
                    if do_vx:
                        level_t(g + 1, lv)

            group_loop(body)
            te.wait_ge(s_flag, 2)
            te.matmul(CQ[0:1, 1:2], rng[:, 1:2], keep[:, 0, 1:2], start=True, stop=True).then_inc(s_flag, 1)

        @block.scalar
        def _(act):
            act.wait_ge(s_slope, 2)
            act.activation(sp[:, 1], sp[:, 0], ACT.Exp, scale=-1.0).then_inc(s_slope, 1)
            act.wait_ge(s_slope, 4)
            act.activation(sp[:, 3], sp[:, 2], ACT.Ln).then_inc(s_slope, 1)
            for i in range(4):
                act.wait_ge(s_wc, i + 1)
                act.activation(wc[:, i // 2, i % 2, :], PJ[i][:, :], ACT.Copy).then_inc(s_wce, 1)
            act.wait_ge(ld["small"], 80)
            act.wait_ge(s_const, 8)

            def bank_view(c):
                return PJ[c][:, :].rearrange("p (b n l) -> p b n l", b=B, n=NCH)

            def evac_z(G, c):
                act.wait_ge(pe["z"], CT * G + c + 1)
                if not (isinstance(G, int) and G == 0 and c < 2):
                    act.wait_ge(ev["z"], CT * G + c - 1)
                act.activation(sz[:, c % 2, :], PJ[c][:, :], ACT.Sigmoid).then_inc(act_sz, 1)

            def evac_l(G, par, c):
                act.wait_ge(pe["l"], CT * G + c + 1)
                act.activation(seg(lam[par], 0, c)[:, :, :, 1:L1], bank_view(c), ACT.Sigmoid,
                               bias=bias[:, 0, c:c + 1]).then_inc(ev["l"], 1)

            def evac_y(G, lv):
                act.wait_ge(pe_y, len(LEVELS) * G + lv + 1)
                act.activation(Ym[:, :, :].rearrange("p n l -> p (n l)"), TI[:, 0:P], ACT.Copy).then_inc(act_y, 1)

            for c in range(CT):
                evac_z(0, c)
            for c in range(CT):
                evac_l(0, 0, c)

            def body(g, par, chain, do_vx, do_zl):
                nxt = 1 - par
                G = g + 1
                if do_vx:
                    if chain:
                        act.wait_ge(s_h, NCH * g + 1)
                    for c in range(CT):
                        act.wait_ge(pe["v"], CT * G + c + 1)
                        act.activation(seg(V[nxt], 0, c), bank_view(c), ACT.Identity,
                                       bias=bias[:, 1, c:c + 1]).then_inc(ev["v"], 1)
                    act.wait_ge(s_scan, NCH * (G + 1))
                    for c in range(CT):
                        act.activation(seg(U[nxt], 0, c), seg(S, 0, c)[:, :, :, 0:L], ACT.Exp,
                                       scale=slope[:, 0, c:c + 1]).then_inc(s_gex, 1)
                    for c in range(CT):
                        lc = seg(lam[nxt], 0, c)[:, :, :, 1:L1]
                        act.activation(lc, lc, ACT.Exp, scale=slope[:, 0, c:c + 1]).then_inc(s_lam, 1)
                    act.wait_ge(s_gex, CT * (G + 1))
                    for c in range(CT):
                        sc = seg(S, 0, c)
                        act.activation(sc, sc, ACT.Exp, scale=slope[:, 1, c:c + 1]).then_inc(s_ginv, 1)
                    for c in range(CT):
                        act.wait_ge(pe["x"], CT * G + c + 1)
                        act.activation(seg(X[nxt], 0, c), bank_view(c), ACT.Copy).then_inc(ev["x"], 1)
                if do_zl:
                    evac_z(g + 2, 0)
                    evac_z(g + 2, 1)
                    evac_z(g + 2, 2)
                if do_vx:
                    evac_y(G, 0)
                if do_zl:
                    evac_z(g + 2, 3)
                    if chain:
                        act.wait_ge(s_h, NCH * (g + 1) + 1)
                    evac_l(g + 2, par, 0)
                for lv in range(1, len(LEVELS)):
                    if do_vx:
                        evac_y(G, lv)
                    if do_zl:
                        evac_l(g + 2, par, lv)

            group_loop(body)

        @block.vector
        def _(dve):
            consts = [(lam[0], 0.0), (lam[1], 0.0), (S, 0.0), (keep, 1.0), (E, 0.0), (Sd[0], 0.0), (Sd[1], 0.0)]
            for i, (t, val) in enumerate(consts):
                dve.memset(t[:], val).then_inc(s_const, 1)
            dve.wait_ge(s_const, len(consts))
            dve.memset(keep[:, :, 0:1], 0.0).then_inc(s_const, 1)
            dve.wait_ge(s_const, 8)

            dve.wait_ge(ld["small"], 80)
            om = bias[:, 2, :]
            dve.tensor_scalar(sp[:, 4], om, -1.0, None, ALU.mult).then_inc(s_slope, 1)
            dve.wait_ge(s_slope, 1)
            dve.tensor_tensor(sp[:, 0], om, sp[:, 4], ALU.max).then_inc(s_slope, 1)
            dve.wait_ge(s_slope, 3)
            dve.tensor_scalar(sp[:, 2], sp[:, 1], 1.0, None, ALU.add).then_inc(s_slope, 1)
            dve.wait_ge(s_slope, 5)
            steps = [
                lambda: dve.tensor_scalar(sp[:, 4], sp[:, 2], 1.0, None, ALU.subtract),
                lambda: dve.tensor_scalar(sp[:, 5], sp[:, 4], 0.0, None, ALU.is_equal),
                lambda: dve.tensor_tensor(sp[:, 4], sp[:, 4], sp[:, 5], ALU.add),
                lambda: dve.reciprocal(sp[:, 6], sp[:, 4]),
                lambda: dve.tensor_tensor(sp[:, 3], sp[:, 3], sp[:, 6], ALU.mult),
                lambda: dve.tensor_tensor(sp[:, 3], sp[:, 3], sp[:, 5], ALU.add),
                lambda: dve.tensor_tensor(sp[:, 3], sp[:, 3], sp[:, 1], ALU.mult),
                lambda: dve.scalar_tensor_tensor(sp[:, 7], om, 0.0, sp[:, 3], ALU.max, ALU.add),
                lambda: dve.tensor_scalar(slope[:, 0], sp[:, 7], -8.0, None, ALU.mult),
                lambda: dve.tensor_scalar(slope[:, 1], sp[:, 7], 8.0, None, ALU.mult),
            ]
            for i, f in enumerate(steps):
                f().then_inc(s_slope, 1)
                dve.wait_ge(s_slope, 6 + i)

            def mul_z(G, c):
                dve.wait_ge(act_sz, CT * G + c + 1)
                out = HG[:, c, :, :].rearrange("p b (g t) -> p g b t", t=GT)[:, G]
                dve.tensor_tensor(out, PJ[c][:, :].rearrange("p (b t) -> p b t", b=B),
                                  sz[:, c % 2, :].rearrange("p (b t) -> p b t", b=B), ALU.mult).then_inc(ev["z"], 1)

            def flat(t, n):
                return t[:, n * CB:(n + 1) * CB, :].rearrange("p s l -> p (s l)")

            def prefix(G, par):
                dve.wait_ge(ev["l"], CT * (G + 1))
                if isinstance(G, int) and G == 0:
                    dve.memset(lam[par][:, 0:CB, 1:2], 0.0).then_inc(s_fix, 1)
                    dve.wait_ge(s_fix, 1)
                else:
                    dve.wait_ge(s_ginv, CT * G)
                for n in range(NCH):
                    dve.tensor_tensor_scan(flat(S, n), keep[:, :, :].rearrange("p s l -> p (s l)"), flat(lam[par], n),
                                           0.0, ALU.mult, ALU.add).then_inc(s_scan, 1)

            def make_u(G, par):
                dve.wait_ge(ev["v"], CT * (G + 1))
                if isinstance(G, int) and G == 0:
                    dve.memset(V[par][:, 0:CB, 0:1], 0.0).then_inc(s_fix, 1)
                    dve.wait_ge(s_fix, 2)
                dve.wait_ge(s_gex, CT * (G + 1))
                dve.tensor_tensor(U[par][:, :, :], U[par][:, :, :], V[par][:, :, :], ALU.mult).then_inc(s_u, 1)

            def make_k(G, par):
                dve.wait_ge(s_ginv, CT * (G + 1))
                if not (isinstance(G, int) and G == 0):
                    dve.wait_ge(pe_gram, G)
                dve.tensor_tensor(KB[:, :, 0, :], V[par][:, :, :], S[:, :, 0:L], ALU.mult).then_inc(s_kb, 1)
                dve.tensor_reduce(rng[:, G:G + 1], S[:, :, L], AX.X, ALU.max).then_inc(s_rng, 1)
                dve.wait_ge(s_lam, CT * (G + 1))
                dve.wait_ge(s_kb, 2 * G + 1)
                dve.tensor_tensor(V[par][:, :, :], V[par][:, :, :], lam[par][:, :, 1:L1], ALU.mult).then_inc(s_a, 1)

            def make_b(G, par):
                dve.wait_ge(ev["x"], CT * (G + 1))
                if isinstance(G, int) and G == 0:
                    dve.tensor_copy(H[1][:, :, L], X[0][:, 0:CB, 0]).then_inc(s_h, 1)
                    dve.wait_ge(s_h, 1)
                dve.scalar_tensor_tensor(X[par][:, :, :], lam[par][:, :, 1:L1], 1.0, X[par][:, :, :],
                                         ALU.subtract, ALU.mult).then_inc(s_nb, 1)
                dve.wait_ge(s_nb, G + 1)
                dve.tensor_tensor(KB[:, :, 1, :], X[par][:, :, :], S[:, :, 1:L1], ALU.mult).then_inc(s_kb, 1)

            def mask(k):
                return tri[:, k, :].unsqueeze(1).broadcast_to([P, NCH, L])

            def t_start(G, par):
                base = TOPS * G
                dve.wait_ge(pe_gram, G + 1)
                A = GR[:, 0:2 * L * NCH].rearrange("p (n two l) -> p n two l", n=NCH, two=2)
                both = tri[:, 0:2, :].unsqueeze(1).broadcast_to([P, NCH, 2, L])
                dve.tensor_tensor(gm[:, :, :, :], A, both, ALU.mult).then_inc(s_t, 1)
                dve.wait_ge(s_t, base + 1)
                dve.tensor_reduce(vc[:, :, :], gm[:, :, :, :], AX.X, ALU.add).then_inc(s_t, 1)
                dve.wait_ge(s_t, base + 2)
                if isinstance(G, int) and G == 0:
                    for b in range(B):
                        dve.memset(vc[L * b:L * b + 1, 0, 0:1], 1.0).then_inc(s_fix, 1)
                    dve.wait_ge(s_fix, 2 + B)
                dve.reciprocal(w[par][:, :], vc[:, :, 0]).then_inc(s_t, 1)
                dve.wait_ge(s_t, base + 3)
                dve.tensor_scalar(w[par][:, :], w[par][:, :], -2.0, None, ALU.mult).then_inc(s_t, 1)
                dve.tensor_copy(negc[par][:, :], vc[:, :, 1]).then_inc(s_t, 1)
                dve.tensor_tensor(N[:, :, :], A[:, :, 0, :], mask(1), ALU.mult).then_inc(s_t, 1)
                dve.wait_ge(s_t, base + 6)
                dve.tensor_tensor(N[:, :, :], N[:, :, :], w[par][:, :].unsqueeze(2).broadcast_to([P, NCH, L]),
                                  ALU.mult).then_inc(s_t, 1)
                dve.wait_ge(s_t, base + 7)
                dve.tensor_tensor(Tm[:, :, :], N[:, :, :], mask(2), ALU.mult).then_inc(s_t, 1)
                dve.wait_ge(s_t, base + 8)
                dve.tensor_tensor(Tm[:, :, :], Tm[:, :, :], mask(0), ALU.add).then_inc(s_t, 1)
                dve.wait_ge(s_t, base + 9)
                dve.transpose(St[:, :, :], Tm[:, :, :]).then_inc(s_t, 1)
                dve.wait_ge(s_t, base + 10)

            def level(G, par, lv):
                base = TOPS * G + TSTART + 3 * lv
                dve.wait_ge(pe_t, len(LEVELS) * G + lv + 1)
                R = TI[:, P:2 * P].rearrange("p (n l) -> p n l", n=NCH)
                dve.tensor_tensor(gm[:, :, 0, :], R, mask(3 + lv), ALU.mult).then_inc(s_t, 1)
                dve.wait_ge(s_t, base + 1)
                dve.tensor_tensor(Tm[:, :, :], Tm[:, :, :], gm[:, :, 0, :], ALU.add).then_inc(s_t, 1)
                dve.wait_ge(s_t, base + 2)
                if lv < len(LEVELS) - 1:
                    dve.transpose(St[:, :, :], Tm[:, :, :]).then_inc(s_t, 1)
                    dve.wait_ge(s_t, base + 3)
                else:
                    for b in range(B):
                        q = slice(L * b, L * b + L)
                        dve.transpose(Sd[par][q, :, b, :], Tm[q, :, :]).then_inc(s_t, 1)
                    dve.wait_ge(s_t, base + 2 + B)

            def chain(g, par, n):
                q = NCH * g + n
                h0, h1 = H[(n + 1) % 2], H[n % 2]
                s0 = n * CB
                dve.tensor_copy(E[:, :, 0:1], h0[:, :, L:L1]).then_inc(s_e, 1)
                dve.wait_ge(pe_q, q + 1)
                dve.tensor_scalar(qs[:, 0:1], CQ[:, 0:1], negc[par][:, n:n + 1], w[par][:, n:n + 1],
                                  ALU.subtract, ALU.mult).then_inc(s_qs, 1)
                dve.wait_ge(pe_p, q + 1)
                p_all = CP[:, 0:P].rearrange("p (b l) -> p b l", b=B).unsqueeze(1).broadcast_to([P, CT, B, L])
                dve.tensor_tensor(E[:, :, 1:L1].rearrange("p (c b) l -> p c b l", c=CT),
                                  V[par][:, s0:s0 + CB, :].rearrange("p (c b) l -> p c b l", c=CT), p_all,
                                  ALU.mult).then_inc(s_e, 1)
                dve.wait_ge(s_e, 3 * q + 2)
                dve.tensor_tensor(E[:, :, 1:L1], E[:, :, 1:L1], X[par][:, s0:s0 + CB, :], ALU.subtract).then_inc(s_e, 1)
                dve.wait_ge(s_e, 3 * q + 3)
                dve.tensor_tensor_scan(h1[:, :, :].rearrange("p s l -> p (s l)"), flat(lam[par], n),
                                       E[:, :, :].rearrange("p s l -> p (s l)"), 0.0, ALU.mult, ALU.add).then_inc(s_h, 1)
                dve.wait_ge(s_h, q + 2)
                t0 = L * n
                hg = HG[:, :, :, :].rearrange("p c b (g t) -> p g (c b) t", t=GT)[:, g][:, :, t0:t0 + L]
                dve.tensor_tensor(hg, hg, h1[:, :, 1:L1], ALU.mult).then_inc(s_g, 1)
                dve.wait_ge(s_g, q + 1)

            for c in range(CT):
                mul_z(0, c)

            def body(g, par, do_chain, do_vx, do_zl):
                nxt = 1 - par
                if do_chain:
                    chain(g, par, 0)
                if do_vx:
                    prefix(g + 1, nxt)
                    make_u(g + 1, nxt)
                if do_chain:
                    chain(g, par, 1)
                if do_vx:
                    make_k(g + 1, nxt)
                    make_b(g + 1, nxt)
                if do_chain:
                    chain(g, par, 2)
                if do_zl:
                    mul_z(g + 2, 0)
                    mul_z(g + 2, 1)
                if do_vx:
                    t_start(g + 1, nxt)
                if do_zl:
                    mul_z(g + 2, 2)
                    mul_z(g + 2, 3)
                if do_vx:
                    level(g + 1, nxt, 0)
                if do_chain:
                    chain(g, par, 3)
                if do_vx:
                    for lv in range(1, len(LEVELS)):
                        level(g + 1, nxt, lv)

            group_loop(body)
            dve.wait_ge(s_rng, NG)
            dve.tensor_reduce(rng[:, 0:1], rng[:, :], AX.X, ALU.max).then_inc(s_flag, 1)
            dve.wait_ge(s_flag, 1)
            dve.tensor_scalar(rng[:, 1:2], rng[:, 0:1], SAFE, 0.0, ALU.is_le, ALU.is_equal).then_inc(s_flag, 1)
            dve.wait_ge(s_flag, 3)
            dve.tensor_scalar(cst["flag"][:, :], CQ[0:1, 1:2], 1.0, None, ALU.min).then_inc(s_flag, 1)


def general_recurrence_block(nc, dram, HG, cst):
    with ExitStack() as ctx:
        def sb(name, shape, dt=F32):
            return ctx.enter_context(nc.sbuf_tensor(name, shape, dt))

        def sem(name):
            return ctx.enter_context(nc.semaphore(name))

        bank = [ctx.enter_context(nc.psum_tensor(f"g_bank{i}", [P, 512], F32)) for i in range(8)]
        PJ, PC, SUM = bank[0:4], bank[4:6], bank[6]
        win_t = sb("g_win_t", [P, KD, 2 * DI])
        win_x = sb("g_win_x", [P, CT, D])
        wlv = sb("g_wlv", [P, 2, CT, DI])
        wc = sb("g_wc", [P, 2, KD, DI])
        xg = sb("g_x", [P, KD, B, GT])
        lam = sb("g_lam", [P, CB, GT])
        v = sb("g_v", [P, CB, GT])
        xi = sb("g_xi", [P, CB, GT])
        ones = sb("g_ones", [P, P])
        h = sb("g_h", [P, CB])
        pr = sb("g_pr", [P, 2, CB])
        sm = sb("g_sm", [P, 2, B])
        co = sb("g_co", [P, B])
        u = sb("g_u", [P, CB])
        s = {k: sem("g_" + k) for k in ("w", "x", "wc", "wce", "init", "pj", "sig", "ev", "lam", "evz", "fix", "nb",
                                        "pr", "sum", "step", "done")}
        SOPS = 8
        block = ctx.enter_context(nc.Block())

        def when_flagged(eng, program):
            value = eng.value_load(cst["flag"][0:1, 0:1], min_val=0, max_val=1)
            with eng.If(value):
                program()

        def groups(eng, body):
            body(0, True)
            with eng.Fori(1, NG) as g:
                body(g, False)

        @block.sync
        def _(sp):
            def program():
                sp.dma_start(wlv[:], dram["wlv_t"].rearrange("w (i p) j -> p w i j", p=P)).then_inc(s["w"], 16)
                sp.dma_start(win_x[:], dram["win"][0:DI, :].rearrange("(i p) d -> p i d", p=P)).then_inc(s["w"], 16)
                sp.dma_start(win_t[:], dram["win_t"].rearrange("(k p) n -> p k n", p=P)).then_inc(s["w"], 16)

                def body(g, first):
                    if not first:
                        sp.wait_ge(s["pj"], 4 * CT * g)
                    for k in range(KD):
                        src = dram["x_t"][k][:, :, bass.ds(g * GT, GT)]
                        sp.dma_start(xg[:, k], src).then_inc(s["x"], 16)
                groups(sp, body)
            when_flagged(sp, program)

        @block.tensor
        def _(te):
            def program():
                te.wait_ge(s["w"], 48)
                for j in range(2):
                    for m in range(KD):
                        for i in range(CT):
                            last = te.matmul(PJ[2 * j + m][:, :], win_x[:, i, m * P:(m + 1) * P], wlv[:, j, i, :],
                                             start=(i == 0), stop=(i == CT - 1))
                        last.then_inc(s["wc"], 1)
                te.wait_ge(s["wce"], 4)
                te.wait_ge(s["init"], 2)

                def body(g, first):
                    te.wait_ge(s["x"], (g + 1) * (16 * KD))
                    if not first:
                        te.wait_ge(s["done"], g)
                    for n in range(4 * CT):
                        kind, c = n // CT, n % CT
                        if kind == 1:
                            te.wait_ge(s["ev"], g * (3 * CT) + (c + 1))
                        if kind == 2:
                            te.wait_ge(s["evz"], g * CT + (c + 1))
                        if kind == 3:
                            te.wait_ge(s["ev"], g * (3 * CT) + (CT + c + 1))
                        for k in range(KD):
                            if kind in (0, 2):
                                lhs = wc[:, kind // 2, k, c * P:(c + 1) * P]
                            else:
                                o = DI * (kind == 1) + c * P
                                lhs = win_t[:, k, o:o + P]
                            last = te.matmul(PJ[n % 4][:, :], lhs, xg[:, k, :, :], start=(k == 0), stop=(k == KD - 1))
                        last.then_inc(s["pj"], 1)
                    with te.Fori(0, GT) as t:
                        te.wait_ge(s["pr"], (g * GT + t) * 2 + 2)
                        te.matmul(SUM[:, 0:2 * CB], ones[:, :], pr[:, :, :], start=True, stop=True).then_inc(s["sum"], 1)
                groups(te, body)
            when_flagged(te, program)

        @block.scalar
        def _(act):
            def program():
                for i in range(4):
                    act.wait_ge(s["wc"], i + 1)
                    act.activation(wc[:, i // 2, i % 2, :], PJ[i][:, :], ACT.Copy).then_inc(s["wce"], 1)

                def body(g, first):
                    for n in range(4 * CT):
                        kind, c = n // CT, n % CT
                        act.wait_ge(s["pj"], g * (4 * CT) + (n + 1))
                        flat = PJ[n % 4][:, :].rearrange("p (b t) -> p b t", b=B)
                        own = slice(c * B, c * B + B)
                        if kind == 0:
                            act.activation(lam[:, own, :], flat, ACT.Sigmoid, bias=cst["bias"][:, 0, c:c + 1]).then_inc(s["ev"], 1)
                        elif kind == 1:
                            act.activation(HG[:, c, :, bass.ds(g * GT, GT)], flat, ACT.Sigmoid).then_inc(s["sig"], 1)
                        elif kind == 2:
                            act.activation(v[:, own, :], flat, ACT.Identity, bias=cst["bias"][:, 1, c:c + 1]).then_inc(s["ev"], 1)
                        else:
                            act.activation(xi[:, own, :], flat, ACT.Copy).then_inc(s["ev"], 1)
                    for c in range(CT):
                        own = slice(c * B, c * B + B)
                        act.activation(lam[:, own, :], lam[:, own, :], ACT.Exp, scale=cst["slope"][:, 0, c:c + 1]).then_inc(s["lam"], 1)
                groups(act, body)
            when_flagged(act, program)

        @block.vector
        def _(dve):
            def program():
                dve.memset(ones[:, :], 1.0).then_inc(s["init"], 1)
                dve.memset(h[:, :], 0.0).then_inc(s["init"], 1)
                dve.wait_ge(s["init"], 2)

                def body(g, first):
                    for c in range(CT):
                        dve.wait_ge(s["sig"], g * CT + (c + 1))
                        hz = HG[:, c, :, bass.ds(g * GT, GT)]
                        dve.tensor_tensor(hz, hz, PJ[c][:, :].rearrange("p (b t) -> p b t", b=B), ALU.mult).then_inc(s["evz"], 1)
                    dve.wait_ge(s["evz"], (g + 1) * CT)
                    dve.wait_ge(s["ev"], (g + 1) * (3 * CT))
                    dve.wait_ge(s["lam"], (g + 1) * CT)
                    if first:
                        dve.memset(lam[:, :, 0:1], 0.0).then_inc(s["fix"], 1)
                        dve.memset(v[:, :, 0:1], 1.0).then_inc(s["fix"], 1)
                        dve.wait_ge(s["fix"], 2)
                    dve.scalar_tensor_tensor(xi[:, :, :], lam[:, :, :], 1.0, xi[:, :, :], ALU.subtract, ALU.mult).then_inc(s["nb"], 1)
                    with dve.Fori(0, GT) as t:
                        k = g * GT + t
                        at = bass.ds(t, 1)
                        vt = v[:, :, at].rearrange("p s o -> p (s o)")
                        lt = lam[:, :, at].rearrange("p s o -> p (s o)")
                        bt = xi[:, :, at].rearrange("p s o -> p (s o)")
                        dve.tensor_tensor(pr[:, 0, :], vt, h[:, :], ALU.mult).then_inc(s["pr"], 1)
                        dve.tensor_tensor(pr[:, 1, :], vt, vt, ALU.mult).then_inc(s["pr"], 1)
                        dve.wait_ge(s["sum"], k + 1)
                        dve.tensor_reduce(sm[:, :, :], SUM[:, 0:2 * CB].rearrange("p (two c b) -> p two b c", two=2, c=CT),
                                          AX.X, ALU.add).then_inc(s["step"], 1)
                        dve.wait_ge(s["step"], k * SOPS + 1)
                        dve.reciprocal(co[:, :], sm[:, 1, :]).then_inc(s["step"], 1)
                        dve.wait_ge(s["step"], k * SOPS + 2)
                        dve.scalar_tensor_tensor(co[:, :], co[:, :], -2.0, sm[:, 0, :], ALU.mult, ALU.mult).then_inc(s["step"], 1)
                        dve.wait_ge(s["step"], k * SOPS + 3)
                        dve.tensor_tensor(u[:, :].rearrange("p (c b) -> p c b", c=CT), vt.rearrange("p (c b) -> p c b", c=CT),
                                          co[:, :].unsqueeze(1).broadcast_to([P, CT, B]), ALU.mult).then_inc(s["step"], 1)
                        dve.wait_ge(s["step"], k * SOPS + 4)
                        dve.tensor_tensor(h[:, :], h[:, :], u[:, :], ALU.add).then_inc(s["step"], 1)
                        dve.wait_ge(s["step"], k * SOPS + 5)
                        dve.tensor_tensor(h[:, :], h[:, :], lt, ALU.mult).then_inc(s["step"], 1)
                        dve.wait_ge(s["step"], k * SOPS + 6)
                        dve.wait_ge(s["nb"], g + 1)
                        dve.tensor_tensor(h[:, :], h[:, :], bt, ALU.subtract).then_inc(s["step"], 1)
                        dve.wait_ge(s["step"], k * SOPS + 7)
                        hg = HG[:, :, :, bass.ds(k, 1)].rearrange("p c b o -> p (c b o)")
                        dve.tensor_tensor(hg, hg, h[:, :], ALU.mult).then_inc(s["step"], 1)
                        dve.wait_ge(s["step"], k * SOPS + SOPS)
                    dve.tensor_copy(co[:, :], sm[:, 0, :]).then_inc(s["done"], 1)
                    dve.wait_ge(s["done"], g + 1)
                groups(dve, body)
            when_flagged(dve, program)



NI = T // P
NT = B * NI
SR = 154
LANES = 32
CW = T // LANES
STEPS = SR + LANES - 1
PAD = LANES - 1
PITCH = SR + 2 * PAD
REC = CW + 1
BIG = 1e30
EPS = 1e-5
KF = KD


def view(t, off, *dims):
    return bass.AP(tensor=t.tensor, offset=t.offset + off, ap=[list(t.ap[0])] + [list(d) for d in dims])


def token_tile(t, i):
    return t[:, i % B, (i // B) * P:(i // B + 1) * P]


def project_and_distance_block(nc, dram, HG, X1, Zd, cst):
    with ExitStack() as ctx:
        def sb(name, shape, dt=F32):
            return ctx.enter_context(nc.sbuf_tensor(name, shape, dt))

        def sem(name):
            return ctx.enter_context(nc.semaphore(name))

        bank = [ctx.enter_context(nc.psum_tensor(f"b_bank{i}", [P, 512], F32)) for i in range(8)]
        PO, PT, PD, PA, PB = bank[0:2], bank[2:4], bank[4:6], bank[6], bank[7]
        wout = sb("wout", [P, CT, D])
        ctxT = sb("ctxT", [P, KD, B, SR])
        sq = sb("sq", [P, KD, B, SR])
        AA = sb("AA", [P, SR])
        x1T = sb("x1T", [P, KD, B, T])
        st = sb("st", [P, 2, 6])
        mv = sb("mv", [P, NT, 2])
        sd = sb("sd", [P, NT])
        rs = sb("rs", [P, NT])
        ssq = sb("ssq", [P, NT])
        junk = sb("junk", [P, 2, D])
        mb = sb("mb", [P, B, 4])
        bb = sb("bb", [P, LANES])
        ones = sb("ones", [P, L])

        ld_w, ld_x, ld_c = sem("b_ld_w"), sem("b_ld_x"), sem("b_ld_c")
        s_sq, s_one, pe_aa, s_aa = sem("b_sq"), sem("b_one"), sem("pe_aa"), sem("s_aa")
        pe_o, s_add, s_st, s_mv, s_sd, s_rs, s_x1 = (sem("b_" + k) for k in ("pe_o", "add", "st", "mv", "sd", "rs", "x1"))
        s_ssq, pe_tr, s_x1T, s_mb, pe_bb, s_bb = (sem("b_" + k) for k in ("ssq", "pe_tr", "x1T", "mb", "pe_bb", "bb"))
        pe_d, s_d2, s_cl, s_zd, s_pad = (sem("b_" + k) for k in ("pe_d", "d2", "cl", "zd", "pad"))
        block = ctx.enter_context(nc.Block())

        @block.sync
        def _(sp):
            sp.dma_start(wout[:, :, :], dram["wout_t"].rearrange("(c p) d -> p c d", p=P)).then_inc(ld_w, 16)
            xt = dram["x_tok"].rearrange("(b i p) d -> p i b d", b=B, p=P)
            for i in range(NI):
                sp.dma_start(X1[:, i * B:(i + 1) * B, :], xt[:, i]).then_inc(ld_x, 16)
            sp.dma_start(ctxT[:, :, :, :], dram["ctx_t"].rearrange("k p b s -> p k b s")).then_inc(ld_c, 16)

        @block.tensor
        def _(te):
            def attention_out(i):
                if i == 0:
                    te.wait_ge(ld_w, 16)
                if i >= 2:
                    te.wait_ge(s_add, i - 1)
                for c in range(CT):
                    last = te.matmul(PO[i % 2][:, 0:D], token_tile(HG[:, c], i), wout[:, c, :],
                                     start=(c == 0), stop=(c == CT - 1))
                last.then_inc(pe_o, 1)

            def turn(i):
                te.wait_ge(s_x1, i + 1)
                if i >= 2:
                    te.wait_ge(s_x1T, i - 1)
                for k in range(KD):
                    last = te.transpose(PT[i % 2][:, k * P:(k + 1) * P], X1[:, i, k * P:(k + 1) * P], cst["eye"][:, :])
                last.then_inc(pe_tr, 1)

            def norms(t):
                te.wait_ge(s_mb, t + 1)
                for b in range(B):
                    last = te.matmul(PB[L * b:L * b + L, 4 * t:4 * t + 4], cst["tri"][:, 0, :], mb[:, b, :],
                                     start=True, stop=True)
                last.then_inc(pe_bb, 1)

            def distances(t):
                te.wait_ge(s_x1T, B * (t + 1))
                for h in range(2):
                    pair = 2 * t + h
                    if pair >= 2:
                        te.wait_ge(s_d2, 2 * (pair - 1))
                    for s in range(2):
                        j0 = (2 * pair + s) * CW
                        for k in range(KD):
                            for b in range(B):
                                last = te.matmul(PD[h][L * b:L * b + L, s * SR:(s + 1) * SR], x1T[:, k, b, j0:j0 + CW],
                                                 ctxT[:, k, b, :], start=(k == 0), stop=(k == KD - 1))
                    last.then_inc(pe_d, 1)

            te.wait_ge(s_one, 1)
            te.wait_ge(s_sq, 1)
            for k in range(KD):
                for b in range(B):
                    last = te.matmul(PA[L * b:L * b + L, 0:SR], ones[:, :], sq[:, k, b, :],
                                     start=(k == 0), stop=(k == KD - 1))
            last.then_inc(pe_aa, 1)
            te.wait_ge(s_sq, 2)
            for i in range(NT + 3):
                if i < NT:
                    attention_out(i)
                if 3 <= i:
                    turn(i - 3)
                    if i % B == 2:
                        norms((i - 3) // B)
                        distances((i - 3) // B)

        @block.scalar
        def _(act):
            act.wait_ge(s_pad, 3)
            act.wait_ge(pe_aa, 1)
            act.activation(AA[:, :], PA[:, 0:SR], ACT.Copy).then_inc(s_aa, 1)
            for i in range(NT + 3):
                if i < NT:
                    act.wait_ge(s_mv, i + 1)
                    act.activation(sd[:, i:i + 1], mv[:, i, 1:2], ACT.Sqrt, bias=cst["eps"][:, 0:1]).then_inc(s_sd, 1)
                if 1 <= i <= NT:
                    j = i - 1
                    act.wait_ge(s_x1, j + 1)
                    if j >= 2:
                        act.wait_ge(s_ssq, j - 1)
                    act.activation(junk[:, j % 2, :], X1[:, j, :], ACT.Square, accum_out=ssq[:, j:j + 1]).then_inc(s_ssq, 1)
                if 3 <= i:
                    j = i - 3
                    act.wait_ge(pe_tr, j + 1)
                    out = x1T[:, :, j % B, (j // B) * P:(j // B + 1) * P]
                    act.activation(out, PT[j % 2][:, 0:KD * P].rearrange("p (k t) -> p k t", k=KD),
                                   ACT.Copy).then_inc(s_x1T, 1)
                    if i % B == 2:
                        t = j // B
                        for h in range(2):
                            pair = 2 * t + h
                            act.wait_ge(s_cl, pair + 1)
                            z = Zd[:, 2 * pair:2 * pair + 2, PAD:PAD + SR]
                            act.activation(z, z, ACT.Sqrt).then_inc(s_zd, 1)

        @block.vector
        def _(dve):
            dve.memset(ones[:, :], 1.0).then_inc(s_one, 1)
            dve.memset(Zd[:, :, 0:PAD], BIG).then_inc(s_pad, 1)
            dve.memset(Zd[:, :, PAD + SR:PITCH], BIG).then_inc(s_pad, 1)
            dve.memset(cst["eps"][:, :], EPS).then_inc(s_pad, 1)
            dve.wait_ge(ld_c, 16)
            dve.tensor_tensor(sq[:], ctxT[:], ctxT[:], ALU.mult).then_inc(s_sq, 1)
            dve.wait_ge(s_sq, 1)
            dve.tensor_scalar(ctxT[:], ctxT[:], -2.0, None, ALU.mult).then_inc(s_sq, 1)
            dve.wait_ge(s_aa, 1)
            for i in range(NT + 4):
                if i < NT:
                    if i % B == 0:
                        dve.wait_ge(ld_x, 16 * (i // B + 1))
                    dve.wait_ge(pe_o, i + 1)
                    dve.tensor_tensor(X1[:, i, :], X1[:, i, :], PO[i % 2][:, 0:D], ALU.add).then_inc(s_add, 1)
                    dve.wait_ge(s_add, i + 1)
                    dve.bn_stats(st[:, i % 2, :], X1[:, i, :]).then_inc(s_st, 1)
                    dve.wait_ge(s_st, i + 1)
                    dve.bn_aggr(mv[:, i, :], st[:, i % 2, :]).then_inc(s_mv, 1)
                if 1 <= i <= NT:
                    j = i - 1
                    dve.wait_ge(s_sd, j + 1)
                    dve.reciprocal(rs[:, j:j + 1], sd[:, j:j + 1]).then_inc(s_rs, 1)
                    dve.wait_ge(s_rs, j + 1)
                    dve.wait_ge(s_mv, j + 1)
                    dve.tensor_scalar(X1[:, j, :], X1[:, j, :], mv[:, j, 0:1], rs[:, j:j + 1],
                                      ALU.subtract, ALU.mult).then_inc(s_x1, 1)
                if i >= 2 and (i - 2) % B == B - 1 and i - 2 < NT:
                    t = (i - 2) // B
                    dve.wait_ge(s_ssq, B * (t + 1))
                    if t >= 1:
                        dve.wait_ge(pe_bb, t)
                    dve.tensor_tensor(mb[:, :, :], ssq[:, B * t:B * t + B].unsqueeze(2).broadcast_to([P, B, 4]),
                                      cst["quad"][:, :].unsqueeze(1).broadcast_to([P, B, 4]), ALU.mult).then_inc(s_mb, 1)
                if i >= 4 and (i - 4) % B == B - 1:
                    t = (i - 4) // B
                    dve.wait_ge(pe_bb, t + 1)
                    dve.tensor_copy(bb[:, 4 * t:4 * t + 4], PB[:, 4 * t:4 * t + 4]).then_inc(s_bb, 1)
                    dve.wait_ge(s_bb, t + 1)
                    for h in range(2):
                        pair = 2 * t + h
                        dve.wait_ge(pe_d, pair + 1)
                        for s in range(2):
                            jb = 2 * pair + s
                            dve.scalar_tensor_tensor(Zd[:, jb, PAD:PAD + SR], PD[h][:, s * SR:(s + 1) * SR],
                                                     bb[:, jb:jb + 1], AA[:, :], ALU.add, ALU.add).then_inc(s_d2, 1)
                        dve.wait_ge(s_d2, 2 * (pair + 1))
                        z = Zd[:, 2 * pair:2 * pair + 2, PAD:PAD + SR]
                        dve.tensor_scalar(z, z, 0.0, None, ALU.max).then_inc(s_cl, 1)


def alignment_block(nc, dram, HG, Zd, PTa, PTb, Cs, Mf, cst):
    with ExitStack() as ctx:
        def sb(name, shape, dt=F32):
            return ctx.enter_context(nc.sbuf_tensor(name, shape, dt))

        def sem(name):
            return ctx.enter_context(nc.semaphore(name))

        Dof, Rof = 0, STEPS * REC
        assert Rof + (STEPS + 1) * REC + 1 + LANES * PITCH // 2 <= CT * B * T
        HGf = HG[:, :, :, :].rearrange("p c b t -> p (c b t)")
        Dk = HGf[:, Dof:Dof + STEPS * REC].rearrange("p (k j) -> p k j", j=REC)
        R = HGf[:, Rof:Rof + (STEPS + 1) * REC].rearrange("p (k j) -> p k j", j=REC)
        M = [sb(f"M{i}", [P, REC]) for i in range(2)]
        edge = sb("edge", [P, 1])
        back = sb("back", [P, 1], BF16)
        PR = 2 * CW
        one_left = sb("one_left", [P, STEPS, PR], BF16)
        up_diag = sb("up_diag", [P, STEPS, PR], BF16)
        G = [sb(f"G{i}", [P, PR], BF16) for i in range(2)]
        Pk = Zd[:, :, :].rearrange("p j i -> p (j i)")[:, 0:STEPS * PR // 2].bitcast(BF16).rearrange("p (k m) -> p k m", m=PR)
        Zof = Rof + (STEPS + 1) * REC + 1
        Zq = HGf[:, Zof:Zof + LANES * PITCH // 2].bitcast(BF16).rearrange("p (j i) -> p j i", i=PITCH)
        eyeb = sb("eyeb", [P, P], BF16)
        room = [t[:, :, :].rearrange("p j i -> p (j i)").bitcast(F32) for t in (PTa, PTb)]
        trg = [room[0][:, i * KF * D:(i + 1) * KF * D].rearrange("p (k d) -> p k d", k=KF) for i in range(3)]
        wri = room[1][:, 0:2 * KF * D].rearrange("p (w k d) -> p w k d", w=2, k=KF)
        p12 = room[1][:, 2 * KF * D:4 * KF * D].rearrange("p (o k d) -> p o k d", o=2, k=KF)
        cf = sb("cf", [P, B, D])
        bank = [ctx.enter_context(nc.psum_tensor(f"c_bank{i}", [P, 512], F32)) for i in range(4)]
        tb = [ctx.enter_context(nc.psum_tensor(f"c_tb{i}", [P, 8, P], BF16)) for i in range(4)]

        ld_f, ld_c = sem("c_ld_f"), sem("c_ld_c")
        s_init, s_skew, s_min, s_row, s_edge = (sem("c_" + k) for k in ("init", "skew", "min", "row", "edge"))
        s_ch, s_bw, s_g, s_back, s_path = (sem("c_" + k) for k in ("ch", "bw", "g", "back", "path"))
        s_zq, pe_z, s_pt, s_split, pe_m, s_m, s_cz = (sem("c_" + k) for k in ("zq", "pe_z", "pt", "split", "pe_m", "m", "cz"))
        block = ctx.enter_context(nc.Block())
        REM = SR - P

        @block.sync
        def _(sp):
            for i, k in enumerate(("cos", "sin", "msin")):
                sp.dma_start(trg[i][:, :, :], dram[k].rearrange("(k p) n -> p k n", p=P)).then_inc(ld_f, 16)
            for i, k in enumerate(("w_re", "w_im")):
                sp.dma_start(wri[:, i], dram[k].rearrange("(k p) n -> p k n", p=P)).then_inc(ld_f, 16)
            cr = dram["ctx"].rearrange("b s d -> s b d")
            sp.dma_start(cf[:, :, :], cr[0:P]).then_inc(ld_c, 16)
            sp.wait_ge(s_split, 5)
            sp.dma_start(cf[0:REM], cr[P:SR]).then_inc(ld_c, 16)

        @block.gpsimd
        def _(pool):
            n = 0
            for sl, rows in ((0, P), (1, REM)):
                pool.wait_ge(ld_c, 16 * (sl + 1))
                c = cf[0:rows]
                for part in range(3):
                    o = Cs[0:rows, sl, part]
                    pool.tensor_copy(o, c).then_inc(s_split, 1)
                    n += 1
                    pool.wait_ge(s_split, n)
                    if part < 2:
                        pool.tensor_tensor(c, c, o, ALU.subtract).then_inc(s_split, 1)
                        n += 1
                        pool.wait_ge(s_split, n)

        @block.tensor
        def _(te):
            te.wait_ge(ld_f, 80)
            terms = (((0, 0), (1, 1)), ((1, 0), (0, 2)))
            for o in range(2):
                for m in range(KF):
                    n = 0
                    for wi, tr in terms[o]:
                        for k in range(KF):
                            last = te.matmul(bank[2 * o + m][:, 0:D], wri[:, wi, k, m * P:(m + 1) * P], trg[tr][:, k, :],
                                             start=(n == 0), stop=(n == 3))
                            n += 1
                    last.then_inc(pe_m, 1)
            te.wait_ge(s_m, 4)
            for m in range(KF):
                n = 0
                for o, tr in ((0, 0), (1, 2)):
                    for k in range(KF):
                        last = te.matmul(bank[m][:, 0:D], p12[:, o, k, m * P:(m + 1) * P], trg[tr][:, k, :],
                                         start=(n == 0), stop=(n == 3))
                        n += 1
                last.then_inc(pe_m, 1)
            te.wait_ge(s_zq, 1)
            for q in range(LANES // 8):
                if q >= 2:
                    te.wait_ge(s_pt, 2 * (q - 1))
                for j in range(8):
                    jb = 8 * q + j
                    te.transpose(tb[q % 2][:, j, :], Zq[:, jb, PAD:PAD + P], eyeb[:, :])
                    last = te.transpose(tb[2 + q % 2][0:REM, j, :], Zq[:, jb, PAD + P:PAD + SR], eyeb[:, :])
                last.then_inc(pe_z, 1)

        @block.scalar
        def _(act):
            for i in range(4):
                act.wait_ge(pe_m, i + 1)
                act.activation(p12[:, i // 2, i % 2, :], bank[i][:, 0:D], ACT.Copy).then_inc(s_m, 1)
            for m in range(KF):
                act.wait_ge(pe_m, 5 + m)
                act.activation(Mf[:, m, :], bank[m][:, 0:D], ACT.Copy, scale=1.0 / D).then_inc(s_m, 1)
            for q in range(LANES // 8):
                act.wait_ge(pe_z, q + 1)
                for rows, pt, b0 in ((P, PTa, 0), (REM, PTb, 2)):
                    out = pt[0:rows].rearrange("p b (j l) -> p j b l", l=L)[:, 8 * q:8 * q + 8]
                    act.activation(out, tb[b0 + q % 2][0:rows].rearrange("p j (b l) -> p j b l", b=B),
                                   ACT.Copy).then_inc(s_pt, 1)

        @block.vector
        def _(dve):
            inits = [(R[:, 0, :], BIG), (M[0][:, :], BIG), (M[1][:, :], BIG), (edge[:, :], BIG), (G[0][:, :], 0.0),
                     (Dk[:, :, 0:1], 0.0), (one_left[:, :, :], 1.0)]
            for a, v in inits:
                dve.memset(a, v).then_inc(s_init, 1)
            dve.wait_ge(s_init, len(inits))
            n0 = len(inits)
            for b in range(B):
                o = slice(L * b, L * b + 1)
                dve.memset(M[0][o, 1:2], 0.0).then_inc(s_init, 1)
                dve.memset(Dk[o, :, 0:1], BIG).then_inc(s_init, 1)
            dve.tensor_copy(eyeb[:, :], cst["eye"][:, :]).then_inc(s_init, 1)
            dve.tensor_copy(back[:, :], cst["last"][:, :]).then_inc(s_init, 1)
            dve.wait_ge(s_init, n0 + 2 * B + 2)
            src = view(Zd[:, :, :], PAD, (1, STEPS), (PITCH - 1, LANES))
            dve.transpose(Dk[:, :, 1:REC], src).then_inc(s_skew, 1)
            dve.wait_ge(s_skew, 1)
            shift = [LANES - 1] + list(range(LANES - 1))
            for k in range(STEPS):
                m = M[k % 2]
                if k >= 1:
                    dve.wait_ge(s_row, k)
                    dve.stream_shuffle(edge[:, :], R[:, k, CW:REC], shift).then_inc(s_edge, 1)
                    dve.tensor_tensor(m[:, 1:REC], R[:, k, 1:REC], R[:, k, 0:CW], ALU.min).then_inc(s_min, 1)
                    dve.wait_ge(s_edge, k)
                    dve.wait_ge(s_min, k)
                dve.tensor_tensor_scan(R[:, k + 1, :], m[:, :], Dk[:, k, :], edge[:, 0:1],
                                       ALU.min, ALU.add).then_inc(s_row, 1)
            dve.wait_ge(s_row, STEPS)
            diag, up, left = R[:, 0:STEPS, 0:CW], R[:, 0:STEPS, 1:REC], R[:, 1:STEPS + 1, 0:CW]
            falling = (2 * STEPS, )
            up_o = view(up_diag[:, :, :], PR - 2, (PR, STEPS), (-2, CW))
            dg_o = view(up_diag[:, :, :], PR - 1, (PR, STEPS), (-2, CW))
            lf_o = view(one_left[:, :, :], PR - 1, (PR, STEPS), (-2, CW))
            best = Dk[:, :, 1:REC]
            dve.tensor_tensor(best, up, left, ALU.min).then_inc(s_ch, 1)
            dve.wait_ge(s_ch, 1)
            dve.tensor_tensor(dg_o, diag, best, ALU.is_le).then_inc(s_ch, 1)
            dve.wait_ge(s_ch, 2)
            dve.tensor_tensor(up_o, up, left, ALU.is_le).then_inc(s_ch, 1)
            dve.wait_ge(s_ch, 3)
            dve.tensor_tensor(best, up_o, dg_o, ALU.max).then_inc(s_ch, 1)
            dve.wait_ge(s_ch, 4)
            dve.tensor_scalar(lf_o, best, 0.0, None, ALU.is_equal).then_inc(s_ch, 1)
            dve.tensor_tensor(up_o, up_o, dg_o, ALU.is_gt).then_inc(s_ch, 1)
            dve.wait_ge(s_ch, 6)
            for b in range(B):
                o = slice(L * b, L * b + 1)
                dve.memset(up_diag[o, :, PR - 1:PR], 0.0).then_inc(s_cz, 1)
                dve.memset(one_left[o, :, PR - 1:PR], 0.0).then_inc(s_cz, 1)
            dve.wait_ge(s_cz, 2 * B)
            shift = list(range(1, LANES)) + [0]
            for n in range(STEPS):
                k = STEPS - 1 - n
                g = G[n % 2]
                if n >= 1:
                    dve.wait_ge(s_path, n)
                    dve.stream_shuffle(back[:, :], Pk[:, k + 1, PR - 1:PR], shift).then_inc(s_back, 1)
                    on = Pk[:, k + 1, :].rearrange("p (j two) -> p j two", two=2)[:, :, 0:1].broadcast_to([P, CW, 2])
                    dve.tensor_tensor(g[:, :].rearrange("p (j two) -> p j two", two=2),
                                      up_diag[:, k + 1, :].rearrange("p (j two) -> p j two", two=2), on,
                                      ALU.mult).then_inc(s_g, 1)
                    dve.wait_ge(s_back, n)
                    dve.wait_ge(s_g, n)
                dve.tensor_tensor_scan(Pk[:, k, :], one_left[:, k, :], g[:, :], back[:, 0:1],
                                       ALU.mult, ALU.add).then_inc(s_path, 1)
            dve.wait_ge(s_path, STEPS)
            dst = view(Zq, PAD, (1, STEPS), (PITCH - 1, LANES))
            dve.transpose(dst, view(Pk, PR - 2, (PR, STEPS), (-2, CW))).then_inc(s_zq, 1)


def output_block(nc, dram, X1, PTa, PTb, Cs, Mf, cst):
    REM = SR - P
    with ExitStack() as ctx:
        def sb(name, shape, dt=F32):
            return ctx.enter_context(nc.sbuf_tensor(name, shape, dt))

        def sem(name):
            return ctx.enter_context(nc.semaphore(name))

        bank = [ctx.enter_context(nc.psum_tensor(f"d_bank{i}", [P, 512], F32)) for i in range(6)]
        PE_, PT, PF = bank[0:2], bank[2:4], bank[4:6]
        x2T = sb("x2T", [P, 4, KD, P])
        xb = sb("xb", [P, 4, D])
        st = sb("d_st", [P, 4, 6])
        mv = sb("d_mv", [P, 2, NT, 2])
        sd = sb("d_sd", [P, 2, NT])
        rs = sb("d_rs", [P, 2, NT])
        bias = sb("d_bias", [P, D])
        s = {k: sem("d_" + k) for k in ("ld", "pe_x", "add", "st", "mv", "sd", "rs", "x2", "pe_t", "x2T", "pe_f", "xb",
                                        "add2", "st2", "mv2", "sd2", "rs2", "y", "out")}
        block = ctx.enter_context(nc.Block())
        LAG_T, LAG_F, LAG_Y = 3, 5, 7

        @block.sync
        def _(sp):
            sp.dma_start(bias[:, :], dram["ffn_bias"].rearrange("(o d) -> o d", o=1).broadcast_to([P, D])).then_inc(s["ld"], 16)
            ot = dram["out"].rearrange("(b i p) d -> p i b d", b=B, p=P)
            for i in range(NI):
                sp.wait_ge(s["y"], B * (i + 1))
                sp.dma_start(ot[:, i], X1[:, i * B:(i + 1) * B, :]).then_inc(s["out"], 16)
            sp.wait_ge(s["out"], 16 * NI)

        @block.tensor
        def _(te):
            for i in range(NT + LAG_F):
                if i < NT:
                    b, t = i % B, i // B
                    if i >= 2:
                        te.wait_ge(s["add"], i - 1)
                    n = 0
                    for sl, rows, pt in ((0, P, PTa), (1, REM, PTb)):
                        lhs = token_tile(pt[0:rows], i)
                        for part in range(3):
                            last = te.matmul(PE_[i % 2][:, 0:D], lhs, Cs[0:rows, sl, part, b, :], start=(n == 0), stop=(n == 5))
                            n += 1
                    last.then_inc(s["pe_x"], 1)
                if LAG_T <= i < NT + LAG_T:
                    j = i - LAG_T
                    te.wait_ge(s["x2"], j + 1)
                    if j >= 2:
                        te.wait_ge(s["x2T"], j - 1)
                    for k in range(KD):
                        last = te.transpose(PT[j % 2][:, k * P:(k + 1) * P], X1[:, j, k * P:(k + 1) * P], cst["eye"][:, :])
                    last.then_inc(s["pe_t"], 1)
                if LAG_F <= i:
                    j = i - LAG_F
                    te.wait_ge(s["x2T"], j + 1)
                    if j >= 2:
                        te.wait_ge(s["add2"], j - 1)
                    for k in range(KD):
                        last = te.matmul(PF[j % 2][:, 0:D], x2T[:, j % 4, k, :], Mf[:, k, :], start=(k == 0), stop=(k == KD - 1))
                    last.then_inc(s["pe_f"], 1)

        @block.gpsimd
        def _(pool):
            pool.wait_ge(s["ld"], 16)
            for i in range(NT):
                pool.wait_ge(s["x2"], i + 1)
                if i >= 4:
                    pool.wait_ge(s["add2"], i - 3)
                pool.tensor_tensor(xb[:, i % 4, :], X1[:, i, :], bias[:, :], ALU.add).then_inc(s["xb"], 1)

        @block.scalar
        def _(act):
            for i in range(NT + LAG_Y):
                if i < NT:
                    act.wait_ge(s["mv"], i + 1)
                    act.activation(sd[:, 0, i:i + 1], mv[:, 0, i, 1:2], ACT.Sqrt, bias=cst["eps"][:, 0:1]).then_inc(s["sd"], 1)
                if LAG_T <= i < NT + LAG_T:
                    j = i - LAG_T
                    act.wait_ge(s["pe_t"], j + 1)
                    if j >= 4:
                        act.wait_ge(s["pe_f"], j - 3)
                    act.activation(x2T[:, j % 4].rearrange("p k t -> p (k t)"), PT[j % 2][:, 0:KD * P], ACT.Copy).then_inc(s["x2T"], 1)
                if i >= LAG_Y - 1 and i - LAG_Y + 1 < NT:
                    j = i - LAG_Y + 1
                    act.wait_ge(s["mv2"], j + 1)
                    act.activation(sd[:, 1, j:j + 1], mv[:, 1, j, 1:2], ACT.Sqrt, bias=cst["eps"][:, 0:1]).then_inc(s["sd2"], 1)

        @block.vector
        def _(dve):
            def stats(i, half, m, a, b_, c_):
                slot = 2 * half + i % 2
                dve.wait_ge(s[a], i + 1)
                dve.bn_stats(st[:, slot, :], X1[:, i, :]).then_inc(s[b_], 1)
                dve.wait_ge(s[b_], i + 1)
                dve.bn_aggr(mv[:, half, i, :], st[:, slot, :]).then_inc(s[c_], 1)

            def normalize(j, half, d, e, c_, out):
                dve.wait_ge(s[d], j + 1)
                dve.reciprocal(rs[:, half, j:j + 1], sd[:, half, j:j + 1]).then_inc(s[e], 1)
                dve.wait_ge(s[e], j + 1)
                dve.wait_ge(s[c_], j + 1)
                dve.tensor_scalar(X1[:, j, :], X1[:, j, :], mv[:, half, j, 0:1], rs[:, half, j:j + 1],
                                  ALU.subtract, ALU.mult).then_inc(s[out], 1)

            for i in range(NT + LAG_Y + 1):
                if i < NT:
                    dve.wait_ge(s["pe_x"], i + 1)
                    dve.tensor_tensor(X1[:, i, :], X1[:, i, :], PE_[i % 2][:, 0:D], ALU.add).then_inc(s["add"], 1)
                    stats(i, 0, i, "add", "st", "mv")
                if 1 <= i <= NT:
                    normalize(i - 1, 0, "sd", "rs", "mv", "x2")
                if i >= LAG_Y - 1 and i - LAG_Y + 1 < NT:
                    j = i - LAG_Y + 1
                    dve.wait_ge(s["pe_f"], j + 1)
                    dve.wait_ge(s["xb"], j + 1)
                    dve.wait_ge(s["pe_t"], j + 1)
                    dve.tensor_tensor(X1[:, j, :], xb[:, j % 4, :], PF[j % 2][:, 0:D], ALU.add).then_inc(s["add2"], 1)
                    stats(j, 1, j, "add2", "st2", "mv2")
                if i >= LAG_Y and i - LAG_Y < NT:
                    normalize(i - LAG_Y, 1, "sd2", "rs2", "mv2", "y")


def build_program(nc, dram):
    with ExitStack() as ctx:
        HG = ctx.enter_context(nc.sbuf_tensor("HG", [P, CT, B, T], F32))
        cst = {"tri": ctx.enter_context(nc.sbuf_tensor("tri", [P, 8, L], F32)),
               "eye": ctx.enter_context(nc.sbuf_tensor("eye", [P, P], F32)),
               "quad": ctx.enter_context(nc.sbuf_tensor("quad", [P, 4], F32)),
               "last": ctx.enter_context(nc.sbuf_tensor("last", [P, 1], F32)),
               "bias": ctx.enter_context(nc.sbuf_tensor("bias", [P, 3, CT], F32)),
               "slope": ctx.enter_context(nc.sbuf_tensor("slope", [P, 2, CT], F32)),
               "flag": ctx.enter_context(nc.sbuf_tensor("flag", [1, 1], I32)),
               "eps": ctx.enter_context(nc.sbuf_tensor("eps", [P, 1], F32))}
        recurrence_block(nc, dram, HG, cst)
        general_recurrence_block(nc, dram, HG, cst)
        X1 = ctx.enter_context(nc.sbuf_tensor("x_all", [P, NT, D], F32))
        Zd = ctx.enter_context(nc.sbuf_tensor("Zd", [P, LANES, PITCH], F32))
        project_and_distance_block(nc, dram, HG, X1, Zd, cst)
        PTa = ctx.enter_context(nc.sbuf_tensor("PTa", [P, B, T], BF16))
        PTb = ctx.enter_context(nc.sbuf_tensor("PTb", [P, B, T], BF16))
        Cs = ctx.enter_context(nc.sbuf_tensor("Cs", [P, 2, 3, B, D], BF16))
        Mf = ctx.enter_context(nc.sbuf_tensor("Mf", [P, KF, D], F32))
        alignment_block(nc, dram, HG, Zd, PTa, PTb, Cs, Mf, cst)
        output_block(nc, dram, X1, PTa, PTb, Cs, Mf, cst)



def constant_tables():
    import numpy as np
    r = np.arange(L)
    eye = (r[:, None] == r[None, :])
    low = (r[:, None] > r[None, :])
    masks = [eye, low]
    for m in (1,) + LEVELS:
        masks.append((r[:, None] // (2 * m) == r[None, :] // (2 * m)) & (r[:, None] // m > r[None, :] // m))
    masks = masks + [eye] * (8 - len(masks))
    tri = np.stack(masks, 1).astype(np.float32)
    return np.ascontiguousarray(np.tile(tri, (B, 1, 1)))



def transform_tables():
    import numpy as np
    n = np.arange(D)
    turn = 2 * np.pi * (np.outer(n, n) % D) / D
    p = np.arange(P)
    return {
        "eye": np.eye(P, dtype=np.float32),
        "quad": (p[:, None] // L == np.arange(4)).astype(np.float32),
        "last": (p[:, None] % L == L - 1).astype(np.float32),
        "cos": np.cos(turn).astype(np.float32),
        "sin": np.sin(turn).astype(np.float32),
        "msin": (-np.sin(turn)).astype(np.float32),
    }


def kernel(x, ctx_1024, L0_attn_omega, L0_attn_Win, L0_attn_Wl, L0_attn_bl, L0_attn_Wv, L0_attn_bv, L0_attn_Wout,
           L0_ffn_w_freq_real, L0_ffn_w_freq_imag, L0_ffn_bias):
    import numpy as np
    import concourse.bacc as bacc
    from concourse.bass_utils import run_bass_kernel_spmd

    def cols(v):
        return np.asarray(v).reshape(CT, P).T

    x = np.asarray(x)
    arrays = {
        "x_tok": x.reshape(B * T, D),
        "x_t": x.transpose(2, 0, 1).reshape(KD, P, B, T),
        "win": np.asarray(L0_attn_Win),
        "win_t": np.asarray(L0_attn_Win).T,
        "wlv_t": np.stack([np.asarray(L0_attn_Wl).T, np.asarray(L0_attn_Wv).T]),
        "bias": np.stack([cols(L0_attn_bl), cols(L0_attn_bv), cols(L0_attn_omega)], 1),
        "wout_t": np.asarray(L0_attn_Wout).T,
        "ctx": np.asarray(ctx_1024),
        "ctx_t": np.asarray(ctx_1024).transpose(2, 0, 1).reshape(KD, P, B, SR),
        "w_re": np.asarray(L0_ffn_w_freq_real),
        "w_im": np.asarray(L0_ffn_w_freq_imag),
        "ffn_bias": np.asarray(L0_ffn_bias),
        "tri": constant_tables(),
        **transform_tables(),
    }
    nc = bacc.Bacc("TRN2", target_bir_lowering=False, num_devices=1)
    ins, dram = {}, {}
    for name, a in arrays.items():
        a = np.ascontiguousarray(a)
        ins["in_" + name] = a
        dram[name] = nc.dram_tensor("in_" + name, a.shape, mybir.dt.from_np(a.dtype), kind="ExternalInput").ap()
    dram["out"] = nc.dram_tensor("out_y", (B * T, D), F32, kind="ExternalOutput").ap()
    build_program(nc, dram)
    r = run_bass_kernel_spmd(nc, [ins], core_ids=[0])
    return r.results[0]["out_y"].reshape(B, T, D)
```

```python
import math
from contextlib import ExitStack

import concourse.bass as bass
from concourse import mybir

ALU = mybir.AluOpType
ACT = mybir.ActivationFunctionType
AX = mybir.AxisListType
F32 = mybir.dt.float32
BF16 = mybir.dt.bfloat16
I32 = mybir.dt.int32

P = 128
B, T, D = 4, 1024, 256
DI = 512
KD = D // P
CT = DI // P
L = 32
NCH = 4
GT = L * NCH
NG = T // GT
CB = CT * B
SEG = NCH * CB
NTOK = B * GT
L1 = L + 1
LEVELS = (2, 4, 8, 16)
SAFE = math.exp(40.0)
TSTART = 10
TOPS = TSTART + 3 * (len(LEVELS) - 1) + 2 + B


def recurrence_block(nc, dram, HG, cst):
    with ExitStack() as ctx:
        def sb(name, shape, dt=F32):
            return ctx.enter_context(nc.sbuf_tensor(name, shape, dt))

        def sem(name):
            return ctx.enter_context(nc.semaphore(name))

        bank = [ctx.enter_context(nc.psum_tensor(f"bank{i}", [P, 512], F32)) for i in range(8)]
        PJ = bank[0:4]
        GR, TI, CQ, CP = bank[4:8]

        win_t = sb("win_t", [P, KD, 2 * DI])
        wc = sb("wc", [P, 2, KD, DI])
        bias = cst["bias"]
        tri = cst["tri"]
        xT = sb("xT", [P, 2, KD, B, GT])
        lam = [sb(f"lam{i}", [P, SEG, L1]) for i in range(2)]
        S = sb("S", [P, SEG, L1])
        V = [sb(f"V{i}", [P, SEG, L]) for i in range(2)]
        X = [sb(f"X{i}", [P, SEG, L]) for i in range(2)]
        U = [sb(f"U{i}", [P, SEG, L]) for i in range(2)]
        KB = sb("KB", [P, SEG, 2, L])
        keep = sb("keep", [P, CB, L1])
        sz = sb("sz", [P, 2, NTOK])
        E = sb("E", [P, CB, L1])
        H = [sb(f"H{i}", [P, CB, L1]) for i in range(NCH)]
        gm = sb("gm", [P, NCH, 2, L])
        vc = sb("vc", [P, NCH, 2])
        negc = [sb(f"negc{i}", [P, NCH]) for i in range(2)]
        w = [sb(f"w{i}", [P, NCH]) for i in range(2)]
        N = sb("N", [P, NCH, L])
        Tm = sb("Tm", [P, NCH, L])
        St = sb("St", [P, NCH, L])
        Ym = sb("Ym", [P, NCH, L])
        Sd = [sb(f"Sd{i}", [P, NCH, B, L]) for i in range(2)]
        qs = sb("qs", [P, 1])
        idle = sb("idle", [P, L], BF16)
        rng = sb("rng", [P, NG])
        sp = sb("sp", [P, 8, CT])
        slope = cst["slope"]
        HGf = HG[:, :, :, :].rearrange("p c b t -> p (c b t)")
        wlv = HGf[:, 0:2 * CT * DI].rearrange("p (w i j) -> p w i j", w=2, i=CT)
        win_x = HGf[:, 2 * CT * DI:2 * CT * DI + CT * D].rearrange("p (i d) -> p i d", i=CT)

        ld = {k: sem("ld_" + k) for k in ("in", "w", "small", "x0", "x1")}
        s_const, s_wc, s_wce, s_slope = sem("s_const"), sem("s_wc"), sem("s_wce"), sem("s_slope")
        pe = {k: sem("pe_" + k) for k in "lzvx"}
        ev = {k: sem("ev_" + k) for k in "lvxz"}
        act_sz = sem("act_sz")
        s_fix = sem("s_fix")
        s_scan, s_gex, s_lam, s_ginv = sem("s_scan"), sem("s_gex"), sem("s_lam"), sem("s_ginv")
        s_u, s_kb, s_nb, s_a, s_rng = sem("s_u"), sem("s_kb"), sem("s_nb"), sem("s_a"), sem("s_rng")
        pe_gram, s_t, pe_y, act_y, pe_t = sem("pe_gram"), sem("s_t"), sem("pe_y"), sem("act_y"), sem("pe_t")
        pe_q, s_qs, pe_p, s_e, s_h, s_g = sem("pe_q"), sem("s_qs"), sem("pe_p"), sem("s_e"), sem("s_h"), sem("s_g")
        s_flag = sem("s_flag")

        def seg(t, n, c):
            return t[:, :, :].rearrange("p (n c b) l -> p c b n l", n=NCH, c=CT)[:, c]

        block = ctx.enter_context(nc.Block())

        @block.sync
        def _(sp_):
            def load_x(g, par):
                for k in range(KD):
                    sp_.dma_start(xT[:, par, k], dram["x_t"][k][:, :, bass.ds(g * GT, GT)]).then_inc(ld[f"x{par}"], 16)

            sp_.dma_start(win_t[:, :, :], dram["win_t"].rearrange("(k p) n -> p k n", p=P)).then_inc(ld["in"], 16)
            load_x(0, 0)
            sp_.dma_start(win_x, dram["win"][0:DI, :].rearrange("(i p) d -> p i d", p=P)).then_inc(ld["w"], 16)
            sp_.dma_start(wlv, dram["wlv_t"].rearrange("w (i p) j -> p w i j", p=P)).then_inc(ld["w"], 16)
            sp_.dma_start(bias[:, :, :], dram["bias"]).then_inc(ld["small"], 16)
            for k in ("tri", "eye", "quad", "last"):
                sp_.dma_start(cst[k][:], dram[k]).then_inc(ld["small"], 16)

            load_x(1, 1)
            with sp_.Fori(1, NG // 2) as pair:
                for par in range(2):
                    sp_.wait_ge(pe["x"], (pair * 2 + (par - 1)) * CT)
                    load_x(pair * 2 + par, par)

        def group_loop(eng, body):
            body(-1, 1, False, True, True)
            with eng.Fori(0, NG // 2 - 1) as pair:
                body(pair * 2, 0, True, True, True)
                body(pair * 2 + 1, 1, True, True, True)
            body(NG - 2, 0, True, True, False)
            body(NG - 1, 1, True, False, False)

        @block.tensor
        def _(te):
            def multiply(kind, par, c, k):
                if kind in "lv":
                    lhs = wc[:, 0 if kind == "l" else 1, k, c * P:(c + 1) * P]
                else:
                    o = DI * (kind == "z") + c * P
                    lhs = win_t[:, k, o:o + P]
                return te.matmul(PJ[c][:, :], lhs, xT[:, par, k, :, :], start=(k == 0), stop=(k == KD - 1))

            def project(kind, G, par, c, halves=(0, 1)):
                if halves == (1,):
                    multiply(kind, par, c, 1).then_inc(pe[kind], 1)
                    return
                before = {"l": ("z", 0), "v": ("l", 0), "x": ("v", 0), "z": ("x", 1)}[kind]
                if not (kind == "z" and isinstance(G, int) and G == 0):
                    te.wait_ge(ev[before[0]], CT * (G - before[1]) + c + 1)
                if kind == "z" and c == 0:
                    te.wait_ge(ld[f"x{par}"], (G - par + 2) * (8 * KD))
                multiply(kind, par, c, 0)
                if halves == (0, 1):
                    multiply(kind, par, c, 1).then_inc(pe[kind], 1)

            def gram(G, par):
                te.wait_ge(s_kb, 2 * (G + 1))
                te.wait_ge(s_u, G + 1)
                for n in range(NCH):
                    for c in range(CT):
                        for b in range(B):
                            s = (n * CT + c) * B + b
                            last = te.matmul(GR[L * b:L * b + L, 2 * L * n:2 * L * (n + 1)], U[par][:, s, :],
                                             KB[:, s, :, :], start=(c == 0), stop=(c == CT - 1))
                last.then_inc(pe_gram, 1)

            def carry():
                te.matmul(TI[0:L, 2 * P:2 * P + 1], idle[:, 0:L], idle[:, 0:1], start=True, stop=True)

            def level_y(G, lv):
                te.wait_ge(s_t, TOPS * G + TSTART + 3 * lv)
                carry()
                for n in range(NCH):
                    for b in range(B):
                        q = slice(L * b, L * b + L)
                        last = te.matmul(TI[q, L * n:L * n + L], N[q, n, :], St[q, n, :], start=True, stop=True)
                last.then_inc(pe_y, 1)

            def level_t(G, lv):
                te.wait_ge(act_y, len(LEVELS) * G + lv + 1)
                carry()
                for n in range(NCH):
                    for b in range(B):
                        q = slice(L * b, L * b + L)
                        last = te.matmul(TI[q, P + L * n:P + L * n + L], Ym[q, n, :], Tm[q, n, :], start=True, stop=True)
                last.then_inc(pe_t, 1)

            def chain_q(g, par, n):
                te.wait_ge(s_h, NCH * g + n + 1)
                h0 = H[n - 1]
                for c in range(CT):
                    for b in range(B):
                        last = te.matmul(CQ[L * b:L * b + L, 0:1], U[par][:, (n * CT + c) * B + b, :],
                                         h0[:, c * B + b, L:L1], start=(c == 0), stop=(c == CT - 1))
                last.then_inc(pe_q, 1)

            def chain_p(g, par, n):
                te.wait_ge(s_qs, NCH * g + n + 1)
                te.matmul(CP[:, 0:P], qs[:, 0:1].broadcast_to([P, P]), Sd[par][:, n, :, :],
                          start=True, stop=True).then_inc(pe_p, 1)

            te.wait_ge(ld["in"], 16)
            for c in range(CT):
                project("z", 0, 0, c)
            te.wait_ge(ld["w"], 32)
            for j in range(2):
                for m in range(KD):
                    for i in range(CT):
                        last = te.matmul(bank[4 + 2 * j + m][:, :], win_x[:, i, m * P:(m + 1) * P], wlv[:, j, i, :],
                                         start=(i == 0), stop=(i == CT - 1))
                    last.then_inc(s_wc, 1)
            te.wait_ge(s_wce, 4)
            te.wait_ge(s_const, 9)
            for c in range(CT):
                project("l", 0, 0, c)

            def body(g, par, chain, do_vx, do_zl):
                nxt = 1 - par
                if chain:
                    chain_q(g, par, 0)
                if do_vx:
                    project("v", g + 1, nxt, 0)
                if chain:
                    chain_p(g, par, 0)
                if do_vx:
                    for c in range(1, CT):
                        project("v", g + 1, nxt, c)
                if chain:
                    chain_q(g, par, 1)
                if do_vx:
                    project("x", g + 1, nxt, 0)
                if chain:
                    chain_p(g, par, 1)
                if do_vx:
                    for c in range(1, CT):
                        project("x", g + 1, nxt, c)
                if chain:
                    chain_q(g, par, 2)
                if do_zl:
                    project("z", g + 2, par, 0)
                if chain:
                    chain_p(g, par, 2)
                if do_zl:
                    project("z", g + 2, par, 1)
                    project("z", g + 2, par, 2)
                if do_vx:
                    gram(g + 1, nxt)
                if chain:
                    chain_q(g, par, 3)
                if do_zl:
                    project("z", g + 2, par, 3)
                if chain:
                    chain_p(g, par, 3)
                for lv in range(len(LEVELS)):
                    if do_zl:
                        project("l", g + 2, par, lv, (0,))
                    if do_vx:
                        level_y(g + 1, lv)
                    if do_zl:
                        project("l", g + 2, par, lv, (1,))
                    if do_vx:
                        level_t(g + 1, lv)

            group_loop(te, body)
            te.wait_ge(s_flag, 2)
            te.matmul(CQ[0:1, 1:2], rng[:, 1:2], keep[:, 0, 1:2], start=True, stop=True).then_inc(s_flag, 1)

        @block.scalar
        def _(act):
            act.wait_ge(s_slope, 2)
            act.activation(sp[:, 1], sp[:, 0], ACT.Exp, scale=-1.0).then_inc(s_slope, 1)
            act.wait_ge(s_slope, 4)
            act.activation(sp[:, 3], sp[:, 2], ACT.Ln).then_inc(s_slope, 1)
            def bank_view(c):
                return PJ[c][:, :].rearrange("p (b n l) -> p b n l", b=B, n=NCH)

            def evac_z(G, c):
                act.wait_ge(pe["z"], CT * G + c + 1)
                if not (isinstance(G, int) and G == 0 and c < 2):
                    act.wait_ge(ev["z"], CT * G + c - 1)
                act.activation(sz[:, c % 2, :], PJ[c][:, :], ACT.Sigmoid).then_inc(act_sz, 1)

            def evac_l(G, par, c):
                act.wait_ge(pe["l"], CT * G + c + 1)
                act.activation(seg(lam[par], 0, c)[:, :, :, 1:L1], bank_view(c), ACT.Sigmoid,
                               bias=bias[:, 0, c:c + 1]).then_inc(ev["l"], 1)

            def evac_y(G, lv):
                act.wait_ge(pe_y, len(LEVELS) * G + lv + 1)
                act.activation(Ym[:, :, :].rearrange("p n l -> p (n l)"), TI[:, 0:P], ACT.Copy).then_inc(act_y, 1)

            for c in range(CT):
                evac_z(0, c)
            for i in range(4):
                act.wait_ge(s_wc, i + 1)
                act.activation(wc[:, i // 2, i % 2, :], bank[4 + i][:, :], ACT.Copy).then_inc(s_wce, 1)
            act.wait_ge(ld["small"], 80)
            act.wait_ge(s_const, 9)
            for c in range(CT):
                evac_l(0, 0, c)

            def body(g, par, chain, do_vx, do_zl):
                nxt = 1 - par
                G = g + 1
                if do_vx:
                    if chain:
                        act.wait_ge(s_h, NCH * g + 1)
                    act.wait_ge(s_scan, NCH * (G + 1))
                    for c in range(CT):
                        act.activation(seg(U[nxt], 0, c), seg(S, 0, c)[:, :, :, 0:L], ACT.Exp,
                                       scale=slope[:, 0, c:c + 1]).then_inc(s_gex, 1)
                    for c in range(CT):
                        act.wait_ge(pe["v"], CT * G + c + 1)
                        act.activation(seg(V[nxt], 0, c), bank_view(c), ACT.Identity,
                                       bias=bias[:, 1, c:c + 1]).then_inc(ev["v"], 1)
                    act.wait_ge(s_gex, CT * (G + 1))
                    for c in range(CT):
                        sc = seg(S, 0, c)
                        act.activation(sc, sc, ACT.Exp, scale=slope[:, 1, c:c + 1]).then_inc(s_ginv, 1)
                    for c in range(CT):
                        lc = seg(lam[nxt], 0, c)[:, :, :, 1:L1]
                        act.activation(lc, lc, ACT.Exp, scale=slope[:, 0, c:c + 1]).then_inc(s_lam, 1)
                    for c in range(CT):
                        act.wait_ge(pe["x"], CT * G + c + 1)
                        act.activation(seg(X[nxt], 0, c), bank_view(c), ACT.Copy).then_inc(ev["x"], 1)
                if do_zl:
                    for c in range(CT):
                        evac_z(g + 2, c)
                for lv in range(len(LEVELS)):
                    if do_vx:
                        evac_y(G, lv)
                    if do_zl:
                        if chain and lv == 0:
                            act.wait_ge(s_h, NCH * (g + 1) + 1)
                        evac_l(g + 2, par, lv)

            group_loop(act, body)

        @block.vector
        def _(dve):
            consts = [(lam[0], 0.0), (lam[1], 0.0), (S, 0.0), (keep, 1.0), (E, 0.0), (Sd[0], 0.0), (Sd[1], 0.0), (idle, 0.0)]
            for i, (t, val) in enumerate(consts):
                dve.memset(t[:], val).then_inc(s_const, 1)
            dve.wait_ge(s_const, len(consts))
            dve.memset(keep[:, :, 0:1], 0.0).then_inc(s_const, 1)
            dve.wait_ge(s_const, 9)

            dve.wait_ge(ld["small"], 80)
            om = bias[:, 2, :]
            dve.tensor_scalar(sp[:, 4], om, -1.0, None, ALU.mult).then_inc(s_slope, 1)
            dve.wait_ge(s_slope, 1)
            dve.tensor_tensor(sp[:, 0], om, sp[:, 4], ALU.max).then_inc(s_slope, 1)
            dve.wait_ge(s_slope, 3)
            dve.tensor_scalar(sp[:, 2], sp[:, 1], 1.0, None, ALU.add).then_inc(s_slope, 1)
            dve.wait_ge(s_slope, 5)
            steps = [
                lambda: dve.tensor_scalar(sp[:, 4], sp[:, 2], 1.0, None, ALU.subtract),
                lambda: dve.tensor_scalar(sp[:, 5], sp[:, 4], 0.0, None, ALU.is_equal),
                lambda: dve.tensor_tensor(sp[:, 4], sp[:, 4], sp[:, 5], ALU.add),
                lambda: dve.reciprocal(sp[:, 6], sp[:, 4]),
                lambda: dve.tensor_tensor(sp[:, 3], sp[:, 3], sp[:, 6], ALU.mult),
                lambda: dve.tensor_tensor(sp[:, 3], sp[:, 3], sp[:, 5], ALU.add),
                lambda: dve.tensor_tensor(sp[:, 3], sp[:, 3], sp[:, 1], ALU.mult),
                lambda: dve.scalar_tensor_tensor(sp[:, 7], om, 0.0, sp[:, 3], ALU.max, ALU.add),
                lambda: dve.tensor_scalar(slope[:, 0], sp[:, 7], -8.0, None, ALU.mult),
                lambda: dve.tensor_scalar(slope[:, 1], sp[:, 7], 8.0, None, ALU.mult),
            ]
            for i, f in enumerate(steps):
                f().then_inc(s_slope, 1)
                dve.wait_ge(s_slope, 6 + i)

            def mul_z(G, c):
                dve.wait_ge(act_sz, CT * G + c + 1)
                out = HG[:, c, :, bass.ds(G * GT, GT)]
                dve.tensor_tensor(out, PJ[c][:, :].rearrange("p (b t) -> p b t", b=B),
                                  sz[:, c % 2, :].rearrange("p (b t) -> p b t", b=B), ALU.mult).then_inc(ev["z"], 1)

            def flat(t, n):
                return t[:, n * CB:(n + 1) * CB, :].rearrange("p s l -> p (s l)")

            def prefix(G, par):
                dve.wait_ge(ev["l"], CT * (G + 1))
                if isinstance(G, int) and G == 0:
                    dve.memset(lam[par][:, 0:CB, 1:2], 0.0).then_inc(s_fix, 1)
                    dve.wait_ge(s_fix, 1)
                else:
                    dve.wait_ge(s_ginv, CT * G)
                for n in range(NCH):
                    dve.tensor_tensor_scan(flat(S, n), keep[:, :, :].rearrange("p s l -> p (s l)"), flat(lam[par], n),
                                           0.0, ALU.mult, ALU.add).then_inc(s_scan, 1)

            def make_u(G, par):
                dve.wait_ge(ev["v"], CT * (G + 1))
                if isinstance(G, int) and G == 0:
                    dve.memset(V[par][:, 0:CB, 0:1], 0.0).then_inc(s_fix, 1)
                    dve.wait_ge(s_fix, 2)
                dve.wait_ge(s_gex, CT * (G + 1))
                dve.tensor_tensor(U[par][:, :, :], U[par][:, :, :], V[par][:, :, :], ALU.mult).then_inc(s_u, 1)

            def make_k(G, par):
                dve.wait_ge(s_ginv, CT * (G + 1))
                if not (isinstance(G, int) and G == 0):
                    dve.wait_ge(pe_gram, G)
                dve.tensor_tensor(KB[:, :, 0, :], V[par][:, :, :], S[:, :, 0:L], ALU.mult).then_inc(s_kb, 1)
                dve.tensor_reduce(rng[:, bass.ds(G, 1)], S[:, :, L], AX.X, ALU.max).then_inc(s_rng, 1)

            def make_a(G, par):
                dve.wait_ge(s_lam, CT * (G + 1))
                dve.wait_ge(s_kb, 2 * G + 1)
                dve.tensor_tensor(V[par][:, :, :], V[par][:, :, :], lam[par][:, :, 1:L1], ALU.mult).then_inc(s_a, 1)

            def make_b(G, par):
                dve.wait_ge(ev["x"], CT * (G + 1))
                if isinstance(G, int) and G == 0:
                    dve.tensor_copy(H[NCH - 1][:, :, L], X[0][:, 0:CB, 0]).then_inc(s_h, 1)
                    dve.wait_ge(s_h, 1)
                dve.wait_ge(s_lam, CT * (G + 1))
                dve.scalar_tensor_tensor(X[par][:, :, :], lam[par][:, :, 1:L1], 1.0, X[par][:, :, :],
                                         ALU.subtract, ALU.mult).then_inc(s_nb, 1)

            def make_kb(G, par):
                dve.wait_ge(s_nb, G + 1)
                dve.tensor_tensor(KB[:, :, 1, :], X[par][:, :, :], S[:, :, 1:L1], ALU.mult).then_inc(s_kb, 1)

            def mask(k):
                return tri[:, k, :].unsqueeze(1).broadcast_to([P, NCH, L])

            def t_start(G, par):
                base = TOPS * G
                dve.wait_ge(pe_gram, G + 1)
                A = GR[:, 0:2 * L * NCH].rearrange("p (n two l) -> p n two l", n=NCH, two=2)
                both = tri[:, 0:2, :].unsqueeze(1).broadcast_to([P, NCH, 2, L])
                dve.tensor_tensor(gm[:, :, :, :], A, both, ALU.mult).then_inc(s_t, 1)
                dve.wait_ge(s_t, base + 1)
                dve.tensor_reduce(vc[:, :, :], gm[:, :, :, :], AX.X, ALU.add).then_inc(s_t, 1)
                dve.wait_ge(s_t, base + 2)
                if isinstance(G, int) and G == 0:
                    for b in range(B):
                        dve.memset(vc[L * b:L * b + 1, 0, 0:1], 1.0).then_inc(s_fix, 1)
                    dve.wait_ge(s_fix, 2 + B)
                dve.reciprocal(w[par][:, :], vc[:, :, 0]).then_inc(s_t, 1)
                dve.wait_ge(s_t, base + 3)
                dve.tensor_scalar(w[par][:, :], w[par][:, :], -2.0, None, ALU.mult).then_inc(s_t, 1)
                dve.tensor_copy(negc[par][:, :], vc[:, :, 1]).then_inc(s_t, 1)
                dve.tensor_tensor(N[:, :, :], A[:, :, 0, :], mask(1), ALU.mult).then_inc(s_t, 1)
                dve.wait_ge(s_t, base + 6)
                dve.tensor_tensor(N[:, :, :], N[:, :, :], w[par][:, :].unsqueeze(2).broadcast_to([P, NCH, L]),
                                  ALU.mult).then_inc(s_t, 1)
                dve.wait_ge(s_t, base + 7)
                dve.tensor_tensor(Tm[:, :, :], N[:, :, :], mask(2), ALU.mult).then_inc(s_t, 1)
                dve.wait_ge(s_t, base + 8)
                dve.tensor_tensor(Tm[:, :, :], Tm[:, :, :], mask(0), ALU.add).then_inc(s_t, 1)
                dve.wait_ge(s_t, base + 9)
                dve.transpose(St[:, :, :], Tm[:, :, :]).then_inc(s_t, 1)
                dve.wait_ge(s_t, base + 10)

            def level(G, par, lv):
                base = TOPS * G + TSTART + 3 * lv
                dve.wait_ge(pe_t, len(LEVELS) * G + lv + 1)
                R = TI[:, P:2 * P].rearrange("p (n l) -> p n l", n=NCH)
                dve.tensor_tensor(gm[:, :, 0, :], R, mask(3 + lv), ALU.mult).then_inc(s_t, 1)
                dve.wait_ge(s_t, base + 1)
                dve.tensor_tensor(Tm[:, :, :], Tm[:, :, :], gm[:, :, 0, :], ALU.add).then_inc(s_t, 1)
                dve.wait_ge(s_t, base + 2)
                if lv < len(LEVELS) - 1:
                    dve.transpose(St[:, :, :], Tm[:, :, :]).then_inc(s_t, 1)
                    dve.wait_ge(s_t, base + 3)
                else:
                    for b in range(B):
                        q = slice(L * b, L * b + L)
                        dve.transpose(Sd[par][q, :, b, :], Tm[q, :, :]).then_inc(s_t, 1)
                    dve.wait_ge(s_t, base + 2 + B)

            def chain_start(g, par, n):
                q = NCH * g + n
                h0 = H[n - 1]
                dve.wait_ge(s_h, q + 1)
                dve.tensor_copy(E[:, :, 0:1], h0[:, :, L:L1]).then_inc(s_e, 1)
                dve.wait_ge(pe_q, q + 1)
                dve.tensor_scalar(qs[:, 0:1], CQ[:, 0:1], negc[par][:, n:n + 1], w[par][:, n:n + 1],
                                  ALU.subtract, ALU.mult).then_inc(s_qs, 1)

            def chain_end(g, par, n):
                q = NCH * g + n
                h1 = H[n]
                s0 = n * CB
                dve.wait_ge(pe_p, q + 1)
                p_all = CP[:, 0:P].rearrange("p (b l) -> p b l", b=B).unsqueeze(1).broadcast_to([P, CT, B, L])
                dve.tensor_tensor(E[:, :, 1:L1].rearrange("p (c b) l -> p c b l", c=CT),
                                  V[par][:, s0:s0 + CB, :].rearrange("p (c b) l -> p c b l", c=CT), p_all,
                                  ALU.mult).then_inc(s_e, 1)
                dve.wait_ge(s_e, 3 * q + 2)
                dve.tensor_tensor(E[:, :, 1:L1], E[:, :, 1:L1], X[par][:, s0:s0 + CB, :], ALU.subtract).then_inc(s_e, 1)
                dve.wait_ge(s_e, 3 * q + 3)
                dve.tensor_tensor_scan(h1[:, :, :].rearrange("p s l -> p (s l)"), flat(lam[par], n),
                                       E[:, :, :].rearrange("p s l -> p (s l)"), 0.0, ALU.mult, ALU.add).then_inc(s_h, 1)

            def gate(g, n):
                q = NCH * g + n
                dve.wait_ge(s_h, q + 2)
                h1 = H[n]
                t0 = L * n
                hg = HG[:, :, :, bass.ds(g * GT + t0, L)].rearrange("p c b t -> p (c b) t")
                dve.tensor_tensor(hg, hg, h1[:, :, 1:L1], ALU.mult).then_inc(s_g, 1)

            dve.wait_ge(s_wc, 4)
            for c in range(CT):
                mul_z(0, c)

            def body(g, par, do_chain, do_vx, do_zl):
                nxt = 1 - par
                if do_chain:
                    chain_start(g, par, 0)
                if do_vx:
                    prefix(g + 1, nxt)
                if do_chain:
                    chain_end(g, par, 0)
                    chain_start(g, par, 1)
                if do_vx:
                    make_u(g + 1, nxt)
                if do_chain:
                    chain_end(g, par, 1)
                if do_vx:
                    make_k(g + 1, nxt)
                if do_chain:
                    chain_start(g, par, 2)
                if do_vx:
                    make_b(g + 1, nxt)
                if do_chain:
                    chain_end(g, par, 2)
                if do_vx:
                    make_kb(g + 1, nxt)
                if do_zl:
                    mul_z(g + 2, 0)
                    mul_z(g + 2, 1)
                if do_vx:
                    make_a(g + 1, nxt)
                if do_chain:
                    chain_start(g, par, 3)
                if do_vx:
                    t_start(g + 1, nxt)
                if do_chain:
                    chain_end(g, par, 3)
                if do_zl:
                    mul_z(g + 2, 2)
                    mul_z(g + 2, 3)
                for lv in range(len(LEVELS)):
                    if do_vx:
                        level(g + 1, nxt, lv)
                    if do_chain:
                        gate(g, lv)
                if do_chain:
                    dve.wait_ge(s_g, NCH * (g + 1))

            group_loop(dve, body)
            dve.wait_ge(s_rng, NG)
            dve.tensor_reduce(rng[:, 0:1], rng[:, :], AX.X, ALU.max).then_inc(s_flag, 1)
            dve.wait_ge(s_flag, 1)
            dve.tensor_scalar(rng[:, 1:2], rng[:, 0:1], SAFE, 0.0, ALU.is_le, ALU.is_equal).then_inc(s_flag, 1)
            dve.wait_ge(s_flag, 3)
            dve.tensor_scalar(cst["flag"][:, :], CQ[0:1, 1:2], 1.0, None, ALU.min).then_inc(s_flag, 1)


def general_recurrence_block(nc, dram, HG, cst):
    with ExitStack() as ctx:
        def sb(name, shape, dt=F32):
            return ctx.enter_context(nc.sbuf_tensor(name, shape, dt))

        def sem(name):
            return ctx.enter_context(nc.semaphore(name))

        bank = [ctx.enter_context(nc.psum_tensor(f"g_bank{i}", [P, 512], F32)) for i in range(8)]
        PJ, PC, SUM = bank[0:4], bank[4:6], bank[6]
        win_t = sb("g_win_t", [P, KD, 2 * DI])
        win_x = sb("g_win_x", [P, CT, D])
        wlv = sb("g_wlv", [P, 2, CT, DI])
        wc = sb("g_wc", [P, 2, KD, DI])
        xg = sb("g_x", [P, KD, B, GT])
        lam = sb("g_lam", [P, CB, GT])
        v = sb("g_v", [P, CB, GT])
        xi = sb("g_xi", [P, CB, GT])
        ones = sb("g_ones", [P, P])
        h = sb("g_h", [P, CB])
        pr = sb("g_pr", [P, 2, CB])
        sm = sb("g_sm", [P, 2, B])
        co = sb("g_co", [P, B])
        u = sb("g_u", [P, CB])
        s = {k: sem("g_" + k) for k in ("w", "x", "wc", "wce", "init", "pj", "sig", "ev", "lam", "evz", "fix", "nb",
                                        "pr", "sum", "step", "done")}
        SOPS = 8
        block = ctx.enter_context(nc.Block())

        def when_flagged(eng, program):
            value = eng.value_load(cst["flag"][0:1, 0:1], min_val=0, max_val=1)
            with eng.If(value):
                program()

        def groups(eng, body):
            body(0, True)
            with eng.Fori(1, NG) as g:
                body(g, False)

        @block.sync
        def _(sp):
            def program():
                sp.dma_start(wlv[:], dram["wlv_t"].rearrange("w (i p) j -> p w i j", p=P)).then_inc(s["w"], 16)
                sp.dma_start(win_x[:], dram["win"][0:DI, :].rearrange("(i p) d -> p i d", p=P)).then_inc(s["w"], 16)
                sp.dma_start(win_t[:], dram["win_t"].rearrange("(k p) n -> p k n", p=P)).then_inc(s["w"], 16)

                def body(g, first):
                    if not first:
                        sp.wait_ge(s["pj"], 4 * CT * g)
                    for k in range(KD):
                        src = dram["x_t"][k][:, :, bass.ds(g * GT, GT)]
                        sp.dma_start(xg[:, k], src).then_inc(s["x"], 16)
                groups(sp, body)
            when_flagged(sp, program)

        @block.tensor
        def _(te):
            def program():
                te.wait_ge(s["w"], 48)
                for j in range(2):
                    for m in range(KD):
                        for i in range(CT):
                            last = te.matmul(PJ[2 * j + m][:, :], win_x[:, i, m * P:(m + 1) * P], wlv[:, j, i, :],
                                             start=(i == 0), stop=(i == CT - 1))
                        last.then_inc(s["wc"], 1)
                te.wait_ge(s["wce"], 4)
                te.wait_ge(s["init"], 2)

                def body(g, first):
                    te.wait_ge(s["x"], (g + 1) * (16 * KD))
                    if not first:
                        te.wait_ge(s["done"], g)
                    for n in range(4 * CT):
                        kind, c = n // CT, n % CT
                        if kind == 1:
                            te.wait_ge(s["ev"], g * (3 * CT) + (c + 1))
                        if kind == 2:
                            te.wait_ge(s["evz"], g * CT + (c + 1))
                        if kind == 3:
                            te.wait_ge(s["ev"], g * (3 * CT) + (CT + c + 1))
                        for k in range(KD):
                            if kind in (0, 2):
                                lhs = wc[:, kind // 2, k, c * P:(c + 1) * P]
                            else:
                                o = DI * (kind == 1) + c * P
                                lhs = win_t[:, k, o:o + P]
                            last = te.matmul(PJ[n % 4][:, :], lhs, xg[:, k, :, :], start=(k == 0), stop=(k == KD - 1))
                        last.then_inc(s["pj"], 1)
                    with te.Fori(0, GT) as t:
                        te.wait_ge(s["pr"], (g * GT + t) * 2 + 2)
                        te.matmul(SUM[:, 0:2 * CB], ones[:, :], pr[:, :, :], start=True, stop=True).then_inc(s["sum"], 1)
                groups(te, body)
            when_flagged(te, program)

        @block.scalar
        def _(act):
            def program():
                for i in range(4):
                    act.wait_ge(s["wc"], i + 1)
                    act.activation(wc[:, i // 2, i % 2, :], PJ[i][:, :], ACT.Copy).then_inc(s["wce"], 1)

                def body(g, first):
                    for n in range(4 * CT):
                        kind, c = n // CT, n % CT
                        act.wait_ge(s["pj"], g * (4 * CT) + (n + 1))
                        flat = PJ[n % 4][:, :].rearrange("p (b t) -> p b t", b=B)
                        own = slice(c * B, c * B + B)
                        if kind == 0:
                            act.activation(lam[:, own, :], flat, ACT.Sigmoid, bias=cst["bias"][:, 0, c:c + 1]).then_inc(s["ev"], 1)
                        elif kind == 1:
                            act.activation(HG[:, c, :, bass.ds(g * GT, GT)], flat, ACT.Sigmoid).then_inc(s["sig"], 1)
                        elif kind == 2:
                            act.activation(v[:, own, :], flat, ACT.Identity, bias=cst["bias"][:, 1, c:c + 1]).then_inc(s["ev"], 1)
                        else:
                            act.activation(xi[:, own, :], flat, ACT.Copy).then_inc(s["ev"], 1)
                    for c in range(CT):
                        own = slice(c * B, c * B + B)
                        act.activation(lam[:, own, :], lam[:, own, :], ACT.Exp, scale=cst["slope"][:, 0, c:c + 1]).then_inc(s["lam"], 1)
                groups(act, body)
            when_flagged(act, program)

        @block.vector
        def _(dve):
            def program():
                dve.memset(ones[:, :], 1.0).then_inc(s["init"], 1)
                dve.memset(h[:, :], 0.0).then_inc(s["init"], 1)
                dve.wait_ge(s["init"], 2)

                def body(g, first):
                    for c in range(CT):
                        dve.wait_ge(s["sig"], g * CT + (c + 1))
                        hz = HG[:, c, :, bass.ds(g * GT, GT)]
                        dve.tensor_tensor(hz, hz, PJ[c][:, :].rearrange("p (b t) -> p b t", b=B), ALU.mult).then_inc(s["evz"], 1)
                    dve.wait_ge(s["evz"], (g + 1) * CT)
                    dve.wait_ge(s["ev"], (g + 1) * (3 * CT))
                    dve.wait_ge(s["lam"], (g + 1) * CT)
                    if first:
                        dve.memset(lam[:, :, 0:1], 0.0).then_inc(s["fix"], 1)
                        dve.memset(v[:, :, 0:1], 1.0).then_inc(s["fix"], 1)
                        dve.wait_ge(s["fix"], 2)
                    dve.scalar_tensor_tensor(xi[:, :, :], lam[:, :, :], 1.0, xi[:, :, :], ALU.subtract, ALU.mult).then_inc(s["nb"], 1)
                    with dve.Fori(0, GT) as t:
                        k = g * GT + t
                        at = bass.ds(t, 1)
                        vt = v[:, :, at].rearrange("p s o -> p (s o)")
                        lt = lam[:, :, at].rearrange("p s o -> p (s o)")
                        bt = xi[:, :, at].rearrange("p s o -> p (s o)")
                        dve.tensor_tensor(pr[:, 0, :], vt, h[:, :], ALU.mult).then_inc(s["pr"], 1)
                        dve.tensor_tensor(pr[:, 1, :], vt, vt, ALU.mult).then_inc(s["pr"], 1)
                        dve.wait_ge(s["sum"], k + 1)
                        dve.tensor_reduce(sm[:, :, :], SUM[:, 0:2 * CB].rearrange("p (two c b) -> p two b c", two=2, c=CT),
                                          AX.X, ALU.add).then_inc(s["step"], 1)
                        dve.wait_ge(s["step"], k * SOPS + 1)
                        dve.reciprocal(co[:, :], sm[:, 1, :]).then_inc(s["step"], 1)
                        dve.wait_ge(s["step"], k * SOPS + 2)
                        dve.scalar_tensor_tensor(co[:, :], co[:, :], -2.0, sm[:, 0, :], ALU.mult, ALU.mult).then_inc(s["step"], 1)
                        dve.wait_ge(s["step"], k * SOPS + 3)
                        dve.tensor_tensor(u[:, :].rearrange("p (c b) -> p c b", c=CT), vt.rearrange("p (c b) -> p c b", c=CT),
                                          co[:, :].unsqueeze(1).broadcast_to([P, CT, B]), ALU.mult).then_inc(s["step"], 1)
                        dve.wait_ge(s["step"], k * SOPS + 4)
                        dve.tensor_tensor(h[:, :], h[:, :], u[:, :], ALU.add).then_inc(s["step"], 1)
                        dve.wait_ge(s["step"], k * SOPS + 5)
                        dve.tensor_tensor(h[:, :], h[:, :], lt, ALU.mult).then_inc(s["step"], 1)
                        dve.wait_ge(s["step"], k * SOPS + 6)
                        dve.wait_ge(s["nb"], g + 1)
                        dve.tensor_tensor(h[:, :], h[:, :], bt, ALU.subtract).then_inc(s["step"], 1)
                        dve.wait_ge(s["step"], k * SOPS + 7)
                        hg = HG[:, :, :, bass.ds(k, 1)].rearrange("p c b o -> p (c b o)")
                        dve.tensor_tensor(hg, hg, h[:, :], ALU.mult).then_inc(s["step"], 1)
                        dve.wait_ge(s["step"], k * SOPS + SOPS)
                    dve.tensor_copy(co[:, :], sm[:, 0, :]).then_inc(s["done"], 1)
                    dve.wait_ge(s["done"], g + 1)
                groups(dve, body)
            when_flagged(dve, program)



NI = T // P
NT = B * NI
SR = 154
LANES = 32
CW = T // LANES
STEPS = SR + LANES - 1
PAD = LANES - 1
PITCH = SR + 2 * PAD
REC = CW + 1
DREC = REC + 1
CHUNK = 4
NCK = -(-STEPS // CHUNK)
BIG = 1e30
EPS = 1e-5


def view(t, off, *dims):
    return bass.AP(tensor=t.tensor, offset=t.offset + off, ap=[list(t.ap[0])] + [list(d) for d in dims])


def token_tile(t, i):
    return t[:, i % B, (i // B) * P:(i // B + 1) * P]


def project_and_distance_block(nc, dram, HG, X1, Zd, cst):
    with ExitStack() as ctx:
        def sb(name, shape, dt=F32):
            return ctx.enter_context(nc.sbuf_tensor(name, shape, dt))

        def sem(name):
            return ctx.enter_context(nc.semaphore(name))

        bank = [ctx.enter_context(nc.psum_tensor(f"b_bank{i}", [P, 512], F32)) for i in range(8)]
        PO, PT, PD, PA, PB = bank[0:2], bank[2:4], bank[4:6], bank[6], bank[7]
        wout = sb("wout", [P, CT, D])
        ctxT = sb("ctxT", [P, KD, B, SR])
        sq = sb("sq", [P, KD, B, SR])
        AA = sb("AA", [P, SR])
        x1T = sb("x1T", [P, KD, B, T])
        st = sb("st", [P, 2, 6])
        mv = sb("mv", [P, NT, 2])
        sd = sb("sd", [P, NT])
        rs = sb("rs", [P, NT])
        ssq = sb("ssq", [P, NT])
        junk = sb("junk", [P, 2, D])
        mb = sb("mb", [P, B, 4])
        bb = sb("bb", [P, LANES])
        ones = sb("ones", [P, L])

        ld_w, ld_c = sem("b_ld_w"), sem("b_ld_c")
        ld_x = [sem(f"b_ld_x{i}") for i in range(NI)]
        s_sq, s_one, pe_aa, s_aa = sem("b_sq"), sem("b_one"), sem("pe_aa"), sem("s_aa")
        pe_o, s_add, s_st, s_mv, s_sd, s_rs, s_x1 = (sem("b_" + k) for k in ("pe_o", "add", "st", "mv", "sd", "rs", "x1"))
        s_ssq, pe_tr, s_x1T, s_mb, pe_bb, s_bb = (sem("b_" + k) for k in ("ssq", "pe_tr", "x1T", "mb", "pe_bb", "bb"))
        pe_d, s_d2, s_cl, s_zd, s_pad = (sem("b_" + k) for k in ("pe_d", "d2", "cl", "zd", "pad"))
        block = ctx.enter_context(nc.Block())

        LAG_T, LAG_D, LAG_Z = 3, 7, 8

        @block.sync
        def _(sp):
            sp.dma_start(ctxT[:, :, :, :], dram["ctx_t"].rearrange("k p b s -> p k b s")).then_inc(ld_c, 16)
            sp.dma_start(wout[:, :, :], dram["wout_t"].rearrange("(c p) d -> p c d", p=P)).then_inc(ld_w, 16)
            xt = dram["x_tok"].rearrange("(b i p) d -> p i b d", b=B, p=P)
            for i in range(NI):
                sp.dma_start(X1[:, i * B:(i + 1) * B, :], xt[:, i]).then_inc(ld_x[i], 16)

        @block.tensor
        def _(te):
            def attention_out(i):
                if i == 0:
                    te.wait_ge(ld_w, 16)
                if i >= 2:
                    te.wait_ge(s_add, i - 1)
                for c in range(CT):
                    last = te.matmul(PO[i % 2][:, 0:D], token_tile(HG[:, c], i), wout[:, c, :],
                                     start=(c == 0), stop=(c == CT - 1))
                last.then_inc(pe_o, 1)

            def turn(i):
                te.wait_ge(s_x1, i + 1)
                if i >= 2:
                    te.wait_ge(s_x1T, i - 1)
                for k in range(KD):
                    last = te.transpose(PT[i % 2][:, k * P:(k + 1) * P], X1[:, i, k * P:(k + 1) * P], cst["eye"][:, :])
                last.then_inc(pe_tr, 1)

            def norms(t):
                te.wait_ge(s_mb, t + 1)
                for b in range(B):
                    last = te.matmul(PB[L * b:L * b + L, 4 * t:4 * t + 4], cst["tri"][:, 0, :], mb[:, b, :],
                                     start=True, stop=True)
                last.then_inc(pe_bb, 1)

            def distances(jb):
                if jb % B == 0:
                    te.wait_ge(s_x1T, jb + B)
                if jb >= 2:
                    te.wait_ge(s_d2, jb - 1)
                for k in range(KD):
                    for b in range(B):
                        last = te.matmul(PD[jb % 2][L * b:L * b + L, 0:SR],
                                         x1T[:, k, b, jb * CW:(jb + 1) * CW], ctxT[:, k, b, :],
                                         start=(k == 0), stop=(k == KD - 1))
                last.then_inc(pe_d, 1)

            te.wait_ge(s_one, 1)
            te.wait_ge(s_sq, 1)
            for k in range(KD):
                for b in range(B):
                    last = te.matmul(PA[L * b:L * b + L, 0:SR], ones[:, :], sq[:, k, b, :],
                                     start=(k == 0), stop=(k == KD - 1))
            last.then_inc(pe_aa, 1)
            te.wait_ge(s_sq, 2)
            for i in range(NT + LAG_D):
                if i < NT:
                    attention_out(i)
                if LAG_T <= i < NT + LAG_T:
                    turn(i - LAG_T)
                if i % B == 2 and B <= i < NT + B:
                    norms(i // B - 1)
                if i >= LAG_D:
                    distances(i - LAG_D)

        @block.scalar
        def _(act):
            act.wait_ge(s_pad, 3)
            act.wait_ge(pe_aa, 1)
            act.activation(AA[:, :], PA[:, 0:SR], ACT.Copy).then_inc(s_aa, 1)
            for i in range(NT + LAG_Z + 1):
                if i < NT:
                    act.wait_ge(s_mv, i + 1)
                    act.activation(sd[:, i:i + 1], mv[:, i, 1:2], ACT.Sqrt, bias=cst["eps"][:, 0:1]).then_inc(s_sd, 1)
                if 1 <= i <= NT:
                    j = i - 1
                    act.wait_ge(s_x1, j + 1)
                    if j >= 2:
                        act.wait_ge(s_ssq, j - 1)
                    act.activation(junk[:, j % 2, :], X1[:, j, :], ACT.Square, accum_out=ssq[:, j:j + 1]).then_inc(s_ssq, 1)
                if LAG_T <= i < NT + LAG_T:
                    j = i - LAG_T
                    act.wait_ge(pe_tr, j + 1)
                    out = x1T[:, :, j % B, (j // B) * P:(j // B + 1) * P]
                    act.activation(out, PT[j % 2][:, 0:KD * P].rearrange("p (k t) -> p k t", k=KD),
                                   ACT.Copy).then_inc(s_x1T, 1)
                if i > LAG_Z and (i - LAG_Z) % 2 == 0:
                    pair = (i - LAG_Z) // 2 - 1
                    act.wait_ge(s_cl, pair + 1)
                    z = Zd[:, 2 * pair:2 * pair + 2, PAD:PAD + SR]
                    act.activation(z, z, ACT.Sqrt).then_inc(s_zd, 1)

        @block.vector
        def _(dve):
            dve.memset(ones[:, :], 1.0).then_inc(s_one, 1)
            dve.memset(Zd[:, :, 0:PAD], BIG).then_inc(s_pad, 1)
            dve.memset(Zd[:, :, PAD + SR:PITCH], BIG).then_inc(s_pad, 1)
            dve.memset(cst["eps"][:, :], EPS).then_inc(s_pad, 1)
            dve.wait_ge(ld_c, 16)
            dve.tensor_tensor(sq[:], ctxT[:], ctxT[:], ALU.mult).then_inc(s_sq, 1)
            dve.wait_ge(s_sq, 1)
            dve.tensor_scalar(ctxT[:], ctxT[:], -2.0, None, ALU.mult).then_inc(s_sq, 1)
            dve.wait_ge(s_aa, 1)
            for i in range(NT + LAG_Z):
                if i < NT:
                    if i % B == 0:
                        dve.wait_ge(ld_x[i // B], 16)
                    dve.wait_ge(pe_o, i + 1)
                    dve.tensor_tensor(X1[:, i, :], X1[:, i, :], PO[i % 2][:, 0:D], ALU.add).then_inc(s_add, 1)
                    dve.wait_ge(s_add, i + 1)
                    dve.bn_stats(st[:, i % 2, :], X1[:, i, :]).then_inc(s_st, 1)
                    dve.wait_ge(s_st, i + 1)
                    dve.bn_aggr(mv[:, i, :], st[:, i % 2, :]).then_inc(s_mv, 1)
                if 1 <= i <= NT:
                    j = i - 1
                    dve.wait_ge(s_sd, j + 1)
                    dve.reciprocal(rs[:, j:j + 1], sd[:, j:j + 1]).then_inc(s_rs, 1)
                    dve.wait_ge(s_rs, j + 1)
                    dve.wait_ge(s_mv, j + 1)
                    dve.tensor_scalar(X1[:, j, :], X1[:, j, :], mv[:, j, 0:1], rs[:, j:j + 1],
                                      ALU.subtract, ALU.mult).then_inc(s_x1, 1)
                if i >= 2 and (i - 2) % B == B - 1 and i - 2 < NT:
                    t = (i - 2) // B
                    dve.wait_ge(s_ssq, B * (t + 1))
                    if t >= 1:
                        dve.wait_ge(pe_bb, t)
                    dve.tensor_tensor(mb[:, :, :], ssq[:, B * t:B * t + B].unsqueeze(2).broadcast_to([P, B, 4]),
                                      cst["quad"][:, :].unsqueeze(1).broadcast_to([P, B, 4]), ALU.mult).then_inc(s_mb, 1)
                if i % B == 2 and B < i < NT + B:
                    t = i // B - 1
                    dve.wait_ge(pe_bb, t + 1)
                    dve.tensor_copy(bb[:, 4 * t:4 * t + 4], PB[:, 4 * t:4 * t + 4]).then_inc(s_bb, 1)
                    dve.wait_ge(s_bb, t + 1)
                if i >= LAG_Z:
                    jb = i - LAG_Z
                    dve.wait_ge(pe_d, jb + 1)
                    dve.scalar_tensor_tensor(Zd[:, jb, PAD:PAD + SR], PD[jb % 2][:, 0:SR],
                                             bb[:, jb:jb + 1], AA[:, :], ALU.add, ALU.add).then_inc(s_d2, 1)
                    if jb % 2 == 1:
                        dve.wait_ge(s_d2, jb + 1)
                        z = Zd[:, jb - 1:jb + 1, PAD:PAD + SR]
                        dve.tensor_scalar(z, z, 0.0, None, ALU.max).then_inc(s_cl, 1)


def alignment_block(nc, dram, HG, Zd, PTa, PTb, Cs, Mf, cst):
    with ExitStack() as ctx:
        def sb(name, shape, dt=F32):
            return ctx.enter_context(nc.sbuf_tensor(name, shape, dt))

        def sem(name):
            return ctx.enter_context(nc.semaphore(name))

        Dof, Rof = 0, (STEPS + 1) * DREC
        assert Rof + (STEPS + 1) * REC + 1 + LANES * PITCH // 2 <= CT * B * T
        HGf = HG[:, :, :, :].rearrange("p c b t -> p (c b t)")
        Dk = HGf[:, Dof:Dof + (STEPS + 1) * DREC].rearrange("p (k j) -> p k j", j=DREC)
        R = HGf[:, Rof:Rof + (STEPS + 1) * REC].rearrange("p (k j) -> p k j", j=REC)
        edge = sb("edge", [P, 1])
        back = sb("back", [P, 1], BF16)
        PR = 2 * CW
        one_left = sb("one_left", [P, STEPS, PR], BF16)
        up_diag = sb("up_diag", [P, STEPS, PR], BF16)
        G = [sb(f"G{i}", [P, PR], BF16) for i in range(2)]
        Pk = Zd[:, :, :].rearrange("p j i -> p (j i)")[:, 0:STEPS * PR // 2].bitcast(BF16).rearrange("p (k m) -> p k m", m=PR)
        Zof = Rof + (STEPS + 1) * REC + 1
        Zq = HGf[:, Zof:Zof + LANES * PITCH // 2].bitcast(BF16).rearrange("p (j i) -> p j i", i=PITCH)
        eyeb = sb("eyeb", [P, P], BF16)
        room = [t[:, :, :].rearrange("p j i -> p (j i)").bitcast(F32) for t in (PTa, PTb)]
        trg = [room[0][:, i * KD * D:(i + 1) * KD * D].rearrange("p (k d) -> p k d", k=KD) for i in range(3)]
        wri = room[1][:, 0:2 * KD * D].rearrange("p (w k d) -> p w k d", w=2, k=KD)
        p12 = room[1][:, 2 * KD * D:4 * KD * D].rearrange("p (o k d) -> p o k d", o=2, k=KD)
        cf = sb("cf", [P, B, D])
        bank = [ctx.enter_context(nc.psum_tensor(f"c_bank{i}", [P, 512], F32)) for i in range(4)]
        tb = [ctx.enter_context(nc.psum_tensor(f"c_tb{i}", [P, 8, P], BF16)) for i in range(4)]

        ld_f, ld_c = sem("c_ld_f"), sem("c_ld_c")
        s_fill, s_eye, pe_r, s_pr = (sem("c_" + k) for k in ("fill", "eye", "pe_r", "pr"))
        s_init, s_skew, s_min, s_row, s_edge = (sem("c_" + k) for k in ("init", "skew", "min", "row", "edge"))
        s_ch, s_bw, s_g, s_back, s_path = (sem("c_" + k) for k in ("ch", "bw", "g", "back", "path"))
        s_zq, pe_z, s_pt, s_split, pe_m, s_m, s_cz = (sem("c_" + k) for k in ("zq", "pe_z", "pt", "split", "pe_m", "m", "cz"))
        block = ctx.enter_context(nc.Block())
        REM = SR - P

        @block.sync
        def _(sp):
            for i, k in enumerate(("cos", "sin", "msin")):
                sp.dma_start(trg[i][:, :, :], dram[k].rearrange("(k p) n -> p k n", p=P)).then_inc(ld_f, 16)
            for i, k in enumerate(("w_re", "w_im")):
                sp.dma_start(wri[:, i], dram[k].rearrange("(k p) n -> p k n", p=P)).then_inc(ld_f, 16)
            cr = dram["ctx"].rearrange("b s d -> s b d")
            sp.dma_start(cf[:, :, :], cr[0:P]).then_inc(ld_c, 16)
            sp.wait_ge(s_split, 5)
            sp.dma_start(cf[0:REM], cr[P:SR]).then_inc(ld_c, 16)

        @block.gpsimd
        def _(pool):
            pool.memset(one_left[:, :, :], 1.0).then_inc(s_fill, 1)
            n = 0
            for sl, rows in ((0, P), (1, REM)):
                pool.wait_ge(ld_c, 16 * (sl + 1))
                c = cf[0:rows]
                for part in range(3):
                    o = Cs[0:rows, sl, part]
                    pool.tensor_copy(o, c).then_inc(s_split, 1)
                    n += 1
                    pool.wait_ge(s_split, n)
                    if part < 2:
                        pool.tensor_tensor(c, c, o, ALU.subtract).then_inc(s_split, 1)
                        n += 1
                        pool.wait_ge(s_split, n)
            pool.wait_ge(s_m, 4 + KD)
            for m in range(KD):
                d = Mf[:, m, m * P:(m + 1) * P]
                pool.tensor_tensor(d, d, cst["eye"][:, :], ALU.add).then_inc(s_eye, 1)
            pool.wait_ge(s_eye, KD)

        @block.tensor
        def _(te):
            te.wait_ge(ld_f, 80)
            terms = (((0, 0), (1, 1)), ((1, 0), (0, 2)))
            for o in range(2):
                for m in range(KD):
                    n = 0
                    for wi, tr in terms[o]:
                        for k in range(KD):
                            last = te.matmul(bank[2 * o + m][:, 0:D], wri[:, wi, k, m * P:(m + 1) * P], trg[tr][:, k, :],
                                             start=(n == 0), stop=(n == 3))
                            n += 1
                    last.then_inc(pe_m, 1)
            te.wait_ge(s_m, 4)
            for m in range(KD):
                n = 0
                for o, tr in ((0, 0), (1, 2)):
                    for k in range(KD):
                        last = te.matmul(bank[m][:, 0:D], p12[:, o, k, m * P:(m + 1) * P], trg[tr][:, k, :],
                                         start=(n == 0), stop=(n == 3))
                        n += 1
                last.then_inc(pe_m, 1)
            te.wait_ge(s_zq, NCK - P // CHUNK)
            for q in range(LANES // 8):
                if q >= 2:
                    te.wait_ge(s_pr, q - 1)
                for j in range(8):
                    last = te.transpose(tb[2 + q % 2][0:REM, j, :], Zq[:, 8 * q + j, PAD + P:PAD + SR], eyeb[:, :])
                last.then_inc(pe_r, 1)
            for i, q in enumerate(reversed(range(LANES // 8))):
                te.wait_ge(s_zq, NCK - 8 * q // CHUNK)
                if i >= 2:
                    te.wait_ge(s_pt, i - 1)
                for j in range(8):
                    last = te.transpose(tb[i % 2][:, j, :], Zq[:, 8 * q + j, PAD:PAD + P], eyeb[:, :])
                last.then_inc(pe_z, 1)

        @block.scalar
        def _(act):
            for i in range(4):
                act.wait_ge(pe_m, i + 1)
                act.activation(p12[:, i // 2, i % 2, :], bank[i][:, 0:D], ACT.Copy).then_inc(s_m, 1)
            for m in range(KD):
                act.wait_ge(pe_m, 5 + m)
                act.activation(Mf[:, m, :], bank[m][:, 0:D], ACT.Copy, scale=1.0 / D).then_inc(s_m, 1)

            def place(pt, rows, q, src):
                out = pt[0:rows].rearrange("p b (j l) -> p j b l", l=L)[:, 8 * q:8 * q + 8]
                return act.activation(out, src[0:rows].rearrange("p j (b l) -> p j b l", b=B), ACT.Copy)

            for q in range(LANES // 8):
                act.wait_ge(pe_r, q + 1)
                place(PTb, REM, q, tb[2 + q % 2]).then_inc(s_pr, 1)
            for i, q in enumerate(reversed(range(LANES // 8))):
                act.wait_ge(pe_z, i + 1)
                place(PTa, P, q, tb[i % 2]).then_inc(s_pt, 1)

        @block.vector
        def _(dve):
            inits = [(R[:, 0, :], BIG), (Dk[:, 0, :], BIG), (Dk[:, 1:STEPS + 1, 0], BIG), (Dk[:, 1:STEPS + 1, 1], 0.0),
                     (edge[:, :], BIG), (G[0][:, :], 0.0)]
            for a, v in inits:
                dve.memset(a, v).then_inc(s_init, 1)
            dve.wait_ge(s_init, len(inits))
            n0 = len(inits)
            for b in range(B):
                o = slice(L * b, L * b + 1)
                dve.memset(Dk[o, 0, 1:2], 0.0).then_inc(s_init, 1)
                dve.memset(Dk[o, 1:STEPS + 1, 1:2], BIG).then_inc(s_init, 1)
            dve.tensor_copy(eyeb[:, :], cst["eye"][:, :]).then_inc(s_init, 1)
            dve.tensor_copy(back[:, :], cst["last"][:, :]).then_inc(s_init, 1)

            def steps_of(c):
                return CHUNK * c, min(CHUNK * (c + 1), STEPS)

            def skew(c):
                k0, k1 = steps_of(c)
                src = view(Zd[:, :, :], PAD + k0, (1, k1 - k0), (PITCH - 1, LANES))
                dve.transpose(Dk[:, k0 + 1:k1 + 1, 2:DREC], src).then_inc(s_skew, 1)

            def choose(c, part):
                k0, k1 = steps_of(c)
                diag, up, left = R[:, k0:k1, 0:CW], R[:, k0:k1, 1:REC], R[:, k0 + 1:k1 + 1, 0:CW]
                to_left, to_up, to_diag = (view(t[:, :, :], PR * k0 + slot, (PR, k1 - k0), (-2, CW)) for t, slot in
                                           ((one_left, PR - 1), (up_diag, PR - 2), (up_diag, PR - 1)))
                if part == 0:
                    if c == 0:
                        dve.wait_ge(s_fill, 1)
                    dve.tensor_tensor(to_left, Dk[:, k0:k1, 1:REC], left, ALU.is_gt).then_inc(s_ch, 1)
                if part == 1:
                    dve.tensor_tensor(to_diag, diag, up, ALU.is_le).then_inc(s_ch, 1)
                if part == 2:
                    dve.wait_ge(s_ch, 4 * c + 2)
                    dve.scalar_tensor_tensor(to_up, to_left, 0.0, to_diag, ALU.is_equal, ALU.is_gt).then_inc(s_ch, 1)
                if part == 3:
                    dve.wait_ge(s_ch, 4 * c + 3)
                    dve.scalar_tensor_tensor(to_diag, to_left, 0.0, to_diag, ALU.is_equal, ALU.mult).then_inc(s_ch, 1)

            dve.wait_ge(s_init, n0 + 2 * B + 2)
            skew(0)
            shift = [LANES - 1] + list(range(LANES - 1))
            for k in range(STEPS):
                if k % CHUNK == 0:
                    dve.wait_ge(s_skew, k // CHUNK + 1)
                if k >= 1:
                    dve.wait_ge(s_row, k)
                    dve.tensor_tensor(Dk[:, k, 1:REC], R[:, k, 1:REC], R[:, k, 0:CW], ALU.min).then_inc(s_min, 1)
                    dve.stream_shuffle(edge[:, :], R[:, k, CW:REC], shift).then_inc(s_edge, 1)
                    c, at = k // CHUNK, k % CHUNK
                    if at == 1 and c + 1 < NCK:
                        skew(c + 1)
                    elif c >= 1:
                        choose(c - 1, {0: 0, 2: 1, 3: 2}[at])
                    dve.wait_ge(s_edge, k)
                    dve.wait_ge(s_min, k)
                dve.tensor_tensor_scan(R[:, k + 1, :], Dk[:, k, 0:REC], Dk[:, k + 1, 1:DREC], edge[:, 0:1],
                                       ALU.min, ALU.add).then_inc(s_row, 1)
                if k % CHUNK == CHUNK - 1 and k >= 2 * CHUNK - 1:
                    choose(k // CHUNK - 1, 3)
            dve.wait_ge(s_row, STEPS)
            last = NCK - 1
            for part in range(4):
                if CHUNK * last + (0, 2, 3, 3)[part] >= STEPS:
                    choose(last - 1, part)
            for part in range(4):
                choose(last, part)
            dve.wait_ge(s_ch, 4 * NCK)
            for b in range(B):
                o = slice(L * b, L * b + 1)
                dve.memset(up_diag[o, :, PR - 1:PR], 0.0).then_inc(s_cz, 1)
                dve.memset(one_left[o, :, PR - 1:PR], 0.0).then_inc(s_cz, 1)
            dve.wait_ge(s_cz, 2 * B)

            def unskew(c):
                k0, k1 = steps_of(c)
                dst = view(Zq, PAD + k0, (1, k1 - k0), (PITCH - 1, LANES))
                dve.transpose(dst, view(Pk, PR * k0 + PR - 2, (PR, k1 - k0), (-2, CW))).then_inc(s_zq, 1)

            shift = list(range(1, LANES)) + [0]
            for n in range(STEPS):
                k = STEPS - 1 - n
                g = G[n % 2]
                if n >= 1:
                    dve.wait_ge(s_path, n)
                    on = Pk[:, k + 1, :].rearrange("p (j two) -> p j two", two=2)[:, :, 0:1].broadcast_to([P, CW, 2])
                    dve.tensor_tensor(g[:, :].rearrange("p (j two) -> p j two", two=2),
                                      up_diag[:, k + 1, :].rearrange("p (j two) -> p j two", two=2), on,
                                      ALU.mult).then_inc(s_g, 1)
                    dve.stream_shuffle(back[:, :], Pk[:, k + 1, PR - 1:PR], shift).then_inc(s_back, 1)
                    if (k + 1) % CHUNK == 0:
                        unskew((k + 1) // CHUNK)
                    dve.wait_ge(s_back, n)
                    dve.wait_ge(s_g, n)
                dve.tensor_tensor_scan(Pk[:, k, :], one_left[:, k, :], g[:, :], back[:, 0:1],
                                       ALU.mult, ALU.add).then_inc(s_path, 1)
            dve.wait_ge(s_path, STEPS)
            unskew(0)
            dve.wait_ge(s_zq, NCK)


def output_block(nc, dram, X1, PTa, PTb, Cs, Mf, cst):
    REM = SR - P
    with ExitStack() as ctx:
        def sb(name, shape, dt=F32):
            return ctx.enter_context(nc.sbuf_tensor(name, shape, dt))

        def sem(name):
            return ctx.enter_context(nc.semaphore(name))

        bank = [ctx.enter_context(nc.psum_tensor(f"d_bank{i}", [P, 512], F32)) for i in range(8)]
        PA, PT, PF = bank[0:2], bank[2:4], bank[4:8]
        x2T = sb("x2T", [P, 4, KD, P])
        st = sb("d_st", [P, 4, 6])
        mv = sb("d_mv", [P, 2, NT, 2])
        sd = sb("d_sd", [P, 2, NT])
        rs = sb("d_rs", [P, 2, NT])
        nm = sb("d_nm", [P, 2, NT])
        bias = sb("d_bias", [1, D])
        ones = sb("d_ones", [1, P])
        s = {k: sem("d_" + k) for k in ("ld", "one", "pe_x", "add", "pe_t", "x2T", "pe_f", "x2", "y", "out")}
        s_st, s_mv, s_sd, s_rs, s_nm = ([sem(f"d_{k}{i}") for i in range(2)] for k in ("st", "mv", "sd", "rs", "nm"))
        block = ctx.enter_context(nc.Block())
        LAG_T, LAG_F, LAG_Y = 3, 5, 6

        @block.sync
        def _(sp):
            sp.dma_start(bias[:, :], dram["ffn_bias"].rearrange("(o d) -> o d", o=1)).then_inc(s["ld"], 16)
            ot = dram["out"].rearrange("(b i p) d -> p i b d", b=B, p=P)
            for i in range(NI):
                sp.wait_ge(s["y"], B * (i + 1))
                sp.dma_start(ot[:, i], X1[:, i * B:(i + 1) * B, :]).then_inc(s["out"], 16)
            sp.wait_ge(s["out"], 16 * NI)

        @block.tensor
        def _(te):
            for i in range(NT + LAG_F):
                if i < NT:
                    b = i % B
                    if i >= 2:
                        te.wait_ge(s["add"], i - 1)
                    n = 0
                    for sl, rows, pt in ((0, P, PTa), (1, REM, PTb)):
                        lhs = token_tile(pt[0:rows], i)
                        for part in range(3):
                            last = te.matmul(PA[i % 2][:, 0:D], lhs, Cs[0:rows, sl, part, b, :], start=(n == 0), stop=(n == 5))
                            n += 1
                    last.then_inc(s["pe_x"], 1)
                if LAG_T <= i < NT + LAG_T:
                    j = i - LAG_T
                    te.wait_ge(s["x2"], j + 1)
                    if j >= 2:
                        te.wait_ge(s["x2T"], j - 1)
                    for k in range(KD):
                        last = te.transpose(PT[j % 2][:, k * P:(k + 1) * P], X1[:, j, k * P:(k + 1) * P], cst["eye"][:, :])
                    last.then_inc(s["pe_t"], 1)
                if LAG_F <= i:
                    j = i - LAG_F
                    if j == 0:
                        te.wait_ge(s["ld"], 16)
                        te.wait_ge(s["one"], 1)
                    if j >= 4:
                        te.wait_ge(s["y"], j - 3)
                    te.matmul(PF[j % 4][:, 0:D], ones[:, :], bias[:, :], start=True, stop=False)
                    te.wait_ge(s["x2T"], j + 1)
                    for k in range(KD):
                        last = te.matmul(PF[j % 4][:, 0:D], x2T[:, j % 4, k, :], Mf[:, k, :], start=False, stop=(k == KD - 1))
                    last.then_inc(s["pe_f"], 1)

        @block.scalar
        def _(act):
            def deviation(j, half):
                act.wait_ge(s_mv[half], j + 1)
                act.activation(sd[:, half, j:j + 1], mv[:, half, j, 1:2], ACT.Sqrt, bias=cst["eps"][:, 0:1]).then_inc(s_sd[half], 1)

            def normalize(j, half, src, done):
                act.wait_ge(s_nm[half], j + 1)
                act.activation(X1[:, j, :], src, ACT.Identity, scale=rs[:, half, j:j + 1],
                               bias=nm[:, half, j:j + 1]).then_inc(done, 1)

            for i in range(NT + LAG_Y + 1):
                if i < NT:
                    deviation(i, 0)
                if 1 <= i <= NT:
                    normalize(i - 1, 0, X1[:, i - 1, :], s["x2"])
                if LAG_T <= i < NT + LAG_T:
                    j = i - LAG_T
                    act.wait_ge(s["pe_t"], j + 1)
                    if j >= 4:
                        act.wait_ge(s["pe_f"], j - 3)
                    act.activation(x2T[:, j % 4].rearrange("p k t -> p (k t)"), PT[j % 2][:, 0:KD * P], ACT.Copy).then_inc(s["x2T"], 1)
                if LAG_Y <= i and i - LAG_Y < NT:
                    deviation(i - LAG_Y, 1)
                if LAG_Y + 1 <= i:
                    j = i - LAG_Y - 1
                    normalize(j, 1, PF[j % 4][:, 0:D], s["y"])

        @block.vector
        def _(dve):
            dve.memset(ones[:, :], 1.0).then_inc(s["one"], 1)

            def moments(j, half, src):
                slot = 2 * half + j % 2
                dve.bn_stats(st[:, slot, :], src).then_inc(s_st[half], 1)
                dve.wait_ge(s_st[half], j + 1)
                dve.bn_aggr(mv[:, half, j, :], st[:, slot, :]).then_inc(s_mv[half], 1)

            def scale(j, half):
                dve.wait_ge(s_sd[half], j + 1)
                dve.reciprocal(rs[:, half, j:j + 1], sd[:, half, j:j + 1]).then_inc(s_rs[half], 1)
                dve.wait_ge(s_rs[half], j + 1)
                dve.wait_ge(s_mv[half], j + 1)
                dve.scalar_tensor_tensor(nm[:, half, j:j + 1], mv[:, half, j, 0:1], -1.0, rs[:, half, j:j + 1],
                                         ALU.mult, ALU.mult).then_inc(s_nm[half], 1)

            for i in range(NT + LAG_Y + 1):
                if i < NT:
                    dve.wait_ge(s["pe_x"], i + 1)
                    dve.tensor_tensor(X1[:, i, :], X1[:, i, :], PA[i % 2][:, 0:D], ALU.add).then_inc(s["add"], 1)
                if 1 <= i <= NT:
                    scale(i - 1, 0)
                if i < NT:
                    dve.wait_ge(s["add"], i + 1)
                    moments(i, 0, X1[:, i, :])
                if LAG_Y <= i and i - LAG_Y < NT:
                    j = i - LAG_Y
                    dve.wait_ge(s["pe_f"], j + 1)
                    moments(j, 1, PF[j % 4][:, 0:D])
                if LAG_Y + 1 <= i:
                    scale(i - LAG_Y - 1, 1)


def build_program(nc, dram):
    with ExitStack() as ctx:
        HG = ctx.enter_context(nc.sbuf_tensor("HG", [P, CT, B, T], F32))
        cst = {"tri": ctx.enter_context(nc.sbuf_tensor("tri", [P, 8, L], F32)),
               "eye": ctx.enter_context(nc.sbuf_tensor("eye", [P, P], F32)),
               "quad": ctx.enter_context(nc.sbuf_tensor("quad", [P, 4], F32)),
               "last": ctx.enter_context(nc.sbuf_tensor("last", [P, 1], F32)),
               "bias": ctx.enter_context(nc.sbuf_tensor("bias", [P, 3, CT], F32)),
               "slope": ctx.enter_context(nc.sbuf_tensor("slope", [P, 2, CT], F32)),
               "flag": ctx.enter_context(nc.sbuf_tensor("flag", [1, 1], I32)),
               "eps": ctx.enter_context(nc.sbuf_tensor("eps", [P, 1], F32))}
        recurrence_block(nc, dram, HG, cst)
        general_recurrence_block(nc, dram, HG, cst)
        X1 = ctx.enter_context(nc.sbuf_tensor("x_all", [P, NT, D], F32))
        Zd = ctx.enter_context(nc.sbuf_tensor("Zd", [P, LANES, PITCH], F32))
        project_and_distance_block(nc, dram, HG, X1, Zd, cst)
        PTa = ctx.enter_context(nc.sbuf_tensor("PTa", [P, B, T], BF16))
        PTb = ctx.enter_context(nc.sbuf_tensor("PTb", [P, B, T], BF16))
        Cs = ctx.enter_context(nc.sbuf_tensor("Cs", [P, 2, 3, B, D], BF16))
        Mf = ctx.enter_context(nc.sbuf_tensor("Mf", [P, KD, D], F32))
        alignment_block(nc, dram, HG, Zd, PTa, PTb, Cs, Mf, cst)
        output_block(nc, dram, X1, PTa, PTb, Cs, Mf, cst)



def constant_tables():
    import numpy as np
    r = np.arange(L)
    eye = (r[:, None] == r[None, :])
    low = (r[:, None] > r[None, :])
    masks = [eye, low]
    for m in (1,) + LEVELS:
        masks.append((r[:, None] // (2 * m) == r[None, :] // (2 * m)) & (r[:, None] // m > r[None, :] // m))
    masks = masks + [eye] * (8 - len(masks))
    tri = np.stack(masks, 1).astype(np.float32)
    return np.ascontiguousarray(np.tile(tri, (B, 1, 1)))



def transform_tables():
    import numpy as np
    n = np.arange(D)
    turn = 2 * np.pi * (np.outer(n, n) % D) / D
    p = np.arange(P)
    return {
        "eye": np.eye(P, dtype=np.float32),
        "quad": (p[:, None] // L == np.arange(4)).astype(np.float32),
        "last": (p[:, None] % L == L - 1).astype(np.float32),
        "cos": np.cos(turn).astype(np.float32),
        "sin": np.sin(turn).astype(np.float32),
        "msin": (-np.sin(turn)).astype(np.float32),
    }


def kernel(x, ctx_1024, L0_attn_omega, L0_attn_Win, L0_attn_Wl, L0_attn_bl, L0_attn_Wv, L0_attn_bv, L0_attn_Wout,
           L0_ffn_w_freq_real, L0_ffn_w_freq_imag, L0_ffn_bias):
    import numpy as np
    import concourse.bacc as bacc
    from concourse.bass_utils import run_bass_kernel_spmd

    def cols(v):
        return np.asarray(v).reshape(CT, P).T

    x = np.asarray(x)
    arrays = {
        "x_tok": x.reshape(B * T, D),
        "x_t": x.transpose(2, 0, 1).reshape(KD, P, B, T),
        "win": np.asarray(L0_attn_Win),
        "win_t": np.asarray(L0_attn_Win).T,
        "wlv_t": np.stack([np.asarray(L0_attn_Wl).T, np.asarray(L0_attn_Wv).T]),
        "bias": np.stack([cols(L0_attn_bl), cols(L0_attn_bv), cols(L0_attn_omega)], 1),
        "wout_t": np.asarray(L0_attn_Wout).T,
        "ctx": np.asarray(ctx_1024),
        "ctx_t": np.asarray(ctx_1024).transpose(2, 0, 1).reshape(KD, P, B, SR),
        "w_re": np.asarray(L0_ffn_w_freq_real),
        "w_im": np.asarray(L0_ffn_w_freq_imag),
        "ffn_bias": np.asarray(L0_ffn_bias),
        "tri": constant_tables(),
        **transform_tables(),
    }
    nc = bacc.Bacc("TRN2", target_bir_lowering=False, num_devices=1)
    ins, dram = {}, {}
    for name, a in arrays.items():
        a = np.ascontiguousarray(a)
        ins["in_" + name] = a
        dram[name] = nc.dram_tensor("in_" + name, a.shape, mybir.dt.from_np(a.dtype), kind="ExternalInput").ap()
    dram["out"] = nc.dram_tensor("out_y", (B * T, D), F32, kind="ExternalOutput").ap()
    build_program(nc, dram)
    r = run_bass_kernel_spmd(nc, [ins], core_ids=[0])
    return r.results[0]["out_y"].reshape(B, T, D)
```

```python
from contextlib import ExitStack

import concourse.bass as bass
from concourse import mybir

ALU = mybir.AluOpType
ACT = mybir.ActivationFunctionType
AX = mybir.AxisListType
F32 = mybir.dt.float32
BF16 = mybir.dt.bfloat16
I32 = mybir.dt.int32

P = 128
B, T, D = 4, 1024, 256
DI = 512
KD = D // P
CT = DI // P
L = 32
NCH = 4
GT = L * NCH
NG = T // GT
CB = CT * B
SEG = NCH * CB
NTOK = B * GT
L1 = L + 1
LEVELS = (2, 4, 8, 16)
STEEP = 40.0 / L
TSTART = 10
TOPS = TSTART + 3 * (len(LEVELS) - 1) + 2 + B


def recurrence_block(nc, dram, HG, ahead, cst):
    with ExitStack() as ctx:
        def sb(name, shape, dt=F32):
            return ctx.enter_context(nc.sbuf_tensor(name, shape, dt))

        def sem(name):
            return ctx.enter_context(nc.semaphore(name))

        bank = [ctx.enter_context(nc.psum_tensor(f"bank{i}", [P, 512], F32)) for i in range(8)]
        PJ = bank[0:4]
        GR, TI, CQ, CP = bank[4:8]

        win_t = sb("win_t", [P, KD, 2 * DI])
        wc = sb("wc", [P, 2, KD, DI])
        bias = cst["bias"]
        tri = cst["tri"]
        xT = sb("xT", [P, 2, KD, B, GT])
        lam = [sb(f"lam{i}", [P, SEG, L1]) for i in range(2)]
        S = sb("S", [P, SEG, L1])
        V = [sb(f"V{i}", [P, SEG, L]) for i in range(2)]
        X = [sb(f"X{i}", [P, SEG, L]) for i in range(2)]
        U = [sb(f"U{i}", [P, SEG, L]) for i in range(2)]
        KB = sb("KB", [P, SEG, 2, L])
        keep = sb("keep", [P, CB, L1])
        sz = sb("sz", [P, 2, NTOK])
        E = sb("E", [P, CB, L1])
        H = [sb(f"H{i}", [P, CB, L1]) for i in range(NCH)]
        gm = sb("gm", [P, NCH, 2, L])
        vc = sb("vc", [P, NCH, 2])
        negc = [sb(f"negc{i}", [P, NCH]) for i in range(2)]
        w = [sb(f"w{i}", [P, NCH]) for i in range(2)]
        N = sb("N", [P, NCH, L])
        Tm = sb("Tm", [P, NCH, L])
        St = sb("St", [P, NCH, L])
        Ym = sb("Ym", [P, NCH, L])
        Sd = [sb(f"Sd{i}", [P, NCH, B, L]) for i in range(2)]
        qs = sb("qs", [P, 1])
        idle = sb("idle", [P, L], BF16)
        rng = sb("rng", [P, 2])
        sp = sb("sp", [P, 8, CT])
        slope = cst["slope"]
        HGf = HG[:, :, :, :].rearrange("p c b t -> p (c b t)")
        wlv = HGf[:, 0:2 * CT * DI].rearrange("p (w i j) -> p w i j", w=2, i=CT)
        win_x = HGf[:, 2 * CT * DI:2 * CT * DI + CT * D].rearrange("p (i d) -> p i d", i=CT)

        ld = {k: sem("ld_" + k) for k in ("in", "w", "small", "x0", "x1")}
        s_const, s_wc, s_wce, s_slope = sem("s_const"), sem("s_wc"), sem("s_wce"), sem("s_slope")
        pe = {k: sem("pe_" + k) for k in "lzvx"}
        ev = {k: sem("ev_" + k) for k in "lvxz"}
        act_sz = sem("act_sz")
        s_fix = sem("s_fix")
        s_scan, s_gex, s_lam, s_ginv = sem("s_scan"), sem("s_gex"), sem("s_lam"), sem("s_ginv")
        s_u, s_kb, s_nb, s_a = sem("s_u"), sem("s_kb"), sem("s_nb"), sem("s_a")
        pe_gram, s_t, pe_y, act_y, pe_t = sem("pe_gram"), sem("s_t"), sem("pe_y"), sem("act_y"), sem("pe_t")
        pe_q, s_qs, pe_p, s_e, s_h, s_g = sem("pe_q"), sem("s_qs"), sem("pe_p"), sem("s_e"), sem("s_h"), sem("s_g")
        s_flag = sem("s_flag")

        def seg(t, c):
            return t[:, :, :].rearrange("p (n c b) l -> p c b n l", n=NCH, c=CT)[:, c]

        block = ctx.enter_context(nc.Block())

        @block.sync
        def _(sp_):
            def load_x(g, par):
                for k in range(KD):
                    sp_.dma_start(xT[:, par, k], dram["x_t"][k][:, :, bass.ds(g * GT, GT)]).then_inc(ld[f"x{par}"], 16)

            sp_.dma_start(win_t[:, :, :], dram["win_t"].rearrange("(k p) n -> p k n", p=P)).then_inc(ld["in"], 16)
            load_x(0, 0)
            sp_.dma_start(win_x, dram["win"][0:DI, :].rearrange("(i p) d -> p i d", p=P)).then_inc(ld["w"], 16)
            sp_.dma_start(wlv, dram["wlv_t"].rearrange("w (i p) j -> p w i j", p=P)).then_inc(ld["w"], 16)
            sp_.dma_start(bias[:, :, :], dram["bias"]).then_inc(ld["small"], 16)
            for k in ("tri", "eye", "quad", "last"):
                sp_.dma_start(cst[k][:], dram[k]).then_inc(ld["small"], 16)

            load_x(1, 1)
            with sp_.Fori(1, NG // 2) as pair:
                for par in range(2):
                    sp_.wait_ge(pe["x"], (pair * 2 + (par - 1)) * CT)
                    load_x(pair * 2 + par, par)
            sp_.dma_start(ahead["ctxT"][:], dram["ctx_t"].rearrange("k p b s -> p k b s")).then_inc(ahead["ld_c"], 16)

        def group_loop(eng, body, before_last=None):
            body(-1, 1, False, True, True)
            with eng.Fori(0, NG // 2 - 1) as pair:
                body(pair * 2, 0, True, True, True)
                body(pair * 2 + 1, 1, True, True, True)
            body(NG - 2, 0, True, True, False)
            if before_last is not None:
                before_last()
            body(NG - 1, 1, True, False, False)

        @block.tensor
        def _(te):
            def multiply(kind, par, c, k):
                if kind in "lv":
                    lhs = wc[:, 0 if kind == "l" else 1, k, c * P:(c + 1) * P]
                else:
                    o = DI * (kind == "z") + c * P
                    lhs = win_t[:, k, o:o + P]
                return te.matmul(PJ[c][:, :], lhs, xT[:, par, k, :, :], start=(k == 0), stop=(k == KD - 1))

            def project(kind, G, par, c, halves=(0, 1)):
                if halves == (1,):
                    multiply(kind, par, c, 1).then_inc(pe[kind], 1)
                    return
                before = {"l": ("z", 0), "v": ("l", 0), "x": ("v", 0), "z": ("x", 1)}[kind]
                if not (kind == "z" and isinstance(G, int) and G == 0):
                    te.wait_ge(ev[before[0]], CT * (G - before[1]) + c + 1)
                if kind == "z" and c == 0:
                    te.wait_ge(ld[f"x{par}"], (G - par + 2) * (8 * KD))
                multiply(kind, par, c, 0)
                if halves == (0, 1):
                    multiply(kind, par, c, 1).then_inc(pe[kind], 1)

            def gram(G, par):
                te.wait_ge(s_kb, 2 * (G + 1))
                te.wait_ge(s_u, G + 1)
                for n in range(NCH):
                    for c in range(CT):
                        for b in range(B):
                            s = (n * CT + c) * B + b
                            last = te.matmul(GR[L * b:L * b + L, 2 * L * n:2 * L * (n + 1)], U[par][:, s, :],
                                             KB[:, s, :, :], start=(c == 0), stop=(c == CT - 1))
                last.then_inc(pe_gram, 1)

            def carry():
                te.matmul(TI[0:L, 2 * P:2 * P + 1], idle[:, 0:L], idle[:, 0:1], start=True, stop=True)

            def level_y(G, lv):
                te.wait_ge(s_t, TOPS * G + TSTART + 3 * lv)
                carry()
                for n in range(NCH):
                    for b in range(B):
                        q = slice(L * b, L * b + L)
                        last = te.matmul(TI[q, L * n:L * n + L], N[q, n, :], St[q, n, :], start=True, stop=True)
                last.then_inc(pe_y, 1)

            def level_t(G, lv):
                te.wait_ge(act_y, len(LEVELS) * G + lv + 1)
                carry()
                for n in range(NCH):
                    for b in range(B):
                        q = slice(L * b, L * b + L)
                        last = te.matmul(TI[q, P + L * n:P + L * n + L], Ym[q, n, :], Tm[q, n, :], start=True, stop=True)
                last.then_inc(pe_t, 1)

            def chain_q(g, par, n):
                te.wait_ge(s_h, NCH * g + n + 1)
                h0 = H[n - 1]
                for c in range(CT):
                    for b in range(B):
                        last = te.matmul(CQ[L * b:L * b + L, 0:1], U[par][:, (n * CT + c) * B + b, :],
                                         h0[:, c * B + b, L:L1], start=(c == 0), stop=(c == CT - 1))
                last.then_inc(pe_q, 1)

            def chain_p(g, par, n):
                te.wait_ge(s_qs, NCH * g + n + 1)
                te.matmul(CP[:, 0:P], qs[:, 0:1].broadcast_to([P, P]), Sd[par][:, n, :, :],
                          start=True, stop=True).then_inc(pe_p, 1)

            te.wait_ge(ld["in"], 16)
            for c in range(CT):
                project("z", 0, 0, c)
            te.wait_ge(ld["w"], 32)
            for j in range(2):
                for m in range(KD):
                    for i in range(CT):
                        last = te.matmul(bank[4 + 2 * j + m][:, :], win_x[:, i, m * P:(m + 1) * P], wlv[:, j, i, :],
                                         start=(i == 0), stop=(i == CT - 1))
                    last.then_inc(s_wc, 1)
            te.wait_ge(s_wce, 4)
            te.wait_ge(s_const, 9)
            for c in range(CT):
                project("l", 0, 0, c)

            def body(g, par, chain, do_vx, do_zl):
                nxt = 1 - par
                if chain:
                    chain_q(g, par, 0)
                if do_vx:
                    project("v", g + 1, nxt, 0)
                if chain:
                    chain_p(g, par, 0)
                if do_vx:
                    for c in range(1, CT):
                        project("v", g + 1, nxt, c)
                if chain:
                    chain_q(g, par, 1)
                if do_vx:
                    project("x", g + 1, nxt, 0)
                if chain:
                    chain_p(g, par, 1)
                if do_vx:
                    for c in range(1, CT):
                        project("x", g + 1, nxt, c)
                if chain:
                    chain_q(g, par, 2)
                if do_zl:
                    project("z", g + 2, par, 0)
                if chain:
                    chain_p(g, par, 2)
                if do_zl:
                    project("z", g + 2, par, 1)
                    project("z", g + 2, par, 2)
                if do_vx:
                    gram(g + 1, nxt)
                if chain:
                    chain_q(g, par, 3)
                if do_zl:
                    project("z", g + 2, par, 3)
                if chain:
                    chain_p(g, par, 3)
                for lv in range(len(LEVELS)):
                    if do_zl:
                        project("l", g + 2, par, lv, (0,))
                    if do_vx:
                        level_y(g + 1, lv)
                    if do_zl:
                        project("l", g + 2, par, lv, (1,))
                    if do_vx:
                        level_t(g + 1, lv)

            def count_outside():
                te.wait_ge(s_flag, 2)
                te.matmul(GR[0:1, 0:1], rng[:, 1:2], keep[:, 0, 1:2], start=True, stop=True).then_inc(s_flag, 1)

            group_loop(te, body, count_outside)

        @block.scalar
        def _(act):
            act.wait_ge(s_slope, 2)
            act.activation(sp[:, 1], sp[:, 0], ACT.Exp, scale=-1.0).then_inc(s_slope, 1)
            act.wait_ge(s_slope, 4)
            act.activation(sp[:, 3], sp[:, 2], ACT.Ln).then_inc(s_slope, 1)
            def bank_view(c):
                return PJ[c][:, :].rearrange("p (b n l) -> p b n l", b=B, n=NCH)

            def evac_z(G, c):
                act.wait_ge(pe["z"], CT * G + c + 1)
                if not (isinstance(G, int) and G == 0 and c < 2):
                    act.wait_ge(ev["z"], CT * G + c - 1)
                act.activation(sz[:, c % 2, :], PJ[c][:, :], ACT.Sigmoid).then_inc(act_sz, 1)

            def evac_l(G, par, c):
                act.wait_ge(pe["l"], CT * G + c + 1)
                act.activation(seg(lam[par], c)[:, :, :, 1:L1], bank_view(c), ACT.Sigmoid,
                               bias=bias[:, 0, c:c + 1]).then_inc(ev["l"], 1)

            def evac_y(G, lv):
                act.wait_ge(pe_y, len(LEVELS) * G + lv + 1)
                act.activation(Ym[:, :, :].rearrange("p n l -> p (n l)"), TI[:, 0:P], ACT.Copy).then_inc(act_y, 1)

            for c in range(CT):
                evac_z(0, c)
            for i in range(4):
                act.wait_ge(s_wc, i + 1)
                act.activation(wc[:, i // 2, i % 2, :], bank[4 + i][:, :], ACT.Copy).then_inc(s_wce, 1)
            act.wait_ge(ld["small"], 80)
            act.wait_ge(s_const, 9)
            for c in range(CT):
                evac_l(0, 0, c)

            def body(g, par, chain, do_vx, do_zl):
                nxt = 1 - par
                G = g + 1
                if do_vx:
                    if chain:
                        act.wait_ge(s_h, NCH * g + 1)
                    act.wait_ge(s_scan, NCH * (G + 1))
                    for c in range(CT):
                        act.activation(seg(U[nxt], c), seg(S, c)[:, :, :, 0:L], ACT.Exp,
                                       scale=slope[:, 0, c:c + 1]).then_inc(s_gex, 1)
                    for c in range(CT):
                        act.wait_ge(pe["v"], CT * G + c + 1)
                        act.activation(seg(V[nxt], c), bank_view(c), ACT.Identity,
                                       bias=bias[:, 1, c:c + 1]).then_inc(ev["v"], 1)
                    act.wait_ge(s_gex, CT * (G + 1))
                    for c in range(CT):
                        sc = seg(S, c)
                        act.activation(sc, sc, ACT.Exp, scale=slope[:, 1, c:c + 1]).then_inc(s_ginv, 1)
                    for c in range(CT):
                        lc = seg(lam[nxt], c)[:, :, :, 1:L1]
                        act.activation(lc, lc, ACT.Exp, scale=slope[:, 0, c:c + 1]).then_inc(s_lam, 1)
                    for c in range(CT):
                        act.wait_ge(pe["x"], CT * G + c + 1)
                        act.activation(seg(X[nxt], c), bank_view(c), ACT.Copy).then_inc(ev["x"], 1)
                if do_zl:
                    for c in range(CT):
                        evac_z(g + 2, c)
                for lv in range(len(LEVELS)):
                    if do_vx:
                        evac_y(G, lv)
                    if do_zl:
                        if chain and lv == 0:
                            act.wait_ge(s_h, NCH * (g + 1) + 1)
                        evac_l(g + 2, par, lv)

            group_loop(act, body)

        @block.vector
        def _(dve):
            consts = [(lam[0], 0.0), (lam[1], 0.0), (S, 0.0), (keep, 1.0), (E, 0.0), (Sd[0], 0.0), (Sd[1], 0.0), (idle, 0.0)]
            for i, (t, val) in enumerate(consts):
                dve.memset(t[:], val).then_inc(s_const, 1)
            dve.wait_ge(s_const, len(consts))
            dve.memset(keep[:, :, 0:1], 0.0).then_inc(s_const, 1)
            dve.wait_ge(s_const, 9)

            dve.wait_ge(ld["small"], 80)
            om = bias[:, 2, :]
            dve.tensor_scalar(sp[:, 4], om, -1.0, None, ALU.mult).then_inc(s_slope, 1)
            dve.wait_ge(s_slope, 1)
            dve.tensor_tensor(sp[:, 0], om, sp[:, 4], ALU.max).then_inc(s_slope, 1)
            dve.wait_ge(s_slope, 3)
            dve.tensor_scalar(sp[:, 2], sp[:, 1], 1.0, None, ALU.add).then_inc(s_slope, 1)
            dve.wait_ge(s_slope, 5)
            dve.tensor_scalar(sp[:, 4], sp[:, 2], 1.0, None, ALU.subtract).then_inc(s_slope, 1)
            dve.wait_ge(s_slope, 6)
            dve.tensor_scalar(sp[:, 5], sp[:, 4], 0.0, None, ALU.is_equal).then_inc(s_slope, 1)
            dve.wait_ge(s_slope, 7)
            dve.tensor_tensor(sp[:, 4], sp[:, 4], sp[:, 5], ALU.add).then_inc(s_slope, 1)
            dve.wait_ge(s_slope, 8)
            dve.reciprocal(sp[:, 6], sp[:, 4]).then_inc(s_slope, 1)
            dve.wait_ge(s_slope, 9)
            dve.tensor_tensor(sp[:, 3], sp[:, 3], sp[:, 6], ALU.mult).then_inc(s_slope, 1)
            dve.wait_ge(s_slope, 10)
            dve.tensor_tensor(sp[:, 3], sp[:, 3], sp[:, 5], ALU.add).then_inc(s_slope, 1)
            dve.wait_ge(s_slope, 11)
            dve.tensor_tensor(sp[:, 3], sp[:, 3], sp[:, 1], ALU.mult).then_inc(s_slope, 1)
            dve.wait_ge(s_slope, 12)
            dve.scalar_tensor_tensor(sp[:, 7], om, 0.0, sp[:, 3], ALU.max, ALU.add).then_inc(s_slope, 1)
            dve.wait_ge(s_slope, 13)
            dve.tensor_scalar(slope[:, 0], sp[:, 7], -8.0, None, ALU.mult).then_inc(s_slope, 1)
            dve.tensor_scalar(slope[:, 1], sp[:, 7], 8.0, STEEP, ALU.mult, ALU.min).then_inc(s_slope, 1)
            dve.wait_ge(s_slope, 15)

            def mul_z(G, c):
                dve.wait_ge(act_sz, CT * G + c + 1)
                out = HG[:, c, :, bass.ds(G * GT, GT)]
                dve.tensor_tensor(out, PJ[c][:, :].rearrange("p (b t) -> p b t", b=B),
                                  sz[:, c % 2, :].rearrange("p (b t) -> p b t", b=B), ALU.mult).then_inc(ev["z"], 1)

            def flat(t, n):
                return t[:, n * CB:(n + 1) * CB, :].rearrange("p s l -> p (s l)")

            def prefix(G, par):
                dve.wait_ge(ev["l"], CT * (G + 1))
                if isinstance(G, int) and G == 0:
                    dve.memset(lam[par][:, 0:CB, 1:2], 0.0).then_inc(s_fix, 1)
                    dve.wait_ge(s_fix, 1)
                else:
                    dve.wait_ge(s_ginv, CT * G)
                for n in range(NCH):
                    dve.tensor_tensor_scan(flat(S, n), keep[:, :, :].rearrange("p s l -> p (s l)"), flat(lam[par], n),
                                           0.0, ALU.mult, ALU.add).then_inc(s_scan, 1)

            def make_u(G, par):
                dve.wait_ge(ev["v"], CT * (G + 1))
                if isinstance(G, int) and G == 0:
                    dve.memset(V[par][:, 0:CB, 0:1], 0.0).then_inc(s_fix, 1)
                    dve.wait_ge(s_fix, 2)
                dve.wait_ge(s_gex, CT * (G + 1))
                dve.tensor_tensor(U[par][:, :, :], U[par][:, :, :], V[par][:, :, :], ALU.mult).then_inc(s_u, 1)

            def make_k(G, par):
                dve.wait_ge(s_ginv, CT * (G + 1))
                if not (isinstance(G, int) and G == 0):
                    dve.wait_ge(pe_gram, G)
                dve.tensor_tensor(KB[:, :, 0, :], V[par][:, :, :], S[:, :, 0:L], ALU.mult).then_inc(s_kb, 1)

            def make_a(G, par):
                dve.wait_ge(s_lam, CT * (G + 1))
                dve.wait_ge(s_kb, 2 * G + 1)
                dve.tensor_tensor(V[par][:, :, :], V[par][:, :, :], lam[par][:, :, 1:L1], ALU.mult).then_inc(s_a, 1)

            def make_b(G, par):
                dve.wait_ge(ev["x"], CT * (G + 1))
                if isinstance(G, int) and G == 0:
                    dve.tensor_copy(H[NCH - 1][:, :, L], X[0][:, 0:CB, 0]).then_inc(s_h, 1)
                    dve.wait_ge(s_h, 1)
                dve.wait_ge(s_lam, CT * (G + 1))
                dve.scalar_tensor_tensor(X[par][:, :, :], lam[par][:, :, 1:L1], 1.0, X[par][:, :, :],
                                         ALU.subtract, ALU.mult).then_inc(s_nb, 1)

            def make_kb(G, par):
                dve.wait_ge(s_nb, G + 1)
                dve.tensor_tensor(KB[:, :, 1, :], X[par][:, :, :], S[:, :, 1:L1], ALU.mult).then_inc(s_kb, 1)

            def mask(k):
                return tri[:, k, :].unsqueeze(1).broadcast_to([P, NCH, L])

            def t_start(G, par):
                base = TOPS * G
                dve.wait_ge(pe_gram, G + 1)
                A = GR[:, 0:2 * L * NCH].rearrange("p (n two l) -> p n two l", n=NCH, two=2)
                both = tri[:, 0:2, :].unsqueeze(1).broadcast_to([P, NCH, 2, L])
                dve.tensor_tensor(gm[:, :, :, :], A, both, ALU.mult).then_inc(s_t, 1)
                dve.wait_ge(s_t, base + 1)
                dve.tensor_reduce(vc[:, :, :], gm[:, :, :, :], AX.X, ALU.add).then_inc(s_t, 1)
                dve.wait_ge(s_t, base + 2)
                if isinstance(G, int) and G == 0:
                    for b in range(B):
                        dve.memset(vc[L * b:L * b + 1, 0, 0:1], 1.0).then_inc(s_fix, 1)
                    dve.wait_ge(s_fix, 2 + B)
                dve.reciprocal(w[par][:, :], vc[:, :, 0]).then_inc(s_t, 1)
                dve.wait_ge(s_t, base + 3)
                dve.tensor_scalar(w[par][:, :], w[par][:, :], -2.0, None, ALU.mult).then_inc(s_t, 1)
                dve.tensor_copy(negc[par][:, :], vc[:, :, 1]).then_inc(s_t, 1)
                dve.tensor_tensor(N[:, :, :], A[:, :, 0, :], mask(1), ALU.mult).then_inc(s_t, 1)
                dve.wait_ge(s_t, base + 6)
                dve.tensor_tensor(N[:, :, :], N[:, :, :], w[par][:, :].unsqueeze(2).broadcast_to([P, NCH, L]),
                                  ALU.mult).then_inc(s_t, 1)
                dve.wait_ge(s_t, base + 7)
                dve.tensor_tensor(Tm[:, :, :], N[:, :, :], mask(2), ALU.mult).then_inc(s_t, 1)
                dve.wait_ge(s_t, base + 8)
                dve.tensor_tensor(Tm[:, :, :], Tm[:, :, :], mask(0), ALU.add).then_inc(s_t, 1)
                dve.wait_ge(s_t, base + 9)
                dve.transpose(St[:, :, :], Tm[:, :, :]).then_inc(s_t, 1)
                dve.wait_ge(s_t, base + 10)

            def level(G, par, lv):
                base = TOPS * G + TSTART + 3 * lv
                dve.wait_ge(pe_t, len(LEVELS) * G + lv + 1)
                R = TI[:, P:2 * P].rearrange("p (n l) -> p n l", n=NCH)
                dve.tensor_tensor(gm[:, :, 0, :], R, mask(3 + lv), ALU.mult).then_inc(s_t, 1)
                dve.wait_ge(s_t, base + 1)
                dve.tensor_tensor(Tm[:, :, :], Tm[:, :, :], gm[:, :, 0, :], ALU.add).then_inc(s_t, 1)
                dve.wait_ge(s_t, base + 2)
                if lv < len(LEVELS) - 1:
                    dve.transpose(St[:, :, :], Tm[:, :, :]).then_inc(s_t, 1)
                    dve.wait_ge(s_t, base + 3)
                else:
                    for b in range(B):
                        q = slice(L * b, L * b + L)
                        dve.transpose(Sd[par][q, :, b, :], Tm[q, :, :]).then_inc(s_t, 1)
                    dve.wait_ge(s_t, base + 2 + B)

            def chain_start(g, par, n):
                q = NCH * g + n
                h0 = H[n - 1]
                dve.wait_ge(s_h, q + 1)
                dve.tensor_copy(E[:, :, 0:1], h0[:, :, L:L1]).then_inc(s_e, 1)
                dve.wait_ge(pe_q, q + 1)
                dve.tensor_scalar(qs[:, 0:1], CQ[:, 0:1], negc[par][:, n:n + 1], w[par][:, n:n + 1],
                                  ALU.subtract, ALU.mult).then_inc(s_qs, 1)

            def chain_end(g, par, n):
                q = NCH * g + n
                h1 = H[n]
                s0 = n * CB
                dve.wait_ge(pe_p, q + 1)
                p_all = CP[:, 0:P].rearrange("p (b l) -> p b l", b=B).unsqueeze(1).broadcast_to([P, CT, B, L])
                dve.tensor_tensor(E[:, :, 1:L1].rearrange("p (c b) l -> p c b l", c=CT),
                                  V[par][:, s0:s0 + CB, :].rearrange("p (c b) l -> p c b l", c=CT), p_all,
                                  ALU.mult).then_inc(s_e, 1)
                dve.wait_ge(s_e, 3 * q + 2)
                dve.tensor_tensor(E[:, :, 1:L1], E[:, :, 1:L1], X[par][:, s0:s0 + CB, :], ALU.subtract).then_inc(s_e, 1)
                dve.wait_ge(s_e, 3 * q + 3)
                dve.tensor_tensor_scan(h1[:, :, :].rearrange("p s l -> p (s l)"), flat(lam[par], n),
                                       E[:, :, :].rearrange("p s l -> p (s l)"), 0.0, ALU.mult, ALU.add).then_inc(s_h, 1)

            def gate(g, n):
                q = NCH * g + n
                dve.wait_ge(s_h, q + 2)
                h1 = H[n]
                t0 = L * n
                hg = HG[:, :, :, bass.ds(g * GT + t0, L)].rearrange("p c b t -> p (c b) t")
                dve.tensor_tensor(hg, hg, h1[:, :, 1:L1], ALU.mult).then_inc(s_g, 1)

            dve.wait_ge(s_wc, 4)
            for c in range(CT):
                mul_z(0, c)

            def body(g, par, do_chain, do_vx, do_zl):
                nxt = 1 - par
                if do_chain:
                    chain_start(g, par, 0)
                if do_vx:
                    prefix(g + 1, nxt)
                if do_chain:
                    chain_end(g, par, 0)
                    chain_start(g, par, 1)
                    if not do_vx:
                        gate(g, 0)
                if do_vx:
                    make_u(g + 1, nxt)
                if do_chain:
                    chain_end(g, par, 1)
                if do_vx:
                    make_k(g + 1, nxt)
                if do_chain:
                    chain_start(g, par, 2)
                    if not do_vx:
                        gate(g, 1)
                if do_vx:
                    make_b(g + 1, nxt)
                if do_chain:
                    chain_end(g, par, 2)
                if do_vx:
                    make_kb(g + 1, nxt)
                if do_zl:
                    mul_z(g + 2, 0)
                    mul_z(g + 2, 1)
                if do_vx:
                    make_a(g + 1, nxt)
                if do_chain:
                    chain_start(g, par, 3)
                    if not do_vx:
                        gate(g, 2)
                if do_vx:
                    t_start(g + 1, nxt)
                if do_chain:
                    chain_end(g, par, 3)
                if do_zl:
                    mul_z(g + 2, 2)
                    mul_z(g + 2, 3)
                for n in range(NCH):
                    if do_vx:
                        level(g + 1, nxt, n)
                    if do_chain and (do_vx or n == NCH - 1):
                        gate(g, n)
                if do_chain:
                    dve.wait_ge(s_g, NCH * (g + 1))

            def set_flag():
                dve.tensor_reduce(rng[:, 0:1], sp[:, 7], AX.X, ALU.max).then_inc(s_flag, 1)
                dve.wait_ge(s_flag, 1)
                dve.tensor_scalar(rng[:, 1:2], rng[:, 0:1], STEEP / 8.0, 0.0, ALU.is_le, ALU.is_equal).then_inc(s_flag, 1)
                dve.wait_ge(s_flag, 3)
                dve.tensor_scalar(cst["flag"][:, :], GR[0:1, 0:1], 1.0, None, ALU.min).then_inc(s_flag, 1)

            group_loop(dve, body, set_flag)


def general_recurrence_block(nc, dram, HG, X1, ahead, cst):
    with ExitStack() as ctx:
        def sb(name, shape, dt=F32):
            return ctx.enter_context(nc.sbuf_tensor(name, shape, dt))

        def sem(name):
            return ctx.enter_context(nc.semaphore(name))

        bank = [ctx.enter_context(nc.psum_tensor(f"g_bank{i}", [P, 512], F32)) for i in range(8)]
        PJ, SUM = bank[0:4], bank[6]
        win_t = sb("g_win_t", [P, KD, 2 * DI])
        win_x = sb("g_win_x", [P, CT, D])
        wlv = sb("g_wlv", [P, 2, CT, DI])
        wc = sb("g_wc", [P, 2, KD, DI])
        xg = sb("g_x", [P, KD, B, GT])
        lam = sb("g_lam", [P, CB, GT])
        v = sb("g_v", [P, CB, GT])
        xi = sb("g_xi", [P, CB, GT])
        ones = sb("g_ones", [P, P])
        h = sb("g_h", [P, CB])
        pr = sb("g_pr", [P, 2, CB])
        sm = sb("g_sm", [P, 2, B])
        co = sb("g_co", [P, B])
        u = sb("g_u", [P, CB])
        s = {k: sem("g_" + k) for k in ("w", "x", "wc", "wce", "init", "pj", "sig", "ev", "lam", "evz", "fix", "nb",
                                        "pr", "sum", "step", "done")}
        SOPS = 8
        block = ctx.enter_context(nc.Block())

        def when_flagged(eng, program):
            value = eng.value_load(cst["flag"][0:1, 0:1], min_val=0, max_val=1)
            with eng.If(value):
                program()

        def groups(eng, body):
            body(0, True)
            with eng.Fori(1, NG) as g:
                body(g, False)

        @block.sync
        def _(sp):
            def program():
                sp.dma_start(wlv[:], dram["wlv_t"].rearrange("w (i p) j -> p w i j", p=P)).then_inc(s["w"], 16)
                sp.dma_start(win_x[:], dram["win"][0:DI, :].rearrange("(i p) d -> p i d", p=P)).then_inc(s["w"], 16)
                sp.dma_start(win_t[:], dram["win_t"].rearrange("(k p) n -> p k n", p=P)).then_inc(s["w"], 16)

                def body(g, first):
                    if not first:
                        sp.wait_ge(s["pj"], 4 * CT * g)
                    for k in range(KD):
                        src = dram["x_t"][k][:, :, bass.ds(g * GT, GT)]
                        sp.dma_start(xg[:, k], src).then_inc(s["x"], 16)
                groups(sp, body)
            sp.dma_start(ahead["wout"][:], dram["wout_t"].rearrange("(c p) d -> p c d", p=P)).then_inc(ahead["ld_w"], 16)
            sp.dma_start(X1[:, 0:B, :], dram["x_tok"].rearrange("(b i p) d -> p i b d", b=B, p=P)[:, 0]).then_inc(ahead["ld_x0"], 16)
            when_flagged(sp, program)

        @block.tensor
        def _(te):
            def program():
                te.wait_ge(s["w"], 48)
                for j in range(2):
                    for m in range(KD):
                        for i in range(CT):
                            last = te.matmul(PJ[2 * j + m][:, :], win_x[:, i, m * P:(m + 1) * P], wlv[:, j, i, :],
                                             start=(i == 0), stop=(i == CT - 1))
                        last.then_inc(s["wc"], 1)
                te.wait_ge(s["wce"], 4)
                te.wait_ge(s["init"], 2)

                def body(g, first):
                    te.wait_ge(s["x"], (g + 1) * (16 * KD))
                    if not first:
                        te.wait_ge(s["done"], g)
                    for n in range(4 * CT):
                        kind, c = n // CT, n % CT
                        if kind == 1:
                            te.wait_ge(s["ev"], g * (3 * CT) + (c + 1))
                        if kind == 2:
                            te.wait_ge(s["evz"], g * CT + (c + 1))
                        if kind == 3:
                            te.wait_ge(s["ev"], g * (3 * CT) + (CT + c + 1))
                        for k in range(KD):
                            if kind in (0, 2):
                                lhs = wc[:, kind // 2, k, c * P:(c + 1) * P]
                            else:
                                o = DI * (kind == 1) + c * P
                                lhs = win_t[:, k, o:o + P]
                            last = te.matmul(PJ[n % 4][:, :], lhs, xg[:, k, :, :], start=(k == 0), stop=(k == KD - 1))
                        last.then_inc(s["pj"], 1)
                    with te.Fori(0, GT) as t:
                        te.wait_ge(s["pr"], (g * GT + t) * 2 + 2)
                        te.matmul(SUM[:, 0:2 * CB], ones[:, :], pr[:, :, :], start=True, stop=True).then_inc(s["sum"], 1)
                groups(te, body)
            when_flagged(te, program)

        @block.scalar
        def _(act):
            def program():
                for i in range(4):
                    act.wait_ge(s["wc"], i + 1)
                    act.activation(wc[:, i // 2, i % 2, :], PJ[i][:, :], ACT.Copy).then_inc(s["wce"], 1)

                def body(g, first):
                    for n in range(4 * CT):
                        kind, c = n // CT, n % CT
                        act.wait_ge(s["pj"], g * (4 * CT) + (n + 1))
                        flat = PJ[n % 4][:, :].rearrange("p (b t) -> p b t", b=B)
                        own = slice(c * B, c * B + B)
                        if kind == 0:
                            act.activation(lam[:, own, :], flat, ACT.Sigmoid, bias=cst["bias"][:, 0, c:c + 1]).then_inc(s["ev"], 1)
                        elif kind == 1:
                            act.activation(HG[:, c, :, bass.ds(g * GT, GT)], flat, ACT.Sigmoid).then_inc(s["sig"], 1)
                        elif kind == 2:
                            act.activation(v[:, own, :], flat, ACT.Identity, bias=cst["bias"][:, 1, c:c + 1]).then_inc(s["ev"], 1)
                        else:
                            act.activation(xi[:, own, :], flat, ACT.Copy).then_inc(s["ev"], 1)
                    for c in range(CT):
                        own = slice(c * B, c * B + B)
                        act.activation(lam[:, own, :], lam[:, own, :], ACT.Exp, scale=cst["slope"][:, 0, c:c + 1]).then_inc(s["lam"], 1)
                groups(act, body)
            when_flagged(act, program)

        @block.vector
        def _(dve):
            def program():
                dve.memset(ones[:, :], 1.0).then_inc(s["init"], 1)
                dve.memset(h[:, :], 0.0).then_inc(s["init"], 1)
                dve.wait_ge(s["init"], 2)

                def body(g, first):
                    for c in range(CT):
                        dve.wait_ge(s["sig"], g * CT + (c + 1))
                        hz = HG[:, c, :, bass.ds(g * GT, GT)]
                        dve.tensor_tensor(hz, hz, PJ[c][:, :].rearrange("p (b t) -> p b t", b=B), ALU.mult).then_inc(s["evz"], 1)
                    dve.wait_ge(s["evz"], (g + 1) * CT)
                    dve.wait_ge(s["ev"], (g + 1) * (3 * CT))
                    dve.wait_ge(s["lam"], (g + 1) * CT)
                    if first:
                        dve.memset(lam[:, :, 0:1], 0.0).then_inc(s["fix"], 1)
                        dve.memset(v[:, :, 0:1], 1.0).then_inc(s["fix"], 1)
                        dve.wait_ge(s["fix"], 2)
                    dve.scalar_tensor_tensor(xi[:, :, :], lam[:, :, :], 1.0, xi[:, :, :], ALU.subtract, ALU.mult).then_inc(s["nb"], 1)
                    with dve.Fori(0, GT) as t:
                        k = g * GT + t
                        at = bass.ds(t, 1)
                        vt = v[:, :, at].rearrange("p s o -> p (s o)")
                        lt = lam[:, :, at].rearrange("p s o -> p (s o)")
                        bt = xi[:, :, at].rearrange("p s o -> p (s o)")
                        dve.tensor_tensor(pr[:, 0, :], vt, h[:, :], ALU.mult).then_inc(s["pr"], 1)
                        dve.tensor_tensor(pr[:, 1, :], vt, vt, ALU.mult).then_inc(s["pr"], 1)
                        dve.wait_ge(s["sum"], k + 1)
                        dve.tensor_reduce(sm[:, :, :], SUM[:, 0:2 * CB].rearrange("p (two c b) -> p two b c", two=2, c=CT),
                                          AX.X, ALU.add).then_inc(s["step"], 1)
                        dve.wait_ge(s["step"], k * SOPS + 1)
                        dve.reciprocal(co[:, :], sm[:, 1, :]).then_inc(s["step"], 1)
                        dve.wait_ge(s["step"], k * SOPS + 2)
                        dve.scalar_tensor_tensor(co[:, :], co[:, :], -2.0, sm[:, 0, :], ALU.mult, ALU.mult).then_inc(s["step"], 1)
                        dve.wait_ge(s["step"], k * SOPS + 3)
                        dve.tensor_tensor(u[:, :].rearrange("p (c b) -> p c b", c=CT), vt.rearrange("p (c b) -> p c b", c=CT),
                                          co[:, :].unsqueeze(1).broadcast_to([P, CT, B]), ALU.mult).then_inc(s["step"], 1)
                        dve.wait_ge(s["step"], k * SOPS + 4)
                        dve.tensor_tensor(h[:, :], h[:, :], u[:, :], ALU.add).then_inc(s["step"], 1)
                        dve.wait_ge(s["step"], k * SOPS + 5)
                        dve.tensor_tensor(h[:, :], h[:, :], lt, ALU.mult).then_inc(s["step"], 1)
                        dve.wait_ge(s["step"], k * SOPS + 6)
                        dve.wait_ge(s["nb"], g + 1)
                        dve.tensor_tensor(h[:, :], h[:, :], bt, ALU.subtract).then_inc(s["step"], 1)
                        dve.wait_ge(s["step"], k * SOPS + 7)
                        hg = HG[:, :, :, bass.ds(k, 1)].rearrange("p c b o -> p (c b o)")
                        dve.tensor_tensor(hg, hg, h[:, :], ALU.mult).then_inc(s["step"], 1)
                        dve.wait_ge(s["step"], k * SOPS + SOPS)
                    dve.tensor_copy(co[:, :], sm[:, 0, :]).then_inc(s["done"], 1)
                    dve.wait_ge(s["done"], g + 1)
                groups(dve, body)
            when_flagged(dve, program)


NI = T // P
NT = B * NI
SR = 154
LANES = 32
CW = T // LANES
STEPS = SR + LANES - 1
PAD = LANES - 1
PITCH = SR + 2 * PAD
REC = CW + 1
DREC = REC + 1
CHUNK = 4
NCK = -(-STEPS // CHUNK)
FIRST = 8
PARTS = 3
BIG = 1e30
EPS = 1e-5


def view(t, off, *dims):
    return bass.AP(tensor=t.tensor, offset=t.offset + off, ap=[list(t.ap[0])] + [list(d) for d in dims])


def token_tile(t, i):
    return t[:, i % B, (i // B) * P:(i // B + 1) * P]


def project_and_distance_block(nc, dram, HG, X1, Zd, ahead, cst):
    with ExitStack() as ctx:
        def sb(name, shape, dt=F32):
            return ctx.enter_context(nc.sbuf_tensor(name, shape, dt))

        def sem(name):
            return ctx.enter_context(nc.semaphore(name))

        bank = [ctx.enter_context(nc.psum_tensor(f"b_bank{i}", [P, 512], F32)) for i in range(8)]
        PO, PT, PD, PA, PB = bank[0:2], bank[2:4], bank[4:6], bank[6], bank[7]
        wout, ctxT = ahead["wout"], ahead["ctxT"]
        sq = sb("sq", [P, KD, B, SR])
        AA = sb("AA", [P, SR])
        x1T = sb("x1T", [P, KD, B, T])
        st = sb("st", [P, 2, 6])
        mv = sb("mv", [P, NT, 2])
        sd = sb("sd", [P, NT])
        rs = sb("rs", [P, NT])
        ssq = sb("ssq", [P, NT])
        junk = sb("junk", [P, 2, D])
        mb = sb("mb", [P, B, 4])
        bb = sb("bb", [P, LANES])
        ones = sb("ones", [P, L])

        ld_w, ld_c = ahead["ld_w"], ahead["ld_c"]
        ld_x = [ahead["ld_x0"]] + [sem(f"b_ld_x{i}") for i in range(1, NI)]
        s_sq, s_one, pe_aa, s_aa = sem("b_sq"), sem("b_one"), sem("pe_aa"), sem("s_aa")
        pe_o, s_add, s_st, s_mv, s_sd, s_rs, s_x1 = (sem("b_" + k) for k in ("pe_o", "add", "st", "mv", "sd", "rs", "x1"))
        s_ssq, pe_tr, s_x1T, s_mb, pe_bb, s_bb = (sem("b_" + k) for k in ("ssq", "pe_tr", "x1T", "mb", "pe_bb", "bb"))
        pe_d, s_d2, s_cl, s_zd, s_pad = (sem("b_" + k) for k in ("pe_d", "d2", "cl", "zd", "pad"))
        block = ctx.enter_context(nc.Block())

        LAG_T, LAG_D, LAG_Z = 3, 7, 8

        @block.sync
        def _(sp):
            xt = dram["x_tok"].rearrange("(b i p) d -> p i b d", b=B, p=P)
            for i in range(1, NI):
                sp.dma_start(X1[:, i * B:(i + 1) * B, :], xt[:, i]).then_inc(ld_x[i], 16)

        @block.gpsimd
        def _(pool):
            pool.memset(Zd[:, :, 0:PAD], BIG).then_inc(s_pad, 1)
            pool.memset(Zd[:, :, PAD + SR:PITCH], BIG).then_inc(s_pad, 1)
            pool.wait_ge(s_pad, 2)

        @block.tensor
        def _(te):
            def attention_out(i):
                if i == 0:
                    te.wait_ge(ld_w, 16)
                if i >= 2:
                    te.wait_ge(s_add, i - 1)
                for c in range(CT):
                    last = te.matmul(PO[i % 2][:, 0:D], token_tile(HG[:, c], i), wout[:, c, :],
                                     start=(c == 0), stop=(c == CT - 1))
                last.then_inc(pe_o, 1)

            def turn(i):
                te.wait_ge(s_x1, i + 1)
                if i >= 2:
                    te.wait_ge(s_x1T, i - 1)
                for k in range(KD):
                    last = te.transpose(PT[i % 2][:, k * P:(k + 1) * P], X1[:, i, k * P:(k + 1) * P], cst["eye"][:, :])
                last.then_inc(pe_tr, 1)

            def norms(t):
                te.wait_ge(s_mb, t + 1)
                for b in range(B):
                    last = te.matmul(PB[L * b:L * b + L, 4 * t:4 * t + 4], cst["tri"][:, 0, :], mb[:, b, :],
                                     start=True, stop=True)
                last.then_inc(pe_bb, 1)

            def distances(jb):
                if jb % B == 0:
                    te.wait_ge(s_x1T, jb + B)
                if jb >= 2:
                    te.wait_ge(s_d2, jb - 1)
                for k in range(KD):
                    for b in range(B):
                        last = te.matmul(PD[jb % 2][L * b:L * b + L, 0:SR],
                                         x1T[:, k, b, jb * CW:(jb + 1) * CW], ctxT[:, k, b, :],
                                         start=(k == 0), stop=(k == KD - 1))
                last.then_inc(pe_d, 1)

            def context_norms():
                te.wait_ge(s_one, 2)
                te.wait_ge(s_sq, 2)
                for k in range(KD):
                    for b in range(B):
                        last = te.matmul(PA[L * b:L * b + L, 0:SR], ones[:, :], sq[:, k, b, :],
                                         start=(k == 0), stop=(k == KD - 1))
                last.then_inc(pe_aa, 1)

            for i in range(NT + LAG_D):
                if i < NT:
                    attention_out(i)
                if i == 2:
                    context_norms()
                if LAG_T <= i < NT + LAG_T:
                    turn(i - LAG_T)
                if i % B == 2 and B <= i < NT + B:
                    norms(i // B - 1)
                if i >= LAG_D:
                    distances(i - LAG_D)

        @block.scalar
        def _(act):
            act.wait_ge(s_one, 1)
            for i in range(NT + LAG_Z + 1):
                if i == LAG_T:
                    act.wait_ge(pe_aa, 1)
                    act.activation(AA[:, :], PA[:, 0:SR], ACT.Copy).then_inc(s_aa, 1)
                if i < NT:
                    act.wait_ge(s_mv, i + 1)
                    act.activation(sd[:, i:i + 1], mv[:, i, 1:2], ACT.Sqrt, bias=cst["eps"][:, 0:1]).then_inc(s_sd, 1)
                if 1 <= i <= NT:
                    j = i - 1
                    act.wait_ge(s_x1, j + 1)
                    if j >= 2:
                        act.wait_ge(s_ssq, j - 1)
                    act.activation(junk[:, j % 2, :], X1[:, j, :], ACT.Square, accum_out=ssq[:, j:j + 1]).then_inc(s_ssq, 1)
                if LAG_T <= i < NT + LAG_T:
                    j = i - LAG_T
                    act.wait_ge(pe_tr, j + 1)
                    out = x1T[:, :, j % B, (j // B) * P:(j // B + 1) * P]
                    act.activation(out, PT[j % 2][:, 0:KD * P].rearrange("p (k t) -> p k t", k=KD),
                                   ACT.Copy).then_inc(s_x1T, 1)
                if i > LAG_Z and (i - LAG_Z) % 2 == 0:
                    pair = (i - LAG_Z) // 2 - 1
                    act.wait_ge(s_cl, pair + 1)
                    z = Zd[:, 2 * pair:2 * pair + 2, PAD:PAD + SR]
                    act.activation(z, z, ACT.Sqrt).then_inc(s_zd, 1)

        @block.vector
        def _(dve):
            dve.memset(cst["eps"][:, :], EPS).then_inc(s_one, 1)
            dve.memset(ones[:, :], 1.0).then_inc(s_one, 1)
            dve.wait_ge(ld_c, 16)
            dve.tensor_tensor(sq[:], ctxT[:], ctxT[:], ALU.mult).then_inc(s_sq, 1)
            dve.wait_ge(s_sq, 1)
            dve.tensor_scalar(ctxT[:], ctxT[:], -2.0, None, ALU.mult).then_inc(s_sq, 1)
            for i in range(NT + LAG_Z):
                if i < NT:
                    if i % B == 0:
                        dve.wait_ge(ld_x[i // B], 16)
                    dve.wait_ge(pe_o, i + 1)
                    dve.tensor_tensor(X1[:, i, :], X1[:, i, :], PO[i % 2][:, 0:D], ALU.add).then_inc(s_add, 1)
                    dve.wait_ge(s_add, i + 1)
                    dve.bn_stats(st[:, i % 2, :], X1[:, i, :]).then_inc(s_st, 1)
                    dve.wait_ge(s_st, i + 1)
                    dve.bn_aggr(mv[:, i, :], st[:, i % 2, :]).then_inc(s_mv, 1)
                if 1 <= i <= NT:
                    j = i - 1
                    dve.wait_ge(s_sd, j + 1)
                    dve.reciprocal(rs[:, j:j + 1], sd[:, j:j + 1]).then_inc(s_rs, 1)
                    dve.wait_ge(s_rs, j + 1)
                    dve.wait_ge(s_mv, j + 1)
                    dve.tensor_scalar(X1[:, j, :], X1[:, j, :], mv[:, j, 0:1], rs[:, j:j + 1],
                                      ALU.subtract, ALU.mult).then_inc(s_x1, 1)
                if i >= 2 and (i - 2) % B == B - 1 and i - 2 < NT:
                    t = (i - 2) // B
                    dve.wait_ge(s_ssq, B * (t + 1))
                    if t >= 1:
                        dve.wait_ge(pe_bb, t)
                    dve.tensor_tensor(mb[:, :, :], ssq[:, B * t:B * t + B].unsqueeze(2).broadcast_to([P, B, 4]),
                                      cst["quad"][:, :].unsqueeze(1).broadcast_to([P, B, 4]), ALU.mult).then_inc(s_mb, 1)
                if i % B == 2 and B < i < NT + B:
                    t = i // B - 1
                    dve.wait_ge(pe_bb, t + 1)
                    dve.tensor_copy(bb[:, 4 * t:4 * t + 4], PB[:, 4 * t:4 * t + 4]).then_inc(s_bb, 1)
                    dve.wait_ge(s_bb, t + 1)
                if i >= LAG_Z:
                    jb = i - LAG_Z
                    if jb == 0:
                        dve.wait_ge(s_aa, 1)
                    dve.wait_ge(pe_d, jb + 1)
                    dve.scalar_tensor_tensor(Zd[:, jb, PAD:PAD + SR], PD[jb % 2][:, 0:SR],
                                             bb[:, jb:jb + 1], AA[:, :], ALU.add, ALU.add).then_inc(s_d2, 1)
                    if jb % 2 == 1:
                        dve.wait_ge(s_d2, jb + 1)
                        z = Zd[:, jb - 1:jb + 1, PAD:PAD + SR]
                        dve.tensor_scalar(z, z, 0.0, None, ALU.max).then_inc(s_cl, 1)


def alignment_block(nc, dram, HG, Zd, ahead, PTa, PTb, Cs, Cr, Bp, Mf, cst):
    with ExitStack() as ctx:
        def sb(name, shape, dt=F32):
            return ctx.enter_context(nc.sbuf_tensor(name, shape, dt))

        def sem(name):
            return ctx.enter_context(nc.semaphore(name))

        Dof, Rof = 0, (STEPS + 1) * DREC
        assert Rof + (STEPS + 1) * REC + 1 + LANES * PITCH // 2 <= CT * B * T
        HGf = HG[:, :, :, :].rearrange("p c b t -> p (c b t)")
        Dk = HGf[:, Dof:Dof + (STEPS + 1) * DREC].rearrange("p (k j) -> p k j", j=DREC)
        R = HGf[:, Rof:Rof + (STEPS + 1) * REC].rearrange("p (k j) -> p k j", j=REC)
        edge = sb("edge", [P, 1])
        back = sb("back", [P, 1], BF16)
        PR = 2 * CW
        one_left = sb("one_left", [P, STEPS, PR], BF16)
        up_diag = sb("up_diag", [P, STEPS, PR], BF16)
        G = [sb(f"G{i}", [P, PR], BF16) for i in range(2)]
        Pk = Zd[:, :, :].rearrange("p j i -> p (j i)")[:, 0:STEPS * PR // 2].bitcast(BF16).rearrange("p (k m) -> p k m", m=PR)
        Zof = Rof + (STEPS + 1) * REC + 1
        Zq = HGf[:, Zof:Zof + LANES * PITCH // 2].bitcast(BF16).rearrange("p (j i) -> p j i", i=PITCH)
        eyeb = sb("eyeb", [P, P], BF16)
        room = [t[:, :, :].rearrange("p j i -> p (j i)").bitcast(F32) for t in (PTa, PTb)]
        trg = [room[0][:, i * KD * D:(i + 1) * KD * D].rearrange("p (k d) -> p k d", k=KD) for i in range(3)]
        wri = room[1][:, 0:2 * KD * D].rearrange("p (w k d) -> p w k d", w=2, k=KD)
        p12 = room[1][:, 2 * KD * D:4 * KD * D].rearrange("p (o k d) -> p o k d", o=2, k=KD)
        cf = sb("cf", [P, B, D])
        bf = ahead["ctxT"][:, :, :, :].rearrange("p k b s -> p (k b s)")[:, 0:D]
        bank = [ctx.enter_context(nc.psum_tensor(f"c_bank{i}", [P, 512], F32)) for i in range(4)]
        tb = [ctx.enter_context(nc.psum_tensor(f"c_tb{i}", [P, 8, P], BF16)) for i in range(4)]

        ld_f, ld_c = sem("c_ld_f"), sem("c_ld_c")
        s_fill, s_eye, pe_r, s_pr = (sem("c_" + k) for k in ("fill", "eye", "pe_r", "pr"))
        s_init, s_skew, s_min, s_row, s_edge = (sem("c_" + k) for k in ("init", "skew", "min", "row", "edge"))
        s_ch, s_g, s_back, s_path = (sem("c_" + k) for k in ("ch", "g", "back", "path"))
        s_zq, pe_z, s_pt, s_split, pe_m, s_m, s_cz = (sem("c_" + k) for k in ("zq", "pe_z", "pt", "split", "pe_m", "m", "cz"))
        block = ctx.enter_context(nc.Block())
        REM = SR - P

        @block.sync
        def _(sp):
            for i, k in enumerate(("cos", "sin", "msin")):
                sp.dma_start(trg[i][:, :, :], dram[k].rearrange("(k p) n -> p k n", p=P)).then_inc(ld_f, 16)
            for i, k in enumerate(("w_re", "w_im")):
                sp.dma_start(wri[:, i], dram[k].rearrange("(k p) n -> p k n", p=P)).then_inc(ld_f, 16)
            cr = dram["ctx"].rearrange("b s d -> s b d")
            sp.dma_start(cf[:, :, :], cr[0:P]).then_inc(ld_c, 16)
            sp.wait_ge(s_split, 2 * PARTS - 1)
            for q in range(PARTS):
                sp.dma_start(cf[L * q:L * q + REM], cr[P:SR]).then_inc(ld_c, 16)
            for q in range(PARTS):
                sp.dma_start(bf[L * q:L * q + 1, :], dram["ffn_bias"].rearrange("(o d) -> o d", o=1)).then_inc(ld_c, 16)

        @block.gpsimd
        def _(pool):
            pool.memset(one_left[:, 0:FIRST * CHUNK, :], 1.0).then_inc(s_fill, 1)
            pool.memset(one_left[:, FIRST * CHUNK:STEPS, :], 1.0).then_inc(s_fill, 1)
            pool.memset(G[0][:, :], 0.0).then_inc(s_fill, 1)
            pool.tensor_copy(back[:, :], cst["last"][:, :]).then_inc(s_fill, 1)
            pool.tensor_copy(eyeb[:, :], cst["eye"][:, :]).then_inc(s_fill, 1)
            pool.memset(Cr[:, :, :], 0.0).then_inc(s_fill, 1)
            pool.memset(Bp[:, 0, :], 0.0).then_inc(s_fill, 1)
            pool.memset(Bp[:, 1, 0:P], 1.0).then_inc(s_fill, 1)
            pool.wait_ge(s_fill, 8)
            steps = 0

            def split(c, parts, steps):
                for i, o in enumerate(parts):
                    pool.tensor_copy(o, c).then_inc(s_split, 1)
                    steps += 1
                    pool.wait_ge(s_split, steps)
                    if i + 1 < len(parts):
                        pool.tensor_tensor(c, c, o, ALU.subtract).then_inc(s_split, 1)
                        steps += 1
                        pool.wait_ge(s_split, steps)
                return steps

            pool.wait_ge(ld_c, 16)
            steps = split(cf[:, :, :], [Cs[:, part] for part in range(PARTS)], steps)
            pool.wait_ge(ld_c, 16 * (1 + 2 * PARTS))
            for q in range(PARTS):
                rows = slice(L * q, L * q + REM)
                steps = split(cf[rows], [Cr[rows]] * (q + 1), steps)
                one = slice(L * q, L * q + 1)
                steps = split(bf[one, :], [Bp[one, 0, :]] * (q + 1), steps)
            pool.wait_ge(s_m, 4 + KD)
            for m in range(KD):
                d = Mf[:, m, m * P:(m + 1) * P]
                pool.tensor_tensor(d, d, cst["eye"][:, :], ALU.add).then_inc(s_eye, 1)
            pool.memset(PTb[:, :, :], 0.0).then_inc(s_eye, 1)
            pool.wait_ge(s_eye, KD + 1)

        @block.tensor
        def _(te):
            te.wait_ge(ld_f, 80)
            terms = (((0, 0), (1, 1)), ((1, 0), (0, 2)))
            for o in range(2):
                for m in range(KD):
                    n = 0
                    for wi, tr in terms[o]:
                        for k in range(KD):
                            last = te.matmul(bank[2 * o + m][:, 0:D], wri[:, wi, k, m * P:(m + 1) * P], trg[tr][:, k, :],
                                             start=(n == 0), stop=(n == 3))
                            n += 1
                    last.then_inc(pe_m, 1)
            te.wait_ge(s_m, 4)
            for m in range(KD):
                n = 0
                for o, tr in ((0, 0), (1, 2)):
                    for k in range(KD):
                        last = te.matmul(bank[m][:, 0:D], p12[:, o, k, m * P:(m + 1) * P], trg[tr][:, k, :],
                                         start=(n == 0), stop=(n == 3))
                        n += 1
                last.then_inc(pe_m, 1)
            te.wait_ge(s_fill, 5)
            te.wait_ge(s_zq, NCK - P // CHUNK)
            for q in range(LANES // 8):
                if q >= 2:
                    te.wait_ge(s_pr, PARTS * (q - 1))
                for j in range(8):
                    last = te.transpose(tb[2 + q % 2][0:REM, j, :], Zq[:, 8 * q + j, PAD + P:PAD + SR], eyeb[:, :])
                last.then_inc(pe_r, 1)
            for i, q in enumerate(reversed(range(LANES // 8))):
                te.wait_ge(s_zq, NCK - 8 * q // CHUNK)
                if i >= 2:
                    te.wait_ge(s_pt, i - 1)
                for j in range(8):
                    last = te.transpose(tb[i % 2][:, j, :], Zq[:, 8 * q + j, PAD:PAD + P], eyeb[:, :])
                last.then_inc(pe_z, 1)

        @block.scalar
        def _(act):
            for i in range(4):
                act.wait_ge(pe_m, i + 1)
                act.activation(p12[:, i // 2, i % 2, :], bank[i][:, 0:D], ACT.Copy).then_inc(s_m, 1)
            for m in range(KD):
                act.wait_ge(pe_m, 5 + m)
                act.activation(Mf[:, m, :], bank[m][:, 0:D], ACT.Copy, scale=1.0 / D).then_inc(s_m, 1)

            def place(pt, first, rows, q, src):
                out = pt[first:first + rows].rearrange("p b (j l) -> p j b l", l=L)[:, 8 * q:8 * q + 8]
                return act.activation(out, src[0:rows].rearrange("p j (b l) -> p j b l", b=B), ACT.Copy)

            act.wait_ge(s_eye, KD + 1)
            for q in range(LANES // 8):
                act.wait_ge(pe_r, q + 1)
                for part in range(PARTS):
                    place(PTb, L * part, REM, q, tb[2 + q % 2]).then_inc(s_pr, 1)
            for i, q in enumerate(reversed(range(LANES // 8))):
                act.wait_ge(pe_z, i + 1)
                place(PTa, 0, P, q, tb[i % 2]).then_inc(s_pt, 1)

        @block.vector
        def _(dve):
            inits = [(R[:, 0, :], BIG), (Dk[:, 0, :], BIG), (Dk[:, 1:STEPS + 1, 0], BIG), (Dk[:, 1:STEPS + 1, 1], 0.0),
                     (edge[:, :], BIG)]
            for a, v in inits:
                dve.memset(a, v).then_inc(s_init, 1)
            dve.wait_ge(s_init, len(inits))
            n0 = len(inits)
            for b in range(B):
                o = slice(L * b, L * b + 1)
                dve.memset(Dk[o, 0, 1:2], 0.0).then_inc(s_init, 1)
                dve.memset(Dk[o, 1:STEPS + 1, 1:2], BIG).then_inc(s_init, 1)

            def steps_of(c):
                return CHUNK * c, min(CHUNK * (c + 1), STEPS)

            def skew(c):
                k0, k1 = steps_of(c)
                src = view(Zd[:, :, :], PAD + k0, (1, k1 - k0), (PITCH - 1, LANES))
                dve.transpose(Dk[:, k0 + 1:k1 + 1, 2:DREC], src).then_inc(s_skew, 1)

            def choose(c, part):
                k0, k1 = steps_of(c)
                diag, up, left = R[:, k0:k1, 0:CW], R[:, k0:k1, 1:REC], R[:, k0 + 1:k1 + 1, 0:CW]
                to_left, to_up, to_diag = (view(t[:, :, :], PR * k0 + slot, (PR, k1 - k0), (-2, CW)) for t, slot in
                                           ((one_left, PR - 1), (up_diag, PR - 2), (up_diag, PR - 1)))
                if part == 0:
                    if c in (0, FIRST):
                        dve.wait_ge(s_fill, 1 + (c == FIRST))
                    dve.tensor_tensor(to_left, Dk[:, k0:k1, 1:REC], left, ALU.is_gt).then_inc(s_ch, 1)
                if part == 1:
                    dve.tensor_tensor(to_diag, diag, up, ALU.is_le).then_inc(s_ch, 1)
                if part == 2:
                    dve.wait_ge(s_ch, 4 * c + 2)
                    dve.scalar_tensor_tensor(to_up, to_left, 0.0, to_diag, ALU.is_equal, ALU.is_gt).then_inc(s_ch, 1)
                if part == 3:
                    dve.wait_ge(s_ch, 4 * c + 3)
                    dve.scalar_tensor_tensor(to_diag, to_left, 0.0, to_diag, ALU.is_equal, ALU.mult).then_inc(s_ch, 1)

            dve.wait_ge(s_init, n0 + 2 * B)
            skew(0)
            shift = [LANES - 1] + list(range(LANES - 1))
            for k in range(STEPS):
                if k % CHUNK == 0:
                    dve.wait_ge(s_skew, k // CHUNK + 1)
                if k >= 1:
                    dve.wait_ge(s_row, k)
                    dve.tensor_tensor(Dk[:, k, 1:REC], R[:, k, 1:REC], R[:, k, 0:CW], ALU.min).then_inc(s_min, 1)
                    dve.stream_shuffle(edge[:, :], R[:, k, CW:REC], shift).then_inc(s_edge, 1)
                    c, at = k // CHUNK, k % CHUNK
                    if at == 1 and c + 1 < NCK:
                        skew(c + 1)
                    elif c >= 1:
                        choose(c - 1, {0: 0, 2: 1, 3: 2}[at])
                    dve.wait_ge(s_edge, k)
                    dve.wait_ge(s_min, k)
                dve.tensor_tensor_scan(R[:, k + 1, :], Dk[:, k, 0:REC], Dk[:, k + 1, 1:DREC], edge[:, 0:1],
                                       ALU.min, ALU.add).then_inc(s_row, 1)
                if k % CHUNK == CHUNK - 1 and k >= 2 * CHUNK - 1:
                    choose(k // CHUNK - 1, 3)
            dve.wait_ge(s_row, STEPS)
            last = NCK - 1
            for part in range(4):
                if CHUNK * last + (0, 2, 3, 3)[part] >= STEPS:
                    choose(last - 1, part)
            for part in range(4):
                choose(last, part)
            dve.wait_ge(s_ch, 4 * NCK)
            for b in range(B):
                o = slice(L * b, L * b + 1)
                dve.memset(up_diag[o, :, PR - 1:PR], 0.0).then_inc(s_cz, 1)
                dve.memset(one_left[o, :, PR - 1:PR], 0.0).then_inc(s_cz, 1)
            dve.wait_ge(s_cz, 2 * B)

            def unskew(c):
                k0, k1 = steps_of(c)
                dst = view(Zq, PAD + k0, (1, k1 - k0), (PITCH - 1, LANES))
                dve.transpose(dst, view(Pk, PR * k0 + PR - 2, (PR, k1 - k0), (-2, CW))).then_inc(s_zq, 1)

            dve.wait_ge(s_fill, 5)
            shift = list(range(1, LANES)) + [0]
            for n in range(STEPS):
                k = STEPS - 1 - n
                g = G[n % 2]
                if n >= 1:
                    dve.wait_ge(s_path, n)
                    on = Pk[:, k + 1, :].rearrange("p (j two) -> p j two", two=2)[:, :, 0:1].broadcast_to([P, CW, 2])
                    dve.tensor_tensor(g[:, :].rearrange("p (j two) -> p j two", two=2),
                                      up_diag[:, k + 1, :].rearrange("p (j two) -> p j two", two=2), on,
                                      ALU.mult).then_inc(s_g, 1)
                    dve.stream_shuffle(back[:, :], Pk[:, k + 1, PR - 1:PR], shift).then_inc(s_back, 1)
                    if (k + 1) % CHUNK == 0:
                        unskew((k + 1) // CHUNK)
                    dve.wait_ge(s_back, n)
                    dve.wait_ge(s_g, n)
                dve.tensor_tensor_scan(Pk[:, k, :], one_left[:, k, :], g[:, :], back[:, 0:1],
                                       ALU.mult, ALU.add).then_inc(s_path, 1)
            dve.wait_ge(s_path, STEPS)
            unskew(0)
            dve.wait_ge(s_zq, NCK)


def output_block(nc, dram, X1, PTa, PTb, Cs, Cr, Bp, Mf, cst):
    with ExitStack() as ctx:
        def sb(name, shape, dt=F32):
            return ctx.enter_context(nc.sbuf_tensor(name, shape, dt))

        def sem(name):
            return ctx.enter_context(nc.semaphore(name))

        bank = [ctx.enter_context(nc.psum_tensor(f"d_bank{i}", [P, 512], F32)) for i in range(8)]
        PA, PT, PF = bank[0:2], bank[2:4], bank[4:8]
        x2T = sb("x2T", [P, 4, KD, P])
        st = sb("d_st", [P, 4, 6])
        mv = sb("d_mv", [P, 2, NT, 2])
        sd = sb("d_sd", [P, 2, NT])
        rs = sb("d_rs", [P, 2, NT])
        nm = sb("d_nm", [P, 2, NT])
        s = {k: sem("d_" + k) for k in ("pe_x", "add", "pe_t", "x2T", "pe_f", "x2", "y", "out")}
        s_st, s_mv, s_sd, s_rs, s_nm = ([sem(f"d_{k}{i}") for i in range(2)] for k in ("st", "mv", "sd", "rs", "nm"))
        block = ctx.enter_context(nc.Block())
        LAG_D, LAG_I, LAG_N, LAG_T, LAG_F, LAG_S, LAG_J, LAG_Y = 1, 2, 4, 5, 7, 8, 9, 10

        def in_range(j):
            return 0 <= j < NT

        def pair_ends(j):
            return in_range(j) and j % 2 == 1

        @block.sync
        def _(sp):
            ot = dram["out"].rearrange("(b i p) d -> p i b d", b=B, p=P)
            for i in range(NI):
                sp.wait_ge(s["y"], B * (i + 1))
                sp.dma_start(ot[:, i], X1[:, i * B:(i + 1) * B, :]).then_inc(s["out"], 16)
            sp.wait_ge(s["out"], 16 * NI)

        @block.tensor
        def _(te):
            for i in range(NT + LAG_F):
                if i < NT:
                    b = i % B
                    if i >= 2:
                        te.wait_ge(s["add"], i - 1)
                    for part in range(PARTS):
                        te.matmul(PA[i % 2][:, 0:D], token_tile(PTa, i), Cs[:, part, b, :], start=(part == 0), stop=False)
                    te.matmul(PA[i % 2][:, 0:D], token_tile(PTb[0:PARTS * L], i), Cr[0:PARTS * L, b, :],
                              start=False, stop=True).then_inc(s["pe_x"], 1)
                if LAG_T <= i < NT + LAG_T:
                    j = i - LAG_T
                    te.wait_ge(s["x2"], j + 1)
                    if j >= 2:
                        te.wait_ge(s["x2T"], j - 1)
                    for k in range(KD):
                        last = te.transpose(PT[j % 2][:, k * P:(k + 1) * P], X1[:, j, k * P:(k + 1) * P], cst["eye"][:, :])
                    last.then_inc(s["pe_t"], 1)
                if LAG_F <= i:
                    j = i - LAG_F
                    if j >= 4:
                        te.wait_ge(s["y"], j - 3)
                    te.matmul(PF[j % 4][:, 0:D], Bp[0:PARTS * L, 1, 0:P], Bp[0:PARTS * L, 0, :], start=True, stop=False)
                    te.wait_ge(s["x2T"], j + 1)
                    for k in range(KD):
                        last = te.matmul(PF[j % 4][:, 0:D], x2T[:, j % 4, k, :], Mf[:, k, :], start=False, stop=(k == KD - 1))
                    last.then_inc(s["pe_f"], 1)

        @block.scalar
        def _(act):
            def deviation(j, half):
                act.wait_ge(s_mv[half], j + 2)
                act.activation(sd[:, half, j:j + 2], mv[:, half, j:j + 2, 1], ACT.Sqrt, bias=cst["eps"][:, 0:1]).then_inc(s_sd[half], 1)

            def normalize(j, half, src, done):
                act.wait_ge(s_nm[half], j // 2 + 1)
                act.activation(X1[:, j, :], src, ACT.Identity, scale=rs[:, half, j:j + 1],
                               bias=nm[:, half, j:j + 1]).then_inc(done, 1)

            for i in range(NT + LAG_Y):
                if in_range(i - LAG_N):
                    normalize(i - LAG_N, 0, X1[:, i - LAG_N, :], s["x2"])
                if pair_ends(i - LAG_D):
                    deviation(i - LAG_D - 1, 0)
                if in_range(i - LAG_T):
                    j = i - LAG_T
                    act.wait_ge(s["pe_t"], j + 1)
                    if j >= 4:
                        act.wait_ge(s["pe_f"], j - 3)
                    act.activation(x2T[:, j % 4].rearrange("p k t -> p (k t)"), PT[j % 2][:, 0:KD * P], ACT.Copy).then_inc(s["x2T"], 1)
                if in_range(i - LAG_Y):
                    normalize(i - LAG_Y, 1, PF[(i - LAG_Y) % 4][:, 0:D], s["y"])
                if pair_ends(i - LAG_S):
                    deviation(i - LAG_S - 1, 1)

        @block.vector
        def _(dve):
            def stats(j, half, src):
                dve.bn_stats(st[:, 2 * half + j % 2, :], src).then_inc(s_st[half], 1)

            def moments(j, half):
                dve.wait_ge(s_st[half], j + 1)
                dve.bn_aggr(mv[:, half, j, :], st[:, 2 * half + j % 2, :]).then_inc(s_mv[half], 1)

            def inverse(j, half):
                dve.wait_ge(s_sd[half], j // 2 + 1)
                dve.reciprocal(rs[:, half, j:j + 2], sd[:, half, j:j + 2]).then_inc(s_rs[half], 1)

            def offset(j, half):
                dve.wait_ge(s_rs[half], j // 2 + 1)
                dve.wait_ge(s_mv[half], j + 2)
                dve.scalar_tensor_tensor(nm[:, half, j:j + 2], mv[:, half, j:j + 2, 0], -1.0, rs[:, half, j:j + 2],
                                         ALU.mult, ALU.mult).then_inc(s_nm[half], 1)

            for i in range(NT + LAG_Y):
                if pair_ends(i - LAG_I):
                    inverse(i - LAG_I - 1, 0)
                if pair_ends(i - LAG_J):
                    inverse(i - LAG_J - 1, 1)
                if pair_ends(i - LAG_I):
                    offset(i - LAG_I - 1, 0)
                if in_range(i):
                    dve.wait_ge(s["pe_x"], i + 1)
                    dve.tensor_tensor(X1[:, i, :], X1[:, i, :], PA[i % 2][:, 0:D], ALU.add).then_inc(s["add"], 1)
                if pair_ends(i - LAG_J):
                    offset(i - LAG_J - 1, 1)
                if in_range(i - LAG_S):
                    dve.wait_ge(s["pe_f"], i - LAG_S + 1)
                    stats(i - LAG_S, 1, PF[(i - LAG_S) % 4][:, 0:D])
                if in_range(i):
                    dve.wait_ge(s["add"], i + 1)
                    stats(i, 0, X1[:, i, :])
                if in_range(i - LAG_S):
                    moments(i - LAG_S, 1)
                if in_range(i):
                    moments(i, 0)


def build_program(nc, dram):
    with ExitStack() as ctx:
        HG = ctx.enter_context(nc.sbuf_tensor("HG", [P, CT, B, T], F32))
        cst = {"tri": ctx.enter_context(nc.sbuf_tensor("tri", [P, 8, L], F32)),
               "eye": ctx.enter_context(nc.sbuf_tensor("eye", [P, P], F32)),
               "quad": ctx.enter_context(nc.sbuf_tensor("quad", [P, 4], F32)),
               "last": ctx.enter_context(nc.sbuf_tensor("last", [P, 1], F32)),
               "bias": ctx.enter_context(nc.sbuf_tensor("bias", [P, 3, CT], F32)),
               "slope": ctx.enter_context(nc.sbuf_tensor("slope", [P, 2, CT], F32)),
               "flag": ctx.enter_context(nc.sbuf_tensor("flag", [1, 1], I32)),
               "eps": ctx.enter_context(nc.sbuf_tensor("eps", [P, 1], F32))}
        ahead = {"ctxT": ctx.enter_context(nc.sbuf_tensor("ctxT", [P, KD, B, SR], F32)),
                 "ld_w": ctx.enter_context(nc.semaphore("ld_wout")),
                 "ld_c": ctx.enter_context(nc.semaphore("ld_ctx")),
                 "ld_x0": ctx.enter_context(nc.semaphore("ld_x0_tok"))}
        recurrence_block(nc, dram, HG, ahead, cst)
        X1 = ctx.enter_context(nc.sbuf_tensor("x_all", [P, NT, D], F32))
        Zd = ctx.enter_context(nc.sbuf_tensor("Zd", [P, LANES, PITCH], F32))
        with nc.sbuf_tensor("wout", [P, CT, D], F32) as wout:
            ahead["wout"] = wout
            general_recurrence_block(nc, dram, HG, X1, ahead, cst)
            project_and_distance_block(nc, dram, HG, X1, Zd, ahead, cst)
        PTa = ctx.enter_context(nc.sbuf_tensor("PTa", [P, B, T], BF16))
        PTb = ctx.enter_context(nc.sbuf_tensor("PTb", [P, B, T], BF16))
        Cs = ctx.enter_context(nc.sbuf_tensor("Cs", [P, PARTS, B, D], BF16))
        Cr = ctx.enter_context(nc.sbuf_tensor("Cr", [P, B, D], BF16))
        Bp = ctx.enter_context(nc.sbuf_tensor("Bp", [P, 2, D], BF16))
        Mf = ctx.enter_context(nc.sbuf_tensor("Mf", [P, KD, D], F32))
        alignment_block(nc, dram, HG, Zd, ahead, PTa, PTb, Cs, Cr, Bp, Mf, cst)
        output_block(nc, dram, X1, PTa, PTb, Cs, Cr, Bp, Mf, cst)


def constant_tables():
    import numpy as np
    r = np.arange(L)
    eye = (r[:, None] == r[None, :])
    low = (r[:, None] > r[None, :])
    masks = [eye, low]
    for m in (1,) + LEVELS:
        masks.append((r[:, None] // (2 * m) == r[None, :] // (2 * m)) & (r[:, None] // m > r[None, :] // m))
    masks = masks + [eye] * (8 - len(masks))
    tri = np.stack(masks, 1).astype(np.float32)
    return np.ascontiguousarray(np.tile(tri, (B, 1, 1)))


def transform_tables():
    import numpy as np
    n = np.arange(D)
    turn = 2 * np.pi * (np.outer(n, n) % D) / D
    p = np.arange(P)
    return {
        "eye": np.eye(P, dtype=np.float32),
        "quad": (p[:, None] // L == np.arange(4)).astype(np.float32),
        "last": (p[:, None] % L == L - 1).astype(np.float32),
        "cos": np.cos(turn).astype(np.float32),
        "sin": np.sin(turn).astype(np.float32),
        "msin": (-np.sin(turn)).astype(np.float32),
    }


def kernel(x, ctx_1024, L0_attn_omega, L0_attn_Win, L0_attn_Wl, L0_attn_bl, L0_attn_Wv, L0_attn_bv, L0_attn_Wout,
           L0_ffn_w_freq_real, L0_ffn_w_freq_imag, L0_ffn_bias):
    import numpy as np
    import concourse.bacc as bacc
    from concourse.bass_utils import run_bass_kernel_spmd

    def cols(v):
        return np.asarray(v).reshape(CT, P).T

    x = np.asarray(x)
    arrays = {
        "x_tok": x.reshape(B * T, D),
        "x_t": x.transpose(2, 0, 1).reshape(KD, P, B, T),
        "win": np.asarray(L0_attn_Win),
        "win_t": np.asarray(L0_attn_Win).T,
        "wlv_t": np.stack([np.asarray(L0_attn_Wl).T, np.asarray(L0_attn_Wv).T]),
        "bias": np.stack([cols(L0_attn_bl), cols(L0_attn_bv), cols(L0_attn_omega)], 1),
        "wout_t": np.asarray(L0_attn_Wout).T,
        "ctx": np.asarray(ctx_1024),
        "ctx_t": np.asarray(ctx_1024).transpose(2, 0, 1).reshape(KD, P, B, SR),
        "w_re": np.asarray(L0_ffn_w_freq_real),
        "w_im": np.asarray(L0_ffn_w_freq_imag),
        "ffn_bias": np.asarray(L0_ffn_bias),
        "tri": constant_tables(),
        **transform_tables(),
    }
    nc = bacc.Bacc("TRN2", target_bir_lowering=False, num_devices=1)
    ins, dram = {}, {}
    for name, a in arrays.items():
        a = np.ascontiguousarray(a)
        ins["in_" + name] = a
        dram[name] = nc.dram_tensor("in_" + name, a.shape, mybir.dt.from_np(a.dtype), kind="ExternalInput").ap()
    dram["out"] = nc.dram_tensor("out_y", (B * T, D), F32, kind="ExternalOutput").ap()
    build_program(nc, dram)
    r = run_bass_kernel_spmd(nc, [ins], core_ids=[0])
    return r.results[0]["out_y"].reshape(B, T, D)
```
